# Optimizing a Trainium2 kernel written in Bass

```python
import numpy as np
import jax
import jax.numpy as jnp

def _softmax(x, axis=-1):
    return jax.nn.softmax(x, axis=axis)

def _gelu(x):
    return jax.nn.gelu(x, approximate=True)

def _silu(x):
    return jax.nn.silu(x)

def _sigmoid(x):
    return jax.nn.sigmoid(x)

def _layernorm(x, axis=-1, eps=1e-05):
    m = jnp.mean(x, axis=axis, keepdims=True)
    v = jnp.var(x, axis=axis, keepdims=True)
    return (x - m) / jnp.sqrt(v + eps)

def _scatter_add(tgt, idx, src, axis=0):
    return tgt.at[idx].add(src)

def _segment_sum(src, seg, n):
    return jax.ops.segment_sum(src, seg, n)
kernel_name = 'mk_prb_d4_jaxref_r8_e63c30'

def setup_inputs(seed: int=0):
    np.random.seed(seed)
    _w = jnp.asarray

    def _L0_attn_setup():
        import jax, jax.numpy as jnp
        import numpy as np
        BLOCK = 128

        def _block_cumsum_flat(x):
            shape = x.shape
            flat = x.reshape(-1, BLOCK)
            y = jnp.cumsum(flat, axis=-1)
            return y.reshape(shape)
        key = jax.random.key(seed)
        k1, k2, k3 = jax.random.split(key, 3)
        b, s, h = (8, 512, 128)
        x = jax.random.normal(k1, (b, s, h), dtype=jnp.float32)
        bound = 1.0 / np.sqrt(h)
        W = jax.random.uniform(k2, (h, h), dtype=jnp.float32, minval=-bound, maxval=bound)
        bias = jax.random.uniform(k3, (h,), dtype=jnp.float32, minval=-bound, maxval=bound)
        return {'x': x, 'W': W, 'bias': bias}
    _L0_attn_in = _L0_attn_setup()

    def _L0_ffn_setup():
        import jax, jax.numpy as jnp
        import numpy as np
        DIM = 128

        def _reference_tuple_inner(x, W_r, W_k, W_v, mu_r, mu_k):
            B, T, C = x.shape
            x_prev = jnp.concatenate([jnp.zeros((B, 1, C), x.dtype), x[:, :-1, :]], axis=1)
            xr = mu_r * x + (1.0 - mu_r) * x_prev
            xk = mu_k * x + (1.0 - mu_k) * x_prev
            r = jax.nn.sigmoid(jnp.einsum('btc,dc->btd', xr, W_r))
            k = jnp.einsum('btc,dc->btd', xk, W_k)
            k_act = jnp.square(jax.nn.relu(k))
            out = r * jnp.einsum('btc,dc->btd', k_act, W_v)
            new_state = x[:, -1, :]
            return (out, new_state)
        key = jax.random.key(seed)
        ks = jax.random.split(key, 6)
        B, T, C = (8, 256, DIM)
        x = jax.random.normal(ks[0], (B, T, C), dtype=jnp.float32)
        s = 1.0 / np.sqrt(C)
        W_r = jax.random.uniform(ks[1], (C, C), jnp.float32, -s, s)
        W_k = jax.random.uniform(ks[2], (C, C), jnp.float32, -s, s)
        W_v = jax.random.uniform(ks[3], (C, C), jnp.float32, -s, s)
        mu_r = jax.random.uniform(ks[4], (C,), jnp.float32)
        mu_k = jax.random.uniform(ks[5], (C,), jnp.float32)
        return {'x': x, 'W_r': W_r, 'W_k': W_k, 'W_v': W_v, 'mu_r': mu_r, 'mu_k': mu_k}
    _L0_ffn_in = _L0_ffn_setup()

    def _L1_attn_setup():
        import jax, jax.numpy as jnp
        import numpy as np
        B, S, H, N, D = (2, 256, 128, 16, 64)
        PAD = -30000.0
        key = jax.random.key(seed)
        kx, kqkv, kout, krpe = jax.random.split(key, 4)
        x = jax.random.normal(kx, (B, S, H), jnp.float32)
        qkv = jax.random.normal(kqkv, (H, 3, N, D), jnp.float32) * H ** (-0.5)
        out_w = jax.random.normal(kout, (N, D, H), jnp.float32) * (N * D) ** (-0.5)
        rpe_bias = jax.random.normal(krpe, (N, S), jnp.float32) * 0.02
        return {'x': x, 'qkv': qkv, 'out_w': out_w, 'rpe_bias': rpe_bias}
    _L1_attn_in = _L1_attn_setup()

    def _L1_ffn_setup():
        import jax, jax.numpy as jnp
        import numpy as np
        TOP_K = 2
        TEMP = 0.9
        EPS = 1e-05
        B, S, D, F, E = (2, 256, 128, 512, 8)

        def _moe_forward(x, gate_w, gate_b, w1, b1, w2, b2, ln_g, ln_b):
            logits = (x @ gate_w + gate_b) / TEMP
            topk_vals, topk_idx = jax.lax.top_k(logits, TOP_K)
            keep = jax.nn.one_hot(topk_idx, E, dtype=jnp.bool_).any(-2)
            masked = jnp.where(keep, logits, -jnp.inf)
            gate_probs = jax.nn.softmax(masked, axis=-1)
            h = jnp.einsum('bsd,edf->bsef', x, w1) + b1
            h = jax.nn.gelu(h, approximate=False)
            expert_out = jnp.einsum('bsef,efd->bsed', h, w2) + b2
            out = jnp.einsum('bse,bsed->bsd', gate_probs, expert_out)
            mu = out.mean(-1, keepdims=True)
            var = out.var(-1, keepdims=True)
            out = (out - mu) / jnp.sqrt(var + EPS) * ln_g + ln_b
            return out
        key = jax.random.key(seed)
        ks = jax.random.split(key, 4)
        scale_in = 1.0 / np.sqrt(D)
        scale_ff = 1.0 / np.sqrt(F)
        return {'x': jax.random.normal(ks[0], (B, S, D), jnp.float32), 'gate_w': jax.random.normal(ks[1], (D, E), jnp.float32) * scale_in, 'gate_b': jnp.zeros((E,), jnp.float32), 'w1': jax.random.normal(ks[2], (E, D, F), jnp.float32) * scale_in, 'b1': jnp.zeros((E, F), jnp.float32), 'w2': jax.random.normal(ks[3], (E, F, D), jnp.float32) * scale_ff, 'b2': jnp.zeros((E, D), jnp.float32), 'ln_g': jnp.ones((D,), jnp.float32), 'ln_b': jnp.zeros((D,), jnp.float32)}
    _L1_ffn_in = _L1_ffn_setup()

    def _L2_attn_setup():
        import math
        import jax, jax.numpy as jnp
        import numpy as np
        NUM_HEAD = 16
        BLOCK_SIZE = 256

        def get_slopes(n):

            def pow2(n):
                start = 2 ** (-2 ** (-(math.log2(n) - 3)))
                return [start * start ** i for i in range(n)]
            if math.log2(n).is_integer():
                return pow2(n)
            c = 2 ** math.floor(math.log2(n))
            return pow2(c) + get_slopes(2 * c)[0::2][:n - c]
        key = jax.random.key(seed)
        ks = jax.random.split(key, 5)
        B, T, C = (4, 256, 128)
        x = jax.random.normal(ks[0], (B, T, C), dtype=jnp.float32)
        Wq = 0.02 * jax.random.normal(ks[1], (C, C), dtype=jnp.float32)
        Wk = 0.02 * jax.random.normal(ks[2], (C, C), dtype=jnp.float32)
        Wv = 0.02 * jax.random.normal(ks[3], (C, C), dtype=jnp.float32)
        Wo = 0.02 * jax.random.normal(ks[4], (C, C), dtype=jnp.float32)
        return {'x': x, 'Wq': Wq, 'Wk': Wk, 'Wv': Wv, 'Wo': Wo}
    _L2_attn_in = _L2_attn_setup()

    def _L2_ffn_setup():
        import jax, jax.numpy as jnp
        import numpy as np
        E = 8
        C = 160
        D = 128
        H = 512
        B, S = (4, 256)
        key = jax.random.key(seed)
        ks = jax.random.split(key, 12)
        sc = 0.02
        return {'input': jax.random.normal(ks[0], (B, S, D), jnp.float32), 'router_w': jax.random.normal(ks[1], (D, E), jnp.float32) * sc, 'router_b': jnp.zeros((E,), jnp.float32), 'w1': jax.random.normal(ks[2], (E, D, H), jnp.float32) * sc, 'b1': jnp.zeros((E, H), jnp.float32), 'w2': jax.random.normal(ks[3], (E, H, D), jnp.float32) * sc, 'b2': jnp.zeros((E, D), jnp.float32), 'ow1': jax.random.normal(ks[4], (D, H), jnp.float32) * sc, 'ob1': jnp.zeros((H,), jnp.float32), 'ow2': jax.random.normal(ks[5], (H, D), jnp.float32) * sc, 'ob2': jnp.zeros((D,), jnp.float32)}
    _L2_ffn_in = _L2_ffn_setup()

    def _L3_attn_setup():
        import jax, jax.numpy as jnp
        import numpy as np
        from jax import lax
        B, T, D, H, K = (8, 256, 128, 16, 64)
        LAYER_ID, N_LAYERS = (6, 12)
        key = jax.random.key(seed)
        ks = jax.random.split(key, 12)
        r01 = LAYER_ID / max(N_LAYERS - 1, 1)
        r10 = 1.0 - LAYER_ID / N_LAYERS
        ddd = (np.arange(D) / D).astype(np.float32)
        conv_w = np.zeros((D, 1, 3), np.float32)
        conv_w[:, 0, 0] = 0.5
        conv_w[:, 0, 2] = 0.5
        decay_speed = (-6.0 + 5.0 * (np.arange(D) / (D - 1)) ** (0.7 + 1.3 * r01)).astype(np.float32)
        u = lambda k, s: jax.random.uniform(k, s, jnp.float32, -0.01, 0.01)
        n = lambda k, s: jax.random.normal(k, s, jnp.float32) / np.sqrt(D)
        return {'x': jax.random.normal(ks[0], (B, T, D), jnp.float32), 'conv_w': jnp.asarray(conv_w), 'maa_x': jnp.asarray(1.0 - ddd ** r10), 'maa_w': jnp.asarray(1.0 - ddd ** r10), 'maa_k': jnp.asarray(1.0 - ddd ** r10), 'maa_v': jnp.asarray(1.0 - (ddd ** r10 + 0.3 * r01)), 'maa_r': jnp.asarray(1.0 - ddd ** (0.5 * r10)), 'maa_g': jnp.asarray(1.0 - ddd ** (0.5 * r10)), 'maa_w1': u(ks[1], (D, 32 * 5)), 'maa_w2': u(ks[2], (5, 32, D)), 'time_decay': jnp.asarray(decay_speed), 'decay_w1': u(ks[3], (D, 64)), 'decay_w2': u(ks[4], (64, D)), 'Wr': n(ks[5], (D, D)), 'Wk': n(ks[6], (D, D)), 'Wv': n(ks[7], (D, D)), 'Wg': n(ks[8], (D, D)), 'Wo': n(ks[9], (D, D)), 'ln_w': jnp.ones((D,), jnp.float32), 'ln_b': jnp.zeros((D,), jnp.float32), 'gate_w': u(ks[10], (D, D)), 'gate_b': 3.0 * jnp.ones((D,), jnp.float32)}
    _L3_attn_in = _L3_attn_setup()

    def _L3_ffn_setup():
        import jax, jax.numpy as jnp
        import numpy as np
        DIM = 128

        def _reference_tuple_inner(x, W_r, W_k, W_v, mu_r, mu_k):
            B, T, C = x.shape
            x_prev = jnp.concatenate([jnp.zeros((B, 1, C), x.dtype), x[:, :-1, :]], axis=1)
            xr = mu_r * x + (1.0 - mu_r) * x_prev
            xk = mu_k * x + (1.0 - mu_k) * x_prev
            r = jax.nn.sigmoid(jnp.einsum('btc,dc->btd', xr, W_r))
            k = jnp.einsum('btc,dc->btd', xk, W_k)
            k_act = jnp.square(jax.nn.relu(k))
            out = r * jnp.einsum('btc,dc->btd', k_act, W_v)
            new_state = x[:, -1, :]
            return (out, new_state)
        key = jax.random.key(seed)
        ks = jax.random.split(key, 6)
        B, T, C = (8, 256, DIM)
        x = jax.random.normal(ks[0], (B, T, C), dtype=jnp.float32)
        s = 1.0 / np.sqrt(C)
        W_r = jax.random.uniform(ks[1], (C, C), jnp.float32, -s, s)
        W_k = jax.random.uniform(ks[2], (C, C), jnp.float32, -s, s)
        W_v = jax.random.uniform(ks[3], (C, C), jnp.float32, -s, s)
        mu_r = jax.random.uniform(ks[4], (C,), jnp.float32)
        mu_k = jax.random.uniform(ks[5], (C,), jnp.float32)
        return {'x': x, 'W_r': W_r, 'W_k': W_k, 'W_v': W_v, 'mu_r': mu_r, 'mu_k': mu_k}
    _L3_ffn_in = _L3_ffn_setup()
    _d = {'L0_attn_x': _L0_attn_in['x'], 'L0_attn_W': _L0_attn_in['W'], 'L0_attn_bias': _L0_attn_in['bias'], 'L0_ffn_W_r': _L0_ffn_in['W_r'], 'L0_ffn_W_k': _L0_ffn_in['W_k'], 'L0_ffn_W_v': _L0_ffn_in['W_v'], 'L0_ffn_mu_r': _L0_ffn_in['mu_r'], 'L0_ffn_mu_k': _L0_ffn_in['mu_k'], 'L1_attn_qkv': _L1_attn_in['qkv'], 'L1_attn_out_w': _L1_attn_in['out_w'], 'L1_attn_rpe_bias': _L1_attn_in['rpe_bias'], 'L1_ffn_gate_w': _L1_ffn_in['gate_w'], 'L1_ffn_gate_b': _L1_ffn_in['gate_b'], 'L1_ffn_w1': _L1_ffn_in['w1'], 'L1_ffn_b1': _L1_ffn_in['b1'], 'L1_ffn_w2': _L1_ffn_in['w2'], 'L1_ffn_b2': _L1_ffn_in['b2'], 'L1_ffn_ln_g': _L1_ffn_in['ln_g'], 'L1_ffn_ln_b': _L1_ffn_in['ln_b'], 'L2_attn_Wq': _L2_attn_in['Wq'], 'L2_attn_Wk': _L2_attn_in['Wk'], 'L2_attn_Wv': _L2_attn_in['Wv'], 'L2_attn_Wo': _L2_attn_in['Wo'], 'L2_ffn_router_w': _L2_ffn_in['router_w'], 'L2_ffn_router_b': _L2_ffn_in['router_b'], 'L2_ffn_w1': _L2_ffn_in['w1'], 'L2_ffn_b1': _L2_ffn_in['b1'], 'L2_ffn_w2': _L2_ffn_in['w2'], 'L2_ffn_b2': _L2_ffn_in['b2'], 'L2_ffn_ow1': _L2_ffn_in['ow1'], 'L2_ffn_ob1': _L2_ffn_in['ob1'], 'L2_ffn_ow2': _L2_ffn_in['ow2'], 'L2_ffn_ob2': _L2_ffn_in['ob2'], 'L3_attn_conv_w': _L3_attn_in['conv_w'], 'L3_attn_maa_x': _L3_attn_in['maa_x'], 'L3_attn_maa_w': _L3_attn_in['maa_w'], 'L3_attn_maa_k': _L3_attn_in['maa_k'], 'L3_attn_maa_v': _L3_attn_in['maa_v'], 'L3_attn_maa_r': _L3_attn_in['maa_r'], 'L3_attn_maa_g': _L3_attn_in['maa_g'], 'L3_attn_maa_w1': _L3_attn_in['maa_w1'], 'L3_attn_maa_w2': _L3_attn_in['maa_w2'], 'L3_attn_time_decay': _L3_attn_in['time_decay'], 'L3_attn_decay_w1': _L3_attn_in['decay_w1'], 'L3_attn_decay_w2': _L3_attn_in['decay_w2'], 'L3_attn_Wr': _L3_attn_in['Wr'], 'L3_attn_Wk': _L3_attn_in['Wk'], 'L3_attn_Wv': _L3_attn_in['Wv'], 'L3_attn_Wg': _L3_attn_in['Wg'], 'L3_attn_Wo': _L3_attn_in['Wo'], 'L3_attn_ln_w': _L3_attn_in['ln_w'], 'L3_attn_ln_b': _L3_attn_in['ln_b'], 'L3_attn_gate_w': _L3_attn_in['gate_w'], 'L3_attn_gate_b': _L3_attn_in['gate_b'], 'L3_ffn_W_r': _L3_ffn_in['W_r'], 'L3_ffn_W_k': _L3_ffn_in['W_k'], 'L3_ffn_W_v': _L3_ffn_in['W_v'], 'L3_ffn_mu_r': _L3_ffn_in['mu_r'], 'L3_ffn_mu_k': _L3_ffn_in['mu_k']}
    _x0 = _d['L0_attn_x']
    _d['L0_attn_x'] = jax.random.normal(jax.random.fold_in(jax.random.key(seed), 1), (4, 1024, 128), dtype=_x0.dtype)
    del _x0
    return _d

def reference(L0_attn_x, L0_attn_W, L0_attn_bias, L0_ffn_W_r, L0_ffn_W_k, L0_ffn_W_v, L0_ffn_mu_r, L0_ffn_mu_k, L1_attn_qkv, L1_attn_out_w, L1_attn_rpe_bias, L1_ffn_gate_w, L1_ffn_gate_b, L1_ffn_w1, L1_ffn_b1, L1_ffn_w2, L1_ffn_b2, L1_ffn_ln_g, L1_ffn_ln_b, L2_attn_Wq, L2_attn_Wk, L2_attn_Wv, L2_attn_Wo, L2_ffn_router_w, L2_ffn_router_b, L2_ffn_w1, L2_ffn_b1, L2_ffn_w2, L2_ffn_b2, L2_ffn_ow1, L2_ffn_ob1, L2_ffn_ow2, L2_ffn_ob2, L3_attn_conv_w, L3_attn_maa_x, L3_attn_maa_w, L3_attn_maa_k, L3_attn_maa_v, L3_attn_maa_r, L3_attn_maa_g, L3_attn_maa_w1, L3_attn_maa_w2, L3_attn_time_decay, L3_attn_decay_w1, L3_attn_decay_w2, L3_attn_Wr, L3_attn_Wk, L3_attn_Wv, L3_attn_Wg, L3_attn_Wo, L3_attn_ln_w, L3_attn_ln_b, L3_attn_gate_w, L3_attn_gate_b, L3_ffn_W_r, L3_ffn_W_k, L3_ffn_W_v, L3_ffn_mu_r, L3_ffn_mu_k):

    def _L0_attn_ref(x, W, bias):
        import jax, jax.numpy as jnp
        import numpy as np
        BLOCK = 128

        def _block_cumsum_flat(x):
            shape = x.shape
            flat = x.reshape(-1, BLOCK)
            y = jnp.cumsum(flat, axis=-1)
            return y.reshape(shape)
        h = jnp.einsum('bsh,oh->bso', x, W) + bias
        return _block_cumsum_flat(h)

    def _L0_ffn_ref(x, W_r, W_k, W_v, mu_r, mu_k):
        import jax, jax.numpy as jnp
        import numpy as np
        DIM = 128

        def _reference_tuple_inner(x, W_r, W_k, W_v, mu_r, mu_k):
            B, T, C = x.shape
            x_prev = jnp.concatenate([jnp.zeros((B, 1, C), x.dtype), x[:, :-1, :]], axis=1)
            xr = mu_r * x + (1.0 - mu_r) * x_prev
            xk = mu_k * x + (1.0 - mu_k) * x_prev
            r = jax.nn.sigmoid(jnp.einsum('btc,dc->btd', xr, W_r))
            k = jnp.einsum('btc,dc->btd', xk, W_k)
            k_act = jnp.square(jax.nn.relu(k))
            out = r * jnp.einsum('btc,dc->btd', k_act, W_v)
            new_state = x[:, -1, :]
            return (out, new_state)
        return _reference_tuple_inner(x, W_r, W_k, W_v, mu_r, mu_k)[0]

    def _L1_attn_ref(x, qkv, out_w, rpe_bias):
        import jax, jax.numpy as jnp
        import numpy as np
        B, S, H, N, D = (2, 256, 128, 16, 64)
        PAD = -30000.0
        q, k, v = jnp.einsum('bsx,xMnd->Mbnsd', x, qkv)
        s = x.shape[1]
        a = jnp.einsum('bnsd,bntd->bnst', q, k) * q.shape[-1] ** (-0.5)
        cum = jnp.cumsum(rpe_bias[:, :s], axis=-1)
        rel = jnp.arange(s)[:, None] - jnp.arange(s)[None, :]
        bias = jnp.where(rel >= 0, cum[:, jnp.clip(rel, 0)], PAD)
        a = jax.nn.softmax(a + bias, axis=-1)
        mix = jnp.einsum('bnst,bntd->bnsd', a, v)
        return jnp.einsum('bnsd,ndx->bsx', mix, out_w)

    def _L1_ffn_ref(x, gate_w, gate_b, w1, b1, w2, b2, ln_g, ln_b):
        import jax, jax.numpy as jnp
        import numpy as np
        TOP_K = 2
        TEMP = 0.9
        EPS = 1e-05
        B, S, D, F, E = (2, 256, 128, 512, 8)

        def _moe_forward(x, gate_w, gate_b, w1, b1, w2, b2, ln_g, ln_b):
            logits = (x @ gate_w + gate_b) / TEMP
            topk_vals, topk_idx = jax.lax.top_k(logits, TOP_K)
            keep = jax.nn.one_hot(topk_idx, E, dtype=jnp.bool_).any(-2)
            masked = jnp.where(keep, logits, -jnp.inf)
            gate_probs = jax.nn.softmax(masked, axis=-1)
            h = jnp.einsum('bsd,edf->bsef', x, w1) + b1
            h = jax.nn.gelu(h, approximate=False)
            expert_out = jnp.einsum('bsef,efd->bsed', h, w2) + b2
            out = jnp.einsum('bse,bsed->bsd', gate_probs, expert_out)
            mu = out.mean(-1, keepdims=True)
            var = out.var(-1, keepdims=True)
            out = (out - mu) / jnp.sqrt(var + EPS) * ln_g + ln_b
            return out
        return _moe_forward(x, gate_w, gate_b, w1, b1, w2, b2, ln_g, ln_b)

    def _L2_attn_ref(x, Wq, Wk, Wv, Wo):
        import math
        import jax, jax.numpy as jnp
        import numpy as np
        NUM_HEAD = 16
        BLOCK_SIZE = 256

        def get_slopes(n):

            def pow2(n):
                start = 2 ** (-2 ** (-(math.log2(n) - 3)))
                return [start * start ** i for i in range(n)]
            if math.log2(n).is_integer():
                return pow2(n)
            c = 2 ** math.floor(math.log2(n))
            return pow2(c) + get_slopes(2 * c)[0::2][:n - c]
        B, T, C = x.shape
        nh, hd = (NUM_HEAD, C // NUM_HEAD)
        q = (x @ Wq).reshape(B, T, nh, hd).transpose(0, 2, 1, 3)
        k = (x @ Wk).reshape(B, T, nh, hd).transpose(0, 2, 1, 3)
        v = (x @ Wv).reshape(B, T, nh, hd).transpose(0, 2, 1, 3)
        attn = jnp.einsum('bhqd,bhkd->bhqk', q, k) / jnp.sqrt(jnp.float32(hd))
        slopes = jnp.asarray(get_slopes(nh), dtype=jnp.float32)
        bias = slopes[:, None] * (jnp.arange(T, dtype=jnp.float32) - (BLOCK_SIZE - 1))
        attn = attn + bias[None, :, None, :]
        causal = jnp.tril(jnp.ones((T, T), dtype=bool))
        masked = jnp.where(causal[None, None], attn.astype(jnp.float32), jnp.finfo(jnp.float32).min)
        probs = jax.nn.softmax(masked, axis=-1)
        out = jnp.einsum('bhqk,bhkd->bhqd', probs, v)
        out = out.transpose(0, 2, 1, 3).reshape(B, T, C)
        return out @ Wo

    def _L2_ffn_ref(input, router_w, router_b, w1, b1, w2, b2, ow1, ob1, ow2, ob2):
        import jax, jax.numpy as jnp
        import numpy as np
        E = 8
        C = 160
        D = 128
        H = 512
        B, S = (4, 256)
        Bq, Sq, Dq = input.shape
        N = Bq * Sq
        xf = input.reshape(N, Dq)
        probs = jax.nn.softmax(xf @ router_w + router_b, axis=-1)
        eid = jnp.argmax(probs, axis=-1)
        onehot = jax.nn.one_hot(eid, E, dtype=xf.dtype)
        rank = (jnp.cumsum(onehot, axis=0)[jnp.arange(N), eid] - 1.0).astype(jnp.int32)
        valid = rank < C
        pos = jnp.where(valid, rank, 0)
        vmask = valid.astype(xf.dtype)[:, None]
        buf = jnp.zeros((E, C, Dq), xf.dtype).at[eid, pos].add(xf * vmask)
        h = jax.nn.relu(jnp.einsum('ecd,edh->ech', buf, w1) + b1[:, None, :])
        y = jnp.einsum('ech,ehd->ecd', h, w2) + b2[:, None, :]
        y_tok = y[eid, pos] * vmask
        yov = jax.nn.relu(xf @ ow1 + ob1) @ ow2 + ob2
        out = y_tok + yov * (1.0 - vmask)
        return out.reshape(Bq, Sq, Dq)

    def _L3_attn_ref(x, conv_w, maa_x, maa_w, maa_k, maa_v, maa_r, maa_g, maa_w1, maa_w2, time_decay, decay_w1, decay_w2, Wr, Wk, Wv, Wg, Wo, ln_w, ln_b, gate_w, gate_b):
        import jax, jax.numpy as jnp
        import numpy as np
        from jax import lax
        B, T, D, H, K = (8, 256, 128, 16, 64)
        LAYER_ID, N_LAYERS = (6, 12)
        B, T, D = x.shape
        H = 16
        K = D // H
        xc = lax.conv_general_dilated(x.transpose(0, 2, 1), conv_w, window_strides=(1,), padding=((1, 1),), feature_group_count=D, dimension_numbers=('NCH', 'OIH', 'NCH')).transpose(0, 2, 1)
        dx = xc - x
        xxx = x + dx * maa_x
        t5 = jnp.tanh(xxx @ maa_w1).reshape(B, T, 5, 32)
        m = jnp.einsum('btfc,fcd->fbtd', t5, maa_w2)
        xw = x + dx * (maa_w + m[0])
        xk = x + dx * (maa_k + m[1])
        xv = x + dx * (maa_v + m[2])
        xr = x + dx * (maa_r + m[3])
        xg = x + dx * (maa_g + m[4])
        r = xr @ Wr
        k = xk @ Wk
        v = xv @ Wv
        g = jax.nn.silu(xg @ Wg)
        w = time_decay + jnp.tanh(xw @ decay_w1) @ decay_w2
        w_log = -jnp.exp(w)
        to_h = lambda a: a.reshape(B, T, H, K).transpose(1, 0, 2, 3)
        r_h, k_h, v_h, wd = (to_h(r), to_h(k), to_h(v), to_h(w_log))
        S0 = jnp.zeros((B, H, K, K), x.dtype)

        def fwd_step(S, inp):
            rt, kt, vt, wt = inp
            S = jnp.exp(wt)[..., None] * S + kt[..., None] * vt[..., None, :]
            return (S, jnp.einsum('bhk,bhkv->bhv', rt, S))
        _, y_f = lax.scan(fwd_step, S0, (r_h, k_h, v_h, wd))

        def bwd_step(S, inp):
            rt, kt, vt, wt = inp
            y = jnp.einsum('bhk,bhkv->bhv', rt, S)
            S = jnp.exp(wt)[..., None] * (S + kt[..., None] * vt[..., None, :])
            return (S, y)
        _, y_b = lax.scan(bwd_step, S0, (r_h, k_h, v_h, wd), reverse=True)
        y = (y_f + y_b).transpose(1, 0, 2, 3).reshape(B, T, D)
        y = y * jax.nn.sigmoid(dx @ gate_w + gate_b)
        eps = 1e-05 * 8.0 ** 2
        yg = y.reshape(B, T, H, K)
        mu = yg.mean(-1, keepdims=True)
        var = yg.var(-1, keepdims=True)
        yn = ((yg - mu) / jnp.sqrt(var + eps)).reshape(B, T, D) * ln_w + ln_b
        return yn * g @ Wo

    def _L3_ffn_ref(x, W_r, W_k, W_v, mu_r, mu_k):
        import jax, jax.numpy as jnp
        import numpy as np
        DIM = 128

        def _reference_tuple_inner(x, W_r, W_k, W_v, mu_r, mu_k):
            B, T, C = x.shape
            x_prev = jnp.concatenate([jnp.zeros((B, 1, C), x.dtype), x[:, :-1, :]], axis=1)
            xr = mu_r * x + (1.0 - mu_r) * x_prev
            xk = mu_k * x + (1.0 - mu_k) * x_prev
            r = jax.nn.sigmoid(jnp.einsum('btc,dc->btd', xr, W_r))
            k = jnp.einsum('btc,dc->btd', xk, W_k)
            k_act = jnp.square(jax.nn.relu(k))
            out = r * jnp.einsum('btc,dc->btd', k_act, W_v)
            new_state = x[:, -1, :]
            return (out, new_state)
        return _reference_tuple_inner(x, W_r, W_k, W_v, mu_r, mu_k)[0]
    x = L0_attn_x
    xn = _layernorm(x, axis=-1)
    x = x + _L0_attn_ref(xn, L0_attn_W, L0_attn_bias) + _L0_ffn_ref(xn, L0_ffn_W_r, L0_ffn_W_k, L0_ffn_W_v, L0_ffn_mu_r, L0_ffn_mu_k)
    xn = _layernorm(x, axis=-1)
    x = x + _L1_attn_ref(xn, L1_attn_qkv, L1_attn_out_w, L1_attn_rpe_bias) + _L1_ffn_ref(xn, L1_ffn_gate_w, L1_ffn_gate_b, L1_ffn_w1, L1_ffn_b1, L1_ffn_w2, L1_ffn_b2, L1_ffn_ln_g, L1_ffn_ln_b)
    xn = _layernorm(x, axis=-1)
    x = x + _L2_attn_ref(xn, L2_attn_Wq, L2_attn_Wk, L2_attn_Wv, L2_attn_Wo) + _L2_ffn_ref(xn, L2_ffn_router_w, L2_ffn_router_b, L2_ffn_w1, L2_ffn_b1, L2_ffn_w2, L2_ffn_b2, L2_ffn_ow1, L2_ffn_ob1, L2_ffn_ow2, L2_ffn_ob2)
    xn = _layernorm(x, axis=-1)
    x = x + _L3_attn_ref(xn, L3_attn_conv_w, L3_attn_maa_x, L3_attn_maa_w, L3_attn_maa_k, L3_attn_maa_v, L3_attn_maa_r, L3_attn_maa_g, L3_attn_maa_w1, L3_attn_maa_w2, L3_attn_time_decay, L3_attn_decay_w1, L3_attn_decay_w2, L3_attn_Wr, L3_attn_Wk, L3_attn_Wv, L3_attn_Wg, L3_attn_Wo, L3_attn_ln_w, L3_attn_ln_b, L3_attn_gate_w, L3_attn_gate_b) + _L3_ffn_ref(xn, L3_ffn_W_r, L3_ffn_W_k, L3_ffn_W_v, L3_ffn_mu_r, L3_ffn_mu_k)
    return x

_drawn_inputs = setup_inputs


def setup_inputs(seed=0):
    import zlib

    import numpy as np

    out = dict(_drawn_inputs(seed))
    spreads = {'L1_ffn_gate_b': (0.0, 0.1),
     'L1_ffn_b1': (0.0, 0.353),
     'L1_ffn_b2': (0.0, 0.1),
     'L1_ffn_ln_g': (1.0, 0.2),
     'L1_ffn_ln_b': (0.0, 0.353),
     'L2_ffn_router_b': (0.0, 0.553),
     'L2_ffn_b1': (0.0, 0.8),
     'L2_ffn_b2': (0.0, 0.674),
     'L2_ffn_ob1': (0.0, 0.8),
     'L2_ffn_ob2': (0.0, 0.499),
     'L3_attn_ln_w': (1.0, 0.6),
     'L3_attn_ln_b': (0.0, 2.0),
     'L3_attn_gate_b': (3.0, 0.6)}
    factors = {'L0_ffn_W_r': 4.956,
     'L0_ffn_mu_r': 6.176,
     'L1_attn_rpe_bias': 8.0,
     'L2_attn_Wq': 8.0,
     'L2_attn_Wk': 8.0,
     'L2_attn_Wv': 8.0,
     'L2_attn_Wo': 8.0,
     'L2_ffn_router_w': 3.541,
     'L2_ffn_w1': 7.904,
     'L2_ffn_w2': 6.084,
     'L2_ffn_ow1': 5.341,
     'L2_ffn_ow2': 4.034,
     'L3_attn_maa_x': 64.0,
     'L3_attn_maa_w': 200.0,
     'L3_attn_maa_w1': 64.0,
     'L3_attn_maa_w2': 64.0,
     'L3_attn_decay_w1': 174.518,
     'L3_attn_decay_w2': 173.021,
     'L3_attn_gate_w': 64.0,
     'L3_ffn_W_r': 8.0,
     'L3_ffn_W_k': 3.451,
     'L3_ffn_W_v': 3.284,
     'L3_ffn_mu_r': 8.0,
     'L3_ffn_mu_k': 6.026,
     'L3_attn_maa_k': 8.0,
     'L3_attn_maa_v': 8.0,
     'L3_attn_maa_r': 8.0,
     'L3_attn_maa_g': 8.0,
     'L3_attn_time_decay': 8.0,
     'L3_attn_Wr': 8.0,
     'L3_attn_Wk': 8.0,
     'L3_attn_Wv': 8.0,
     'L3_attn_Wg': 8.0,
     'L3_attn_Wo': 8.0}
    for name, (base, spread) in spreads.items():
        noise = np.random.default_rng([zlib.crc32(name.encode()), seed]).standard_normal(out[name].shape)
        drawn = base * np.exp(spread * noise) if base else spread * noise
        out[name] = jnp.asarray(drawn.astype(out[name].dtype))
    for name, factor in factors.items():
        out[name] = (out[name] * factor).astype(out[name].dtype)
    return out
```

```python
import concourse.bass as bass
from concourse import mybir
from contextlib import ExitStack
import numpy as np

F32 = mybir.dt.float32
BF16 = mybir.dt.bfloat16
U32 = mybir.dt.uint32
I32 = mybir.dt.int32
ALU = mybir.AluOpType
ACT = mybir.ActivationFunctionType
AX = mybir.AxisListType

P = 128
B, T = 4, 1024
N = B * T
NT = N // P
TT = T // P
CH = 512
CT = CH // P
TP = T + 2
LN_EPS = 1e-5


class Phase:

    def __init__(self, nc, tag):
        self.nc, self.tag, self.ctx, self.sems = nc, tag, ExitStack(), []

    def sb(self, name, shape, dt=F32):
        return self.ctx.enter_context(self.nc.sbuf_tensor(f"{self.tag}_{name}", shape, dt))

    def ps(self, name, shape=(P, CH), dt=F32):
        return self.ctx.enter_context(self.nc.psum_tensor(f"{self.tag}_{name}", list(shape), dt))

    def sem(self, name):
        s = self.nc.alloc_semaphore(f"{self.tag}_{name}")
        self.sems.append(s)
        return s

    def end(self):
        self.nc.clear_and_free_semaphores(self.sems)
        self.nc.all_engine_barrier()
        self.ctx.close()


def load_columns(sp, sem, dst, src, lo=0, hi=None):
    hi = hi or src.shape[1]
    cuts = list(range(lo, hi, 2048)) + [hi]
    for a, z in zip(cuts, cuts[1:]):
        sp.dma_start(dst[:, a:z], src[:, a:z]).then_inc(sem, 16)
    return 16 * (len(cuts) - 1)


def constants(nc, G, wts, first):
    ph = Phase(nc, "init")
    loaded, made = ph.sem("loaded"), ph.sem("made")
    with nc.Block() as block:
        @block.sync
        def _(sp):
            sp.dma_start(G["X"][:, :, :], G["x_dram"].rearrange("(n p) d -> p n d", p=P)).then_inc(loaded, 16)
            n = 16 + load_columns(sp, loaded, G["WA"], wts[0], 0, first)
            G["in1_n"] = load_columns(sp, G["in1"], G["WA"], wts[0], first)
            G["in2_n"] = load_columns(sp, G["in2"], G["WB"], wts[1])
            sp.wait_ge(loaded, n)

        @block.gpsimd
        def _(pool):
            pool.memset(G["ident"][:, :], 0.0).then_inc(made, 1)
            pool.memset(G["tri"][:, :], 1.0).then_inc(made, 1)
            pool.memset(G["ones"][:, :], 1.0).then_inc(made, 1)
            pool.memset(G["XNT"][:, :, 0:1], 0.0)
            pool.memset(G["XNT"][:, :, TP - 1:TP], 0.0)
            pool.memset(G["eps"][:, :], LN_EPS)
            pool.wait_ge(made, 3)
            pool.affine_select(out=G["ident"][:, :], in_=G["ident"][:, :], compare_op=ALU.not_equal, fill=1.0,
                               base=0, pattern=[[-1, P]], channel_multiplier=1).then_inc(made, 1)
            pool.affine_select(out=G["tri"][:, :], in_=G["tri"][:, :], compare_op=ALU.is_ge, fill=0.0,
                               base=0, pattern=[[1, P]], channel_multiplier=-1).then_inc(made, 1)
    ph.end()


def layernorm(nc, G, tag, loads=None):
    ph = Phase(nc, tag)
    X, XNT = G["X"], G["XNT"]
    stats = ph.sb("stats", [P, NT, 6])
    mean = ph.sb("mean", [P, NT])
    half = ph.sb("half", [P, NT])
    sq = ph.sb("sq", [P, NT])
    m2 = ph.sb("m2", [P, NT])
    var = ph.sb("var", [P, NT])
    sd = ph.sb("sd", [P, NT])
    rstd = ph.sb("rstd", [P, NT])
    XR = G["XR"]
    pst = [ph.ps(f"t{i}") for i in range(2)]
    stats_done, mv_done, sd_done, rstd_done = (ph.sem(n) for n in ("stats", "mv", "sd", "rstd"))
    xn_done, tr_done, out_done = (ph.sem(n) for n in ("xn", "tr", "out"))
    with nc.Block() as block:
        if loads:
            @block.sync
            def _(sp):
                loads(sp)

        @block.vector
        def _(dve):
            with dve.Fori(0, NT // CT) as c:
                for k in range(CT):
                    ins = dve.bn_stats(stats[:, c * CT + k, :], X[:, c * CT + k, :])
                ins.then_inc(stats_done, 1)
            dve.wait_ge(stats_done, NT // CT)
            dve.tensor_tensor(mean[:, :], stats[:, :, 1], stats[:, :, 4], ALU.add)
            dve.tensor_tensor(half[:, :], stats[:, :, 1], stats[:, :, 4], ALU.subtract)
            dve.tensor_tensor(m2[:, :], stats[:, :, 2], stats[:, :, 5], ALU.add).then_inc(stats_done, 1)
            dve.wait_ge(stats_done, NT // CT + 1)
            dve.tensor_scalar(mean[:, :], mean[:, :], 0.5, None, ALU.mult)
            dve.tensor_tensor(sq[:, :], half[:, :], half[:, :], ALU.mult)
            dve.tensor_scalar(m2[:, :], m2[:, :], 4.0 / P, None, ALU.mult).then_inc(stats_done, 1)
            dve.wait_ge(stats_done, NT // CT + 2)
            dve.tensor_tensor(var[:, :], sq[:, :], m2[:, :], ALU.add).then_inc(mv_done, 1)
            dve.wait_ge(sd_done, 1)
            dve.reciprocal(rstd[:, :], sd[:, :]).then_inc(rstd_done, 1)
            dve.wait_ge(rstd_done, 1)
            with dve.Fori(0, B) as b:
                for h in range(2):
                    for k in range(CT):
                        n = b * TT + (h * CT + k)
                        ins = dve.tensor_scalar(XR[:, n, :], X[:, n, :], mean[:, bass.ds(n, 1)], rstd[:, bass.ds(n, 1)],
                                                ALU.subtract, ALU.mult)
                    ins.then_inc(xn_done, 1)

        @block.scalar
        def _(act):
            act.wait_ge(mv_done, 1)
            act.activation(sd[:, :], var[:, :], ACT.Sqrt, bias=G["eps"][:, 0:1], scale=0.25).then_inc(sd_done, 1)
            with act.Fori(0, B) as b:
                for h in range(2):
                    act.wait_ge(tr_done, b * 2 + h + 1)
                    act.copy(XNT[:, b, 1 + h * CH:1 + (h + 1) * CH], pst[h][:, :]).then_inc(out_done, 1)

        @block.tensor
        def _(pe):
            for c in range(NT // CT):
                pe.wait_ge(xn_done, c + 1)
                if c >= 2:
                    pe.wait_ge(out_done, c - 1)
                for k in range(CT):
                    ins = pe.transpose(pst[c % 2][:, k * P:(k + 1) * P], XR[:, c * CT + k, :], G["ident"][:, :])
                ins.then_inc(tr_done, 1)
    ph.end()


def channel_mix(nc, G, tag, wr, wk, wv, mu_r, mu_k, attn=None):
    ph = Phase(nc, tag)
    X, XNT = G["X"], G["XNT"]
    dx = ph.sb("dx", [P, 2, CH])
    xr = ph.sb("xr", [P, 2, CH])
    xk = ph.sb("xk", [P, 2, CH])
    sig = ph.sb("sig", [P, 2, CH])
    kr = ph.sb("kr", [P, 2, CH])
    k2 = ph.sb("k2", [P, 2, CH])
    prod = ph.sb("prod", [P, 2, CH])
    delta = ph.sb("delta", [P, 2, CH])
    wc = ph.sb("wc", [P, P])
    bc = ph.sb("bc", [P, 1])
    psr = [ph.ps(f"r{i}") for i in range(2)]
    psk = [ph.ps(f"k{i}") for i in range(2)]
    psa = [ph.ps(f"a{i}") for i in range(2)]
    names = ("dx", "mixed", "rk", "relu", "k2", "v", "prod", "delta", "tr", "x", "wcp", "wc")
    dx_done, mixed, rk_done, relu_done, k2_done, v_done, prod_done, delta_done, tr_done, x_done, wc_psum, wc_done = (
        ph.sem(n) for n in names)
    with nc.Block() as block:
        @block.vector
        def _(dve):
            if attn:
                dve.wait_ge(wc_psum, 1)
                dve.tensor_copy(wc[:, :], psa[0][:, 0:P]).then_inc(wc_done, 1)
                dve.tensor_copy(bc[:, :], psa[0][:, P:P + 1]).then_inc(wc_done, 1)
                dve.wait_ge(wc_done, 2)
            with dve.Fori(0, B) as b:
                for h in range(2):
                    c = b * 2 + h
                    cur = XNT[:, b, 1 + h * CH:1 + (h + 1) * CH]
                    prev = XNT[:, b, h * CH:(h + 1) * CH]
                    dve.tensor_tensor(dx[:, h, :], cur, prev, ALU.subtract).then_inc(dx_done, 1)
                    dve.wait_ge(dx_done, c + 1)
                    dve.scalar_tensor_tensor(xr[:, h, :], dx[:, h, :], mu_r, prev, ALU.mult, ALU.add)
                    dve.scalar_tensor_tensor(xk[:, h, :], dx[:, h, :], mu_k, prev, ALU.mult,
                                             ALU.add).then_inc(mixed, 1)
                for h in range(2):
                    c = b * 2 + h
                    dve.wait_ge(v_done, c + 1)
                    if attn:
                        dve.tensor_tensor(prod[:, h, :], sig[:, h, :], psr[h][:, :], ALU.mult).then_inc(prod_done, 1)
                        dve.wait_ge(prod_done, c + 1)
                        dve.scalar_tensor_tensor(delta[:, h, :], psa[h][:, :], bc[:, 0:1], prod[:, h, :], ALU.add,
                                                 ALU.add).then_inc(delta_done, 1)
                    else:
                        dve.tensor_tensor(delta[:, h, :], sig[:, h, :], psr[h][:, :], ALU.mult).then_inc(delta_done, 1)
                for h in range(2):
                    c = b * 2 + h
                    dve.wait_ge(tr_done, c + 1)
                    xv = X[:, bass.ds(b * TT + h * CT, CT), :]
                    dve.tensor_tensor(xv, xv, psk[h][:, :].rearrange("p (k d) -> p k d", k=CT),
                                      ALU.add).then_inc(x_done, 1)

        @block.scalar
        def _(act):
            with act.Fori(0, B) as b:
                for h in range(2):
                    c = b * 2 + h
                    act.wait_ge(rk_done, c + 1)
                    act.activation(sig[:, h, :], psr[h][:, :], ACT.Sigmoid)
                    act.activation(kr[:, h, :], psk[h][:, :], ACT.Relu).then_inc(relu_done, 1)
                    act.wait_ge(relu_done, c + 1)
                    act.activation(k2[:, h, :], kr[:, h, :], ACT.Square).then_inc(k2_done, 1)

        @block.tensor
        def _(pe):
            if attn:
                pe.matmul(psa[0][:, 0:P], attn[0], G["tri"][:, :], start=True, stop=True)
                pe.matmul(psa[0][:, P:P + 1], G["tri"][:, :], attn[1], start=True, stop=True).then_inc(wc_psum, 1)
                pe.wait_ge(wc_done, 2)
            pe.sem_inc(x_done, 2)
            with pe.Fori(0, B) as b:
                for h in range(2):
                    c = b * 2 + h
                    pe.wait_ge(mixed, c + 1)
                    pe.wait_ge(x_done, c + 1)
                    pe.matmul(psr[h][:, :], wr, xr[:, h, :], start=True, stop=True)
                    ins = pe.matmul(psk[h][:, :], wk, xk[:, h, :], start=True, stop=True)
                    ins.then_inc(rk_done, 1)
                    if attn:
                        pe.matmul(psa[h][:, :], wc[:, :], XNT[:, b, 1 + h * CH:1 + (h + 1) * CH], start=True, stop=True)
                for h in range(2):
                    c = b * 2 + h
                    pe.wait_ge(k2_done, c + 1)
                    pe.matmul(psr[h][:, :], wv, k2[:, h, :], start=True, stop=True).then_inc(v_done, 1)
                for h in range(2):
                    c = b * 2 + h
                    pe.wait_ge(delta_done, c + 1)
                    for k in range(CT):
                        ins = pe.transpose(psk[h][:, k * P:(k + 1) * P], delta[:, h, k * P:(k + 1) * P], G["ident"][:, :])
                    ins.then_inc(tr_done, 1)
    ph.end()


def tables(nc, G, rpe, slopes, tab1, tab2):
    ph = Phase(nc, "tab")
    K = P - 1
    S = 256
    t1 = ph.sb("t1", [16, K + T])
    t2 = ph.sb("t2", [16, K + T])
    dist = ph.sb("dist", [16, T])
    zero = ph.sb("zero", [16, T])
    made, scanned, filled, stored = (ph.sem(n) for n in ("made", "scanned", "filled", "stored"))
    with nc.Block() as block:
        @block.gpsimd
        def _(pool):
            pool.iota(dist[:, :], [[1, T]], base=0, channel_multiplier=0, allow_small_or_imprecise_dtypes=True)
            pool.memset(zero[:, :], 0.0)
            pool.memset(t1[:, 0:K], -30000.0)
            pool.memset(t2[:, 0:K], -3.0e38).then_inc(made, 1)

        @block.vector
        def _(dve):
            dve.wait_ge(made, 1)
            dve.tensor_tensor_scan(t1[:, K:K + S], rpe, zero[:, 0:S], 0.0, ALU.add, ALU.add).then_inc(scanned, 1)
            dve.tensor_scalar(t2[:, K:K + T], dist[:, :], slopes, None, ALU.mult)
            dve.wait_ge(scanned, 1)
            dve.tensor_scalar(t1[:, K + S:K + T], zero[:, S:T], t1[:, K + S - 1:K + S], None,
                              ALU.add).then_inc(filled, 1)

        @block.sync
        def _(sp):
            sp.wait_ge(filled, 1)
            sp.dma_start(tab1, t1[:, :]).then_inc(stored, 16)
            sp.dma_start(tab2, t2[:, :]).then_inc(stored, 16)
            sp.wait_ge(stored, 32)
    ph.end()


def attention(nc, G, tag, hd, heads, wq_all, wk_all, wv_all, wo_all, tab, scale):
    ph = Phase(nc, tag)
    X, XNT = G["X"], G["XNT"]
    HG = 2 if hd == 64 else 4
    RS = P // HG
    NG = heads // HG
    MV = HG * hd
    U = HG * TT
    units = [(u, i) for i in range(TT) for u in range(HG)]
    K = P - 1
    wq, wk = ph.sb("wq", [P, P]), ph.sb("wk", [P, P])
    wv, wo = ph.sb("wv", [P, MV]), ph.sb("wo", [MV, P])
    tb = ph.sb("tb", [P, HG, T])
    QT, KT, vT = ph.sb("QT", [P, T]), ph.sb("KT", [P, T]), ph.sb("vT", [MV, T])
    V = ph.sb("V", [P, TT, MV])
    NS = 2
    Sb = ph.sb("S", [P, NS, T])
    Pb = ph.sb("P", [P, NS, T])
    PT = ph.sb("PT", [P, NS, T])
    mix = ph.sb("mix", [P, TT, MV])
    mT = ph.sb("mT", [MV, T])
    nmax, rsum, rinv = (ph.sb(n, [P, U]) for n in ("nmax", "rsum", "rinv"))
    DT = G["XR"][:, :, :].rearrange("p (b k) d -> p b (k d)", b=B)
    pS = [ph.ps(f"S{i}", (P, 2 * CH)) for i in range(2)]
    pT = [ph.ps(f"T{i}") for i in range(2)]
    pO = [ph.ps(f"O{i}") for i in range(2)]
    runs = [(n, r) for n, (u, i) in enumerate(units) for r in range(i // CT + 1)]
    last_run = {n: k for k, (n, r) in enumerate(runs)}
    R = len(runs)
    w_in, w_copied, group_done, dt_zero = (ph.sem(n) for n in ("win", "wcopied", "groupdone", "dtzero"))
    q_ps, k_ps, v_ps, q_sb, k_sb, v_sb = (ph.sem(n) for n in ("qps", "kps", "vps", "qsb", "ksb", "vsb"))
    vt_ps, vt_sb = ph.sem("vtps"), ph.sem("vtsb")
    s_ps, s_sb, p_sb, t_ps, t_sb_a, t_sb_d, o_ps, o_sb, r_inv = (
        ph.sem(n) for n in ("sps", "ssb", "psb", "tps", "tsba", "tsbd", "ops", "osb", "rinv"))
    passed, passed_pe = ph.sem("passed"), ph.sem("passedpe")
    m_ps, m_sb, y_ps, y_sb, f_ps, f_sb = (ph.sem(n) for n in ("mps", "msb", "yps", "ysb", "fps", "fsb"))
    on_act = [n % 3 != 2 for n, r in runs]
    acts = [k for k in range(R) if on_act[k]]
    dves = [k for k in range(R) if not on_act[k]]

    def nth(k):
        return (t_sb_a, len(acts), acts.index(k) + 1) if on_act[k] else (t_sb_d, len(dves), dves.index(k) + 1)

    def length(i):
        return (i + 1) * P

    with nc.Block() as block:
        @block.sync
        def _(sp):
            with sp.Fori(0, NG) as g:
                sp.wait_ge(group_done, g + 1)
                for u in range(HG):
                    src = bass.AP(tab.tensor, (g * HG + u) * (K + T), [[1, P], [1, T]])
                    sp.dma_start(tb[:, u, :], src).then_inc(w_in, 16)

        @block.gpsimd
        def _(pool):
            pool.memset(DT[:, :, :], 0.0).then_inc(dt_zero, 1)
            pool.sem_inc(group_done, 1)
            with pool.Fori(0, NG) as g:
                pool.wait_ge(group_done, g + 1)
                pool.tensor_copy(wq[:, :], wq_all[:, bass.ds(g * P, P)])
                pool.tensor_copy(wk[:, :], wk_all[:, bass.ds(g * P, P)])
                pool.tensor_copy(wv[:, :], wv_all[:, bass.ds(g * MV, MV)])
                pool.tensor_copy(wo[:, :], wo_all[:, bass.ds(g * P, P)]).then_inc(w_copied, 1)

        @block.tensor
        def _(pe):
            def scores(n, it):
                u, i = units[n]
                if n >= 2:
                    pe.wait_ge(s_sb, it * U + n - 1)
                rows = slice(u * RS, u * RS + hd)
                for lo in range(0, length(i), CH):
                    hi = min(lo + CH, length(i))
                    ins = pe.matmul(pS[n % 2][:, lo:hi], QT[rows, i * P:(i + 1) * P], KT[rows, lo:hi],
                                    start=True, stop=True)
                ins.then_inc(s_ps, 1)

            def transposes(n, it):
                u, i = units[n]
                pe.wait_ge(p_sb, it * U + n + 1)
                for k, (m, r) in enumerate(runs):
                    if m != n:
                        continue
                    if k >= 2:
                        s, per, place = nth(k - 2)
                        pe.wait_ge(s, it * per + place)
                    for j in range(r * CT, min(r * CT + CT, i + 1)):
                        ins = pe.transpose(pT[k % 2][:, (j % CT) * P:(j % CT + 1) * P], Pb[:, n % NS, j * P:(j + 1) * P],
                                           G["ident"][:, :])
                    ins.then_inc(t_ps, 1)

            def values(n, it):
                u, i = units[n]
                s, per, place = nth(last_run[n])
                pe.wait_ge(s, it * per + place)
                if n >= 2:
                    pe.wait_ge(o_sb, it * U + n - 1)
                for j in range(i + 1):
                    ins = pe.matmul(pO[n % 2][:, 0:hd], PT[:, n % NS, j * P:(j + 1) * P], V[:, j, u * hd:(u + 1) * hd],
                                    start=(j == 0), stop=(j == i))
                ins.then_inc(o_ps, 1)

            pe.wait_ge(dt_zero, 1)
            with pe.Fori(0, NG) as g:
                with pe.Fori(0, B) as b:
                    it = g * B + b
                    pe.wait_ge(w_copied, g + 1)
                    for half in range(2):
                        x = XNT[:, b, 1 + half * CH:1 + (half + 1) * CH]
                        cut = slice(half * CH, (half + 1) * CH)
                        pe.matmul(pS[0][:, cut], wq[:, :], x, start=True, stop=True)
                        ins = pe.matmul(pS[1][:, cut], wk[:, :], x, start=True, stop=True)
                        ins.then_inc(q_ps, 1)
                    for half in range(2):
                        x = XNT[:, b, 1 + half * CH:1 + (half + 1) * CH]
                        pe.matmul(pT[half][0:MV, :], wv[:, :], x, start=True, stop=True).then_inc(v_ps, 1)
                    pe.wait_ge(v_sb, it + 1)
                    pe.sem_inc(passed_pe, 1)
                    for j in range(TT):
                        ins = pe.transpose(pT[j // CT][:, (j % CT) * MV:(j % CT + 1) * MV], vT[:, j * P:(j + 1) * P],
                                           G["ident"][0:MV, 0:MV])
                    ins.then_inc(vt_ps, 1)
                    pe.wait_ge(q_sb, it + 1)
                    pe.wait_ge(k_sb, it + 1)
                    scores(0, it)
                    pe.wait_ge(vt_sb, it + 1)
                    for n in range(U):
                        if n + 1 < U:
                            scores(n + 1, it)
                        transposes(n, it)
                        if n >= 1:
                            values(n - 1, it)
                    values(U - 1, it)
                    pe.wait_ge(o_sb, it * U + U)
                    for j in range(TT):
                        ins = pe.transpose(pS[0][0:MV, j * P:(j + 1) * P], mix[:, j, :], G["ident"][:, :])
                    ins.then_inc(m_ps, 1)
                    pe.wait_ge(m_sb, it + 1)
                    for half in range(2):
                        cut = slice(half * CH, (half + 1) * CH)
                        ins = pe.matmul(pS[1][:, cut], wo[:, :], mT[:, cut], start=True, stop=True)
                    ins.then_inc(y_ps, 1)
                    pe.wait_ge(y_sb, it + 1)
                pe.sem_inc(group_done, 1)
            for c in range(NT // CT):
                if c >= 2:
                    pe.wait_ge(f_sb, c - 1)
                for j in range(CT):
                    t = c * CT + j
                    ins = pe.transpose(pT[c % 2][:, j * P:(j + 1) * P], DT[:, t // TT, (t % TT) * P:(t % TT + 1) * P],
                                       G["ident"][:, :])
                ins.then_inc(f_ps, 1)

        @block.scalar
        def _(act):
            with act.Fori(0, NG) as g:
                with act.Fori(0, B) as b:
                    it = g * B + b
                    act.wait_ge(q_ps, it * 2 + 2)
                    act.activation(QT[:, :], pS[0][:, :], ACT.Copy, scale=scale).then_inc(q_sb, 1)
                    act.wait_ge(v_ps, it * 2 + 2)
                    act.copy(vT[:, 0:CH], pT[0][0:MV, :])
                    act.copy(vT[:, CH:T], pT[1][0:MV, :]).then_inc(v_sb, 1)
                    act.wait_ge(vt_ps, it + 1)
                    for h in range(2):
                        ins = act.copy(V[:, h * CT:(h + 1) * CT, :],
                                       pT[h][:, 0:CT * MV].rearrange("p (k m) -> p k m", k=CT))
                    ins.then_inc(vt_sb, 1)

                    def copies(n):
                        u, i = units[n]
                        for k, (m, r) in enumerate(runs):
                            if m == n and on_act[k]:
                                act.wait_ge(t_ps, it * R + k + 1)
                                cut = slice(r * CH, min(r * CH + CH, length(i)))
                                act.copy(PT[:, n % NS, cut], pT[k % 2][:, 0:cut.stop - cut.start]).then_inc(t_sb_a, 1)

                    for n in range(U):
                        u, i = units[n]
                        act.wait_ge(s_sb, it * U + n + 1)
                        if n >= NS:
                            act.wait_ge(t_ps, it * R + last_run[n - NS] + 1)
                        act.activation(Pb[:, n % NS, 0:length(i)], Sb[:, n % NS, 0:length(i)], ACT.Exp,
                                       bias=nmax[:, n:n + 1], scale=-1.0, accum_out=rsum[:, n:n + 1]).then_inc(p_sb, 1)
                        if n >= 1:
                            copies(n - 1)
                    copies(U - 1)
                    act.wait_ge(m_ps, it + 1)
                    act.copy(mT[:, :], pS[0][0:MV, :]).then_inc(m_sb, 1)

        @block.vector
        def _(dve):
            with dve.Fori(0, NG) as g:
                with dve.Fori(0, B) as b:
                    it = g * B + b
                    dve.wait_ge(w_in, g * 16 * HG + 16 * HG)
                    dve.wait_ge(q_ps, it * 2 + 2)
                    dve.tensor_copy(KT[:, :], pS[1][:, :]).then_inc(k_sb, 1)

                    def copies(n):
                        u, i = units[n]
                        for k, (m, r) in enumerate(runs):
                            if m == n and not on_act[k]:
                                dve.wait_ge(t_ps, it * R + k + 1)
                                cut = slice(r * CH, min(r * CH + CH, length(i)))
                                dve.tensor_copy(PT[:, n % NS, cut], pT[k % 2][:, 0:cut.stop - cut.start])\
                                   .then_inc(t_sb_d, 1)

                    def normalise(n):
                        u, i = units[n]
                        dve.wait_ge(p_sb, it * U + n + 1)
                        dve.reciprocal(rinv[:, n:n + 1], rsum[:, n:n + 1]).then_inc(r_inv, 1)
                        dve.wait_ge(o_ps, it * U + n + 1)
                        dve.wait_ge(r_inv, it * U + n + 1)
                        dve.tensor_scalar(mix[:, i, u * hd:(u + 1) * hd], pO[n % 2][:, 0:hd], rinv[:, n:n + 1], None,
                                          ALU.mult).then_inc(o_sb, 1)

                    for n in range(U):
                        u, i = units[n]
                        L = length(i)
                        dve.wait_ge(s_ps, it * U + n + 1)
                        if n >= NS:
                            dve.wait_ge(p_sb, it * U + n - NS + 1)
                        dve.sem_inc(passed, 1)
                        dve.tensor_tensor_reduce(out=Sb[:, n % NS, 0:L], in0=pS[n % 2][:, 0:L],
                                                 in1=tb[:, u, L - 1::-1], scale=-1.0, scalar=3.0e38,
                                                 op0=ALU.add, op1=ALU.min, accum_out=nmax[:, n:n + 1]).then_inc(s_sb, 1)
                        if n >= 1:
                            copies(n - 1)
                        if n >= 2:
                            normalise(n - 2)
                    copies(U - 1)
                    normalise(U - 2)
                    normalise(U - 1)
                    dve.wait_ge(y_ps, it + 1)
                    dve.tensor_tensor(DT[:, b, :], DT[:, b, :], pS[1][:, :], ALU.add).then_inc(y_sb, 1)
            for c in range(NT // CT):
                dve.wait_ge(f_ps, c + 1)
                xv = X[:, c * CT:(c + 1) * CT, :]
                dve.tensor_tensor(xv, xv, pT[c % 2][:, :].rearrange("p (k d) -> p k d", k=CT), ALU.add).then_inc(f_sb, 1)
    ph.end()


def moe_top2(nc, G, tag, gw, gb, w1, b1, w2, b2, rows):
    ph = Phase(nc, tag)
    X, XNT = G["X"], G["XNT"]
    E, FC = 8, 4
    lng, lnb = ph.sb("lng", [P, P]), ph.sb("lnb", [P, P])
    lg = ph.sb("lg", [P, CH])
    lgt, ex, pr = (ph.sb(n, [P, CT, E]) for n in ("lgt", "ex", "pr"))
    mx = ph.sb("mx", [P, CT, E])
    mi = ph.sb("mi", [P, CT, E], U32)
    mf, keep1, keep = (ph.sb(n, [P, CT, E]) for n in ("mf", "keep1", "keep"))
    io = ph.sb("io", [P, CT, E])
    sm, ri = ph.sb("sm", [P, CT]), ph.sb("ri", [P, CT])
    prT = ph.sb("prT", [E, CH])
    h = ph.sb("h", [P, 2, FC, CH])
    acc = ph.sb("acc", [P, CT, P])
    st, mv = ph.sb("st", [P, CT, 6]), ph.sb("mv", [P, CT, 2])
    sd, rs = ph.sb("sd", [P, CT]), ph.sb("rs", [P, CT])
    on = ph.sb("on", [P, CT, P])
    pU = [ph.ps(f"U{i}") for i in range(3)]
    pY = [ph.ps(f"Y{i}") for i in range(2)]
    pR = ph.ps("R")
    rows_in, io_done = ph.sem("rowsin"), ph.sem("iodone")
    names = ("lg_ps", "lg_sb", "lgt_ps", "lgt_sb", "mx_done", "mi_done", "mf_done", "keep1_done", "keep_done", "sub_done",
             "exp_done", "mask_done", "sum_done", "ri_done", "pr_done", "prT_ps", "prT_sb", "bias_ps", "acc0", "st_done",
             "mv_done", "sd_done", "rs_done", "on_done", "aff_done", "x_done")
    S = {n: ph.sem(n) for n in names}
    up, gelu, down, added = (ph.sem(n) for n in ("up", "gelu", "down", "added"))
    with nc.Block() as block:
        @block.sync
        def _(sp):
            sp.dma_start(lng[:, :], bass.AP(rows.tensor, 0, [[0, P], [1, P]])).then_inc(rows_in, 16)
            sp.dma_start(lnb[:, :], bass.AP(rows.tensor, P, [[0, P], [1, P]])).then_inc(rows_in, 16)
            sp.wait_ge(rows_in, 32)

        @block.gpsimd
        def _(pool):
            pool.iota(io[:, :, :], [[0, CT], [1, E]], base=0, channel_multiplier=0,
                      allow_small_or_imprecise_dtypes=True).then_inc(io_done, 1)
            pool.memset(lg[:, :], 0.0).then_inc(io_done, 1)

        @block.tensor
        def _(pe):
            with pe.Fori(0, B) as b:
                with pe.Fori(0, 2) as half:
                    c = b * 2 + half
                    x = XNT[:, b, bass.ds(half * CH + 1, CH)]

                    def ups(e):
                        for f in range(FC):
                            n = e * FC + f
                            if n >= 3:
                                pe.wait_ge(gelu, c * (E * FC) + n - 2)
                            pe.matmul(pU[n % 3][:, :], w1[:, n * P:(n + 1) * P], x, start=True, stop=True).then_inc(up, 1)

                    def downs(e):
                        pe.wait_ge(gelu, c * (E * FC) + (e + 1) * FC)
                        if e >= 2:
                            pe.wait_ge(added, c * E + e - 1)
                        for k in range(CT):
                            for f in range(FC):
                                ins = pe.matmul(pY[e % 2][:, k * P:(k + 1) * P], h[:, e % 2, f, k * P:(k + 1) * P],
                                                w2[:, (e * FC + f) * P:(e * FC + f + 1) * P],
                                                start=(f == 0), stop=(f == FC - 1))
                        ins.then_inc(down, 1)

                    pe.matmul(pR[0:E, :], gw, x, start=True, stop=True).then_inc(S["lg_ps"], 1)
                    ups(0)
                    pe.wait_ge(S["lg_sb"], c + 1)
                    for k in range(CT):
                        ins = pe.transpose(pR[:, k * P:(k + 1) * P], lg[:, k * P:(k + 1) * P], G["ident"][:, :])
                    ins.then_inc(S["lgt_ps"], 1)
                    ups(1)
                    pe.wait_ge(S["pr_done"], c + 1)
                    for k in range(CT):
                        ins = pe.transpose(pR[0:E, k * P:(k + 1) * P], pr[:, k, :], G["ident"][:, :])
                    ins.then_inc(S["prT_ps"], 1)
                    pe.wait_ge(S["prT_sb"], c + 1)
                    for k in range(CT):
                        ins = pe.matmul(pR[:, k * P:(k + 1) * P], prT[:, k * P:(k + 1) * P], b2, start=True, stop=True)
                    ins.then_inc(S["bias_ps"], 1)
                    for e in range(E):
                        downs(e)
                        if e + 2 < E:
                            ups(e + 2)
                    pe.wait_ge(added, c * E + E)
                    pe.wait_ge(S["acc0"], c + 1)

        @block.scalar
        def _(act):
            with act.Fori(0, B) as b:
                with act.Fori(0, 2) as half:
                    c = b * 2 + half

                    def gelus(e):
                        if e >= 2:
                            act.wait_ge(down, c * E + e - 1)
                        for f in range(FC):
                            n = e * FC + f
                            act.wait_ge(up, c * (E * FC) + n + 1)
                            act.activation(h[:, e % 2, f, :], pU[n % 3][:, :], ACT.Gelu, bias=b1[:, n:n + 1]).then_inc(gelu, 1)

                    gelus(0)
                    act.wait_ge(S["sub_done"], c + 1)
                    act.activation(ex[:, :, :], ex[:, :, :], ACT.Exp).then_inc(S["exp_done"], 1)
                    for e in range(1, E):
                        gelus(e)
                    act.wait_ge(S["mv_done"], c + 1)
                    act.activation(sd[:, :], mv[:, :, 1], ACT.Sqrt, bias=G["eps"][:, 0:1]).then_inc(S["sd_done"], 1)

        @block.vector
        def _(dve):
            dve.wait_ge(io_done, 2)
            dve.wait_ge(rows_in, 32)
            with dve.Fori(0, B) as b:
                with dve.Fori(0, 2) as half:
                    c = b * 2 + half

                    def step(name, ins):
                        ins.then_inc(S[name], 1)
                        dve.wait_ge(io_done, 1)
                        dve.wait_ge(S[name], c + 1)

                    dve.wait_ge(S["lg_ps"], c + 1)
                    dve.tensor_scalar(lg[0:E, :], pR[0:E, :], gb, 1.0 / 0.9, ALU.add, ALU.mult).then_inc(S["lg_sb"], 1)
                    dve.wait_ge(S["lgt_ps"], c + 1)
                    step("lgt_sb", dve.tensor_copy(lgt[:, :, :], pR[:, :].rearrange("p (k e) -> p k e", k=CT)[:, :, 0:E]))
                    for k in range(CT):
                        ins = dve.max(mx[:, k, :], lgt[:, k, :])
                    step("mx_done", ins)
                    for k in range(CT):
                        ins = dve.max_index(mi[:, k, :], mx[:, k, :], lgt[:, k, :])
                    ins.then_inc(S["mi_done"], 1)
                    dve.tensor_tensor(ex[:, :, :], lgt[:, :, :], mx[:, :, 0:1].to_broadcast([P, CT, E]),
                                      ALU.subtract).then_inc(S["sub_done"], 1)
                    dve.wait_ge(S["mi_done"], c + 1)
                    step("mf_done", dve.tensor_copy(mf[:, :, :], mi[:, :, :]))
                    dve.tensor_tensor(keep1[:, :, :], io[:, :, :], mf[:, :, 0:1].to_broadcast([P, CT, E]), ALU.is_equal)
                    step("keep1_done", dve.tensor_tensor(keep[:, :, :], io[:, :, :],
                                                         mf[:, :, 1:2].to_broadcast([P, CT, E]), ALU.is_equal))
                    step("keep_done", dve.tensor_tensor(keep[:, :, :], keep[:, :, :], keep1[:, :, :], ALU.add))
                    dve.wait_ge(S["exp_done"], c + 1)
                    step("mask_done", dve.tensor_tensor(keep1[:, :, :], ex[:, :, :], keep[:, :, :], ALU.mult))
                    step("sum_done", dve.tensor_reduce(sm[:, :], keep1[:, :, :], AX.X, ALU.add))
                    step("ri_done", dve.reciprocal(ri[:, :], sm[:, :]))
                    step("pr_done", dve.tensor_tensor(pr[:, :, :], keep1[:, :, :],
                                                      ri[:, :].rearrange("p (k o) -> p k o", o=1).to_broadcast([P, CT, E]), ALU.mult))
                    dve.wait_ge(S["prT_ps"], c + 1)
                    dve.tensor_copy(prT[:, :], pR[0:E, :]).then_inc(S["prT_sb"], 1)
                    dve.wait_ge(S["bias_ps"], c + 1)
                    step("acc0", dve.tensor_copy(acc[:, :, :], pR[:, :].rearrange("p (k d) -> p k d", k=CT)))
                    for e in range(E):
                        dve.wait_ge(down, c * E + e + 1)
                        if e:
                            dve.wait_ge(added, c * E + e)
                        for k in range(CT):
                            ins = dve.scalar_tensor_tensor(acc[:, k, :], pY[e % 2][:, k * P:(k + 1) * P], pr[:, k, e:e + 1],
                                                           acc[:, k, :], ALU.mult, ALU.add)
                        ins.then_inc(added, 1)
                    dve.wait_ge(added, c * E + E)
                    for k in range(CT):
                        ins = dve.bn_stats(st[:, k, :], acc[:, k, :])
                    step("st_done", ins)
                    for k in range(CT):
                        ins = dve.bn_aggr(mv[:, k, :], st[:, k, :])
                    step("mv_done", ins)
                    dve.wait_ge(S["sd_done"], c + 1)
                    step("rs_done", dve.reciprocal(rs[:, :], sd[:, :]))
                    for k in range(CT):
                        ins = dve.tensor_scalar(on[:, k, :], acc[:, k, :], mv[:, k, 0:1], rs[:, k:k + 1], ALU.subtract, ALU.mult)
                    step("on_done", ins)
                    wide = [P, CT, P]
                    step("aff_done", dve.tensor_tensor(acc[:, :, :], on[:, :, :],
                                                       lng[:, :].rearrange("p (o d) -> p o d", o=1).to_broadcast(wide), ALU.mult))
                    step("x_done", dve.tensor_tensor(on[:, :, :], acc[:, :, :],
                                                     lnb[:, :].rearrange("p (o d) -> p o d", o=1).to_broadcast(wide), ALU.add))
                    xv = X[:, bass.ds(c * CT, CT), :]
                    dve.tensor_tensor(xv, xv, on[:, :, :], ALU.add)
    ph.end()


def moe_capacity(nc, G, tag, rw, rb, w1, b1, w2, b2, ow1, ob1, ow2, rows, buf, ybuf):
    ph = Phase(nc, tag)
    X, XNT, XR = G["X"], G["XNT"], G["XR"]
    E, FC, CAP = 8, 4, 160
    SL = E * CAP
    ST = SL // P
    lg = ph.sb("lg", [E, 2, CH])
    lgt, mx, oh, cum, tot, run, sel = (ph.sb(n, [P, NT, E]) for n in ("lgt", "mx", "oh", "cum", "tot", "run", "sel"))
    mi = ph.sb("mi", [P, NT, E], U32)
    io = ph.sb("io", [P, NT, E])
    zero = ph.sb("zero", [P, NT])
    eid, rank, valid, inval, spare, slot, sc_f, ga_f, tmp = (
        ph.sb(n, [P, NT]) for n in ("eid", "rank", "valid", "inval", "spare", "slot", "scf", "gaf", "tmp"))
    sc_i, ga_i = ph.sb("sci", [P, NT], U32), ph.sb("gai", [P, NT], U32)
    zrow = ph.sb("zrow", [P, P])
    bt = ph.sb("bt", [P, ST, P])
    bT = ph.sb("bT", [P, SL])
    he = ph.sb("he", [P, 2, FC, CAP])
    yT = ph.sb("yT", [P, SL])
    yr = ph.sb("yr", [P, ST, P])
    ob2 = ph.sb("ob2", [1, P])
    h = ph.sb("h", [P, 2, FC, CH])
    yg = ph.sb("yg", [P, 8, P])
    pU = [ph.ps(f"U{i}") for i in range(3)]
    pY = [ph.ps(f"Y{i}") for i in range(2)]
    pR = [ph.ps(f"R{i}") for i in range(2)]
    const, zeroed, scattered, loaded, stored, ob_in = (
        ph.sem(n) for n in ("const", "zeroed", "scattered", "loaded", "stored", "obin"))
    gathered = [ph.sem(f"gathered{i}") for i in range(8)]
    lg_ps, lg_sb, lgt_ps, lgt_sb, cnt_ps, own = (ph.sem(n) for n in ("lgps", "lgsb", "lgtps", "lgtsb", "cntps", "own"))
    slots_done, bt_ps, bt_sb, up, act_up, down, act_down, yt_ps, yt_sb, valid_done = (
        ph.sem(n) for n in ("slots", "btps", "btsb", "up", "actup", "down", "actdown", "ytps", "ytsb", "valid"))
    o_up, o_relu, o_down, o_add, g_add = (ph.sem(n) for n in ("oup", "orelu", "odown", "oadd", "gadd"))
    with nc.Block() as block:
        @block.sync
        def _(sp):
            sp.dma_start(ob2[:, :], rows[2:3, :]).then_inc(ob_in, 16)
            sp.wait_ge(const, 1)
            for t in range(ST):
                sp.dma_start(buf[t * P:(t + 1) * P, :], zrow[:, :]).then_inc(zeroed, 16)
            sp.dma_start(ybuf[SL:SL + 1, :], zrow[0:1, :]).then_inc(zeroed, 16)
            sp.wait_ge(scattered, 16 * NT)
            sp.dma_start(bt[:, :, :], buf[0:SL, :].rearrange("(t p) d -> p t d", p=P)).then_inc(loaded, 16)
            sp.wait_ge(yt_sb, ST)
            sp.dma_start(ybuf[0:SL, :].rearrange("(t p) d -> p t d", p=P), yr[:, :, :]).then_inc(stored, 16)
            sp.wait_ge(ob_in, 16)

        @block.gpsimd
        def _(pool):
            pool.memset(zrow[:, :], 0.0).then_inc(const, 1)
            pool.iota(io[:, :, :], [[0, NT], [1, E]], base=0, channel_multiplier=0,
                      allow_small_or_imprecise_dtypes=True).then_inc(const, 1)
            pool.iota(spare[:, :], [[P, NT]], base=SL, channel_multiplier=1,
                      allow_small_or_imprecise_dtypes=True).then_inc(const, 1)
            pool.memset(zero[:, :], 0.0).then_inc(const, 1)
            pool.wait_ge(slots_done, 1)
            pool.wait_ge(zeroed, 16 * (ST + 1))
            for t in range(NT):
                pool.indirect_dma_start(out=buf[:, :], out_offset=bass.IndirectOffsetOnAxis(ap=sc_i[:, t:t + 1], axis=0),
                                        in_=XR[:, t, :], in_offset=None).then_inc(scattered, 16)
            pool.wait_ge(stored, 16)
            for t in range(NT):
                if t >= 8:
                    pool.wait_ge(g_add, t - 7)
                pool.indirect_dma_start(out=yg[:, t % 8, :], out_offset=None, in_=ybuf[:, :],
                                        in_offset=bass.IndirectOffsetOnAxis(ap=ga_i[:, t:t + 1], axis=0)).then_inc(gathered[t % 8], 16)

        @block.tensor
        def _(pe):
            pe.wait_ge(ob_in, 16)
            for c in range(NT // CT):
                x = XNT[:, c // 2, 1 + (c % 2) * CH:1 + (c % 2 + 1) * CH]
                if c >= 2:
                    pe.wait_ge(lgt_sb, c - 1)
                pe.matmul(pR[c % 2][0:E, :], rw, x, start=True, stop=True).then_inc(lg_ps, 1)
                pe.wait_ge(lg_sb, c + 1)
                for k in range(CT):
                    ins = pe.transpose(pR[c % 2][:, k * E:(k + 1) * E], lg[:, c % 2, k * P:(k + 1) * P], G["ident"][0:E, 0:E])
                ins.then_inc(lgt_ps, 1)
            pe.wait_ge(own, 3)
            flat = oh[:, :, :].rearrange("p n e -> p (n e)")
            pe.matmul(pR[0][:, 0:NT * E], G["tri"][:, :], flat, start=True, stop=True)
            pe.matmul(pR[1][:, 0:NT * E], G["ones"][:, :], flat, start=True, stop=True).then_inc(cnt_ps, 1)

            with pe.Fori(0, B) as b:
                with pe.Fori(0, 2) as half:
                    c = b * 2 + half
                    x = XNT[:, b, bass.ds(half * CH + 1, CH)]
                    for f in range(FC):
                        if f >= 3:
                            pe.wait_ge(o_relu, c * FC + f - 2)
                        pe.matmul(pU[f % 3][:, :], ow1[:, f * P:(f + 1) * P], x, start=True, stop=True).then_inc(o_up, 1)
                    pe.wait_ge(o_relu, c * FC + FC)
                    for k in range(CT):
                        for f in range(FC):
                            pe.matmul(pY[0][:, k * P:(k + 1) * P], h[:, 0, f, k * P:(k + 1) * P], ow2[:, f * P:(f + 1) * P],
                                      start=(f == 0), stop=False)
                        ins = pe.matmul(pY[0][:, k * P:(k + 1) * P], G["ones"][0:1, :], ob2[:, :], start=False, stop=True)
                    ins.then_inc(o_down, 1)
                    pe.wait_ge(o_add, c + 1)
            pe.wait_ge(loaded, 16)
            for t in range(ST):
                if t >= 2:
                    pe.wait_ge(bt_sb, t - 1)
                pe.transpose(pR[t % 2][:, 0:P], bt[:, t, :], G["ident"][:, :]).then_inc(bt_ps, 1)
            pe.wait_ge(bt_sb, ST)

            def ups(e):
                for f in range(FC):
                    n = e * FC + f
                    if n >= 3:
                        pe.wait_ge(act_up, n - 2)
                    pe.matmul(pU[n % 3][:, 0:CAP], w1[:, n * P:(n + 1) * P], bT[:, e * CAP:(e + 1) * CAP],
                              start=True, stop=True).then_inc(up, 1)

            def downs(e):
                pe.wait_ge(act_up, (e + 1) * FC)
                if e >= 2:
                    pe.wait_ge(act_down, e - 1)
                for f in range(FC):
                    n = e * FC + f
                    ins = pe.matmul(pY[e % 2][:, 0:CAP], w2[:, n * P:(n + 1) * P], he[:, e % 2, f, :],
                                    start=(f == 0), stop=(f == FC - 1))
                ins.then_inc(down, 1)

            ups(0)
            for e in range(E):
                if e + 1 < E:
                    ups(e + 1)
                downs(e)
            pe.wait_ge(act_down, E)
            for t in range(ST):
                if t >= 2:
                    pe.wait_ge(yt_sb, t - 1)
                pe.transpose(pR[t % 2][:, 0:P], yT[:, t * P:(t + 1) * P], G["ident"][:, :]).then_inc(yt_ps, 1)

        @block.scalar
        def _(act):
            with act.Fori(0, B) as b:
                with act.Fori(0, 2) as half:
                    c = b * 2 + half
                    for f in range(FC):
                        act.wait_ge(o_up, c * FC + f + 1)
                        act.activation(h[:, 0, f, :], pU[f % 3][:, :], ACT.Relu, bias=ob1[:, f:f + 1]).then_inc(o_relu, 1)
            def outputs(e):
                act.wait_ge(down, e + 1)
                act.activation(yT[:, e * CAP:(e + 1) * CAP], pY[e % 2][:, 0:CAP], ACT.Identity,
                               bias=b2[:, e:e + 1]).then_inc(act_down, 1)

            for e in range(E):
                for f in range(FC):
                    n = e * FC + f
                    if e >= 2:
                        act.wait_ge(down, e - 1)
                    act.wait_ge(up, n + 1)
                    act.activation(he[:, e % 2, f, :], pU[n % 3][:, 0:CAP], ACT.Relu, bias=b1[:, n:n + 1]).then_inc(act_up, 1)
                if e >= 1:
                    outputs(e - 1)
            outputs(E - 1)

        @block.vector
        def _(dve):
            done = [0]

            def chain(ins):
                done[0] += 1
                ins.then_inc(own, 1)
                dve.wait_ge(own, done[0])

            for c in range(NT // CT):
                dve.wait_ge(lg_ps, c + 1)
                dve.tensor_scalar(lg[:, c % 2, :], pR[c % 2][0:E, :], rb, None, ALU.add).then_inc(lg_sb, 1)
                dve.wait_ge(lgt_ps, c + 1)
                dve.tensor_copy(lgt[:, c * CT:(c + 1) * CT, :],
                                pR[c % 2][:, 0:CT * E].rearrange("p (k e) -> p k e", k=CT)).then_inc(lgt_sb, 1)
            dve.wait_ge(lgt_sb, NT // CT)
            dve.wait_ge(const, 4)
            for t in range(NT):
                ins = dve.max(mx[:, t, :], lgt[:, t, :])
            chain(ins)
            for t in range(NT):
                ins = dve.max_index(mi[:, t, :], mx[:, t, :], lgt[:, t, :])
            chain(ins)
            dve.tensor_copy(eid[:, :], mi[:, :, 0]).then_inc(valid_done, 1)
            dve.wait_ge(valid_done, 1)
            wide = [P, NT, E]
            chain(dve.tensor_tensor(oh[:, :, :], io[:, :, :],
                                    eid[:, :].rearrange("p (n o) -> p n o", o=1).to_broadcast(wide), ALU.is_equal))
            dve.wait_ge(cnt_ps, 1)
            dve.tensor_copy(cum[:, :, :], pR[0][:, 0:NT * E].rearrange("p (n e) -> p n e", e=E))
            chain(dve.tensor_copy(tot[:, :, :], pR[1][:, 0:NT * E].rearrange("p (n e) -> p n e", e=E)))
            for e in range(E):
                ins = dve.tensor_tensor_scan(run[:, :, e], tot[:, :, e], zero[:, :], 0.0, ALU.add, ALU.add)
            chain(ins)
            chain(dve.tensor_tensor(run[:, :, :], run[:, :, :], tot[:, :, :], ALU.subtract))
            chain(dve.tensor_tensor(cum[:, :, :], cum[:, :, :], run[:, :, :], ALU.add))
            chain(dve.tensor_tensor(sel[:, :, :], cum[:, :, :], oh[:, :, :], ALU.mult))
            chain(dve.tensor_reduce(rank[:, :], sel[:, :, :], AX.X, ALU.add))
            chain(dve.tensor_scalar(valid[:, :], rank[:, :], float(CAP), None, ALU.is_le))
            dve.tensor_scalar(inval[:, :], valid[:, :], -1.0, 1.0, ALU.mult, ALU.add)
            chain(dve.tensor_scalar(tmp[:, :], eid[:, :], float(CAP), -1.0, ALU.mult, ALU.add))
            chain(dve.tensor_tensor(slot[:, :], tmp[:, :], rank[:, :], ALU.add))
            chain(dve.tensor_tensor(slot[:, :], slot[:, :], valid[:, :], ALU.mult))
            dve.tensor_tensor(tmp[:, :], spare[:, :], inval[:, :], ALU.mult)
            chain(dve.tensor_scalar(ga_f[:, :], inval[:, :], float(SL), None, ALU.mult))
            chain(dve.tensor_tensor(sc_f[:, :], slot[:, :], tmp[:, :], ALU.add))
            chain(dve.tensor_tensor(ga_f[:, :], slot[:, :], ga_f[:, :], ALU.add))
            dve.tensor_copy(sc_i[:, :], sc_f[:, :])
            dve.tensor_copy(ga_i[:, :], ga_f[:, :]).then_inc(slots_done, 1)
            for c in range(NT // CT):
                dve.wait_ge(o_down, c + 1)
                for k in range(CT):
                    t = c * CT + k
                    ins = dve.scalar_tensor_tensor(X[:, t, :], pY[0][:, k * P:(k + 1) * P], inval[:, t:t + 1], X[:, t, :],
                                                   ALU.mult, ALU.add)
                ins.then_inc(o_add, 1)
            for t in range(ST):
                dve.wait_ge(bt_ps, t + 1)
                dve.tensor_copy(bT[:, t * P:(t + 1) * P], pR[t % 2][:, 0:P]).then_inc(bt_sb, 1)
            for t in range(ST):
                dve.wait_ge(yt_ps, t + 1)
                dve.tensor_copy(yr[:, t, :], pR[t % 2][:, 0:P]).then_inc(yt_sb, 1)
            for t in range(NT):
                dve.wait_ge(gathered[t % 8], 16 * (t // 8 + 1))
                dve.tensor_tensor(X[:, t, :], X[:, t, :], yg[:, t % 8, :], ALU.add).then_inc(g_add, 1)
    ph.end()


def wkv(nc, G, tag, w):
    ph = Phase(nc, tag)
    X, XNT = G["X"], G["XNT"]
    HK = 8
    GN_EPS = 1e-5 * 64
    dx, x5, t5a, xa, xb = (ph.sb(n, [P, T]) for n in ("dx", "x5", "t5a", "xa", "xb"))
    t5b = ph.sb("t5b", [32, T])
    td = ph.sb("td", [64, T])
    r, k, dec, g, gate = (ph.sb(n, [P, T]) for n in ("r", "k", "dec", "g", "gate"))
    kv, Sf, Ss, Sr = (ph.sb(n, [P, 2, T]) for n in ("kv", "Sf", "Ss", "Sr"))
    Sb = ph.sb("Sb", [P, 2, T + 1])
    eps = ph.sb("geps", [P, 1])
    pA, pB, pC, pD = (ph.ps(n, (P, 2 * CH)) for n in "ABCD")
    setup = ph.sem("setup")
    made = {}

    def S(name):
        if name not in made:
            made[name] = ph.sem(name)
        return made[name]

    def halves():
        return (slice(0, CH), slice(CH, T))

    mixes = ["w", "k", "v", "r", "g"]
    with nc.Block() as block:
        @block.gpsimd
        def _(pool):
            pool.memset(eps[:, :], GN_EPS)
            pool.memset(Sb[:, :, T:T + 1], 0.0).then_inc(setup, 1)
            with pool.Fori(0, B) as b:
                for v in range(HK):
                    n = b * HK + v
                    pool.wait_ge(S("bwd"), n + 1)
                    if v >= 2:
                        pool.wait_ge(S("y_mm"), n - 1)
                    pool.tensor_tensor(Ss[:, v % 2, :], Sf[:, v % 2, :], Sb[:, v % 2, 1:T + 1], ALU.add).then_inc(S("ssum"), 1)
                    pool.wait_ge(S("ssum"), n + 1)
                    pool.tensor_tensor(Sr[:, v % 2, :], Ss[:, v % 2, :], r[:, :], ALU.mult).then_inc(S("sr"), 1)

        @block.tensor
        def _(pe):
            def product(out, lhsT, rhs, name):
                for cut in halves():
                    ins = pe.matmul(out[:, cut], lhsT, rhs[:, cut], start=True, stop=True)
                ins.then_inc(S(name), 1)

            def reduce(pe, b, v):
                n = b * HK + v
                if v == 0:
                    pe.wait_ge(S("g_sb"), b + 1)
                pe.wait_ge(S("sr"), n + 1)
                for cut in halves():
                    ins = pe.matmul(pD[:, cut], w["pick"][:, v * P:(v + 1) * P], Sr[:, v % 2, cut],
                                    start=(v == 0), stop=(v == HK - 1), skip_group_check=True)
                ins.then_inc(S("y_mm"), 1)

            def projection(pe, b, product, name):
                if name == "v":
                    return
                pe.wait_ge(S("mix2_" + name), b + 1)
                src = {"w": xa, "k": xb, "r": xb, "g": xa}[name]
                if name == "w":
                    pe.wait_ge(S("gate"), b + 1)
                    product(pC[0:64, :], w["decay_w1"], src, "d1_ps")
                    pe.wait_ge(S("td"), b + 1)
                    product(pC, w["decay_w2"][0:64, :], td, "d2_ps")
                else:
                    last = {"k": "dec", "r": "k", "g": "r"}[name]
                    bank = {"k": pD, "r": pC, "g": pD}[name]
                    pe.wait_ge(S(last + "_sb"), b + 1)
                    product(bank, w["W" + name], src, name + "_ps")

            with pe.Fori(0, B) as b:
                pe.wait_ge(S("x5"), b + 1)
                product(pA, w["maa_w1"][:, 0:P], x5, "t5a_ps")
                product(pB[0:32, :], w["maa_w1"][:, P:P + 32], x5, "t5b_ps")
                pe.wait_ge(S("dx"), b + 1)
                product(pC, w["gate_w"], dx, "gate_ps")
                pe.wait_ge(S("t5"), b + 1)
                for n, name in enumerate(mixes):
                    bank = (pA, pB)[n % 2]
                    if n >= 2:
                        pe.wait_ge(S("mix_" + mixes[n - 2]), b + 1)
                    if n < 4:
                        product(bank, w["maa_w2"][:, n * P:(n + 1) * P], t5a, "m_" + name)
                    else:
                        product(bank, w["maa_w2e"], t5b, "m_" + name)
                    if n >= 1:
                        projection(pe, b, product, mixes[n - 1])
                projection(pe, b, product, "g")
                pe.wait_ge(S("mix_g"), b + 1)
                for v in range(HK):
                    n = b * HK + v
                    bank = (pA, pB)[v % 2]
                    if v >= 2:
                        pe.wait_ge(S("kv"), n - 1)
                    if v == 0:
                        pe.wait_ge(S("mix2_v"), b + 1)
                    for cut in halves():
                        ins = pe.matmul(bank[:, cut], w["Wv8"][:, v * P:(v + 1) * P], x5[:, cut], start=True, stop=True)
                    ins.then_inc(S("v_ps"), 1)
                    if v >= 2:
                        reduce(pe, b, v - 2)
                reduce(pe, b, HK - 2)
                reduce(pe, b, HK - 1)
                pe.wait_ge(S("yg"), b + 1)
                product(pA, w["mean8"], xa, "mu_ps")
                pe.wait_ge(S("sq"), b + 1)
                product(pB, w["mean8"], dx, "var_ps")
                pe.wait_ge(S("gn"), b + 1)
                product(pC, w["Wo"], xa, "o_ps")
                pe.wait_ge(S("o_sb"), b + 1)
                for t in range(TT):
                    ins = pe.transpose(pA[:, t * P:(t + 1) * P], xb[:, t * P:(t + 1) * P], G["ident"][:, :])
                ins.then_inc(S("tr"), 1)
                pe.wait_ge(S("x"), b + 1)

        @block.scalar
        def _(act):
            act.wait_ge(setup, 1)
            with act.Fori(0, B) as b:
                act.wait_ge(S("t5a_ps"), b + 1)
                act.activation(t5a[:, :], pA[:, :], ACT.Tanh)
                act.wait_ge(S("t5b_ps"), b + 1)
                act.activation(t5b[:, :], pB[0:32, :], ACT.Tanh).then_inc(S("t5"), 1)
                act.wait_ge(S("gate_ps"), b + 1)
                act.activation(gate[:, :], pC[:, :], ACT.Sigmoid, bias=w["gate_b"]).then_inc(S("gate"), 1)
                act.wait_ge(S("d1_ps"), b + 1)
                act.activation(td[:, :], pC[0:64, :], ACT.Tanh).then_inc(S("td"), 1)
                act.wait_ge(S("d2_ps"), b + 1)
                act.activation(dec[:, :], pC[:, :], ACT.Exp, bias=w["time_decay"]).then_inc(S("dec_e"), 1)
                act.wait_ge(S("dec_e"), b + 1)
                act.activation(dec[:, :], dec[:, :], ACT.Exp, scale=-1.0).then_inc(S("dec_sb"), 1)
                act.wait_ge(S("k_ps"), b + 1)
                act.copy(k[:, :], pD[:, :]).then_inc(S("k_sb"), 1)
                act.wait_ge(S("r_ps"), b + 1)
                act.copy(r[:, :], pC[:, :]).then_inc(S("r_sb"), 1)
                act.wait_ge(S("g_ps"), b + 1)
                act.activation(g[:, :], pD[:, :], ACT.Silu).then_inc(S("g_sb"), 1)
                act.wait_ge(S("yc"), b + 1)
                act.activation(dx[:, :], xb[:, :], ACT.Square).then_inc(S("sq"), 1)
                act.wait_ge(S("var_ps"), b + 1)
                act.activation(Ss[:, 0, :], pB[:, :], ACT.Sqrt, bias=eps[:, 0:1]).then_inc(S("gsd"), 1)
                act.wait_ge(S("o_ps"), b + 1)
                act.copy(xb[:, :], pC[:, :]).then_inc(S("o_sb"), 1)

        @block.vector
        def _(dve):
            with dve.Fori(0, B) as b:
                def step(name, ins):
                    ins.then_inc(S(name), 1)
                    dve.wait_ge(S(name), b + 1)

                cur, prev, nxt = (XNT[:, b, a:a + T] for a in (1, 0, 2))
                cw = w["conv_w"]
                step("c1", dve.tensor_scalar(dx[:, :], prev, cw[:, 0:1], None, ALU.mult))
                step("c2", dve.scalar_tensor_tensor(xa[:, :], cur, cw[:, 1:2], dx[:, :], ALU.mult, ALU.add))
                step("c3", dve.scalar_tensor_tensor(dx[:, :], nxt, cw[:, 2:3], xa[:, :], ALU.mult, ALU.add))
                step("dx", dve.tensor_tensor(dx[:, :], dx[:, :], cur, ALU.subtract))
                step("x5", dve.scalar_tensor_tensor(x5[:, :], dx[:, :], w["maa_x"], cur, ALU.mult, ALU.add))
                for n, name in enumerate(mixes):
                    dst = {"w": xa, "k": xb, "v": x5, "r": xb, "g": xa}[name]
                    bank = (pA, pB)[n % 2]
                    dve.wait_ge(S("m_" + name), b + 1)
                    if name == "r":
                        dve.wait_ge(S("k_ps"), b + 1)
                    if name == "g":
                        dve.wait_ge(S("d1_ps"), b + 1)
                    step("mix_" + name, dve.scalar_tensor_tensor(dst[:, :], bank[:, :], w["maa_" + name], dx[:, :],
                                                                 ALU.add, ALU.mult))
                    step("mix2_" + name, dve.tensor_tensor(dst[:, :], dst[:, :], cur, ALU.add))
                dve.wait_ge(S("k_sb"), b + 1)
                dve.wait_ge(S("r_sb"), b + 1)
                for v in range(HK):
                    n = b * HK + v
                    bank = (pA, pB)[v % 2]
                    dve.wait_ge(S("v_ps"), n + 1)
                    dve.tensor_tensor(kv[:, v % 2, :], bank[:, :], k[:, :], ALU.mult).then_inc(S("kv"), 1)
                    if v >= 2:
                        dve.wait_ge(S("ssum"), n - 1)
                    dve.wait_ge(S("kv"), n + 1)
                    dve.tensor_tensor_scan(Sf[:, v % 2, :], dec[:, :], kv[:, v % 2, :], 0.0, ALU.mult, ALU.add)
                    dve.tensor_tensor_scan(Sb[:, v % 2, T - 1::-1], kv[:, v % 2, ::-1], dec[:, ::-1], 0.0,
                                           ALU.add, ALU.mult).then_inc(S("bwd"), 1)
                dve.wait_ge(S("g_sb"), b + 1)
                dve.wait_ge(S("y_mm"), b * HK + HK)
                step("yg", dve.tensor_tensor(xa[:, :], pD[:, :], gate[:, :], ALU.mult))
                dve.wait_ge(S("mu_ps"), b + 1)
                step("yc", dve.tensor_tensor(xb[:, :], xa[:, :], pA[:, :], ALU.subtract))
                dve.wait_ge(S("gsd"), b + 1)
                step("grs", dve.reciprocal(Ss[:, 1, :], Ss[:, 0, :]))
                step("g1", dve.tensor_tensor(xa[:, :], xb[:, :], Ss[:, 1, :], ALU.mult))
                step("g2", dve.tensor_scalar(xb[:, :], xa[:, :], w["ln_w"], w["ln_b"], ALU.mult, ALU.add))
                step("gn", dve.tensor_tensor(xa[:, :], xb[:, :], g[:, :], ALU.mult))
                dve.wait_ge(S("tr"), b + 1)
                xv = X[:, bass.ds(b * TT, TT), :]
                dve.tensor_tensor(xv, xv, pA[:, :].rearrange("p (k d) -> p k d", k=TT), ALU.add).then_inc(S("x"), 1)
    ph.end()


def store_out(nc, G, out):
    ph = Phase(nc, "fin")
    stored = ph.sem("stored")
    with nc.Block() as block:
        @block.sync
        def _(sp):
            sp.dma_start(out.rearrange("(n p) d -> p n d", p=P), G["X"][:, :, :]).then_inc(stored, 16)
            sp.wait_ge(stored, 16)
    ph.end()


def pack(inputs):
    a = {k: np.asarray(v) for k, v in inputs.items()}
    cols, at = [[], [], []], {}

    def put(name, m, part=0):
        m = np.asarray(m)
        if m.shape[0] < P:
            m = np.concatenate([m, np.zeros((P - m.shape[0], m.shape[1]), m.dtype)], 0)
        at[name] = (part, sum(c.shape[1] for c in cols[part]), m.shape[1])
        cols[part].append(m)

    put("W0", a["L0_attn_W"])
    put("b0", a["L0_attn_bias"].reshape(P, 1))
    for layer in ("L0", "L3"):
        for w in ("W_r", "W_k", "W_v"):
            put(f"{layer}{w}", a[f"{layer}_ffn_{w}"].T, 2 if layer == "L3" else 0)
        for w in ("mu_r", "mu_k"):
            put(f"{layer}{w}", a[f"{layer}_ffn_{w}"].reshape(P, 1), 2 if layer == "L3" else 0)
    put("rpe", a["L1_attn_rpe_bias"][:, :256])
    put("slopes", np.asarray([[-(2.0 ** (-0.5 * (h + 1)))] for h in range(16)], np.float32))
    for m, name in enumerate("qkv"):
        put(f"L1{name}", a["L1_attn_qkv"][:, m].reshape(P, 1024))
    put("L1o", a["L1_attn_out_w"].reshape(8, P, P).transpose(1, 0, 2).reshape(P, 1024))
    for name in "qk":
        m = a[f"L2_attn_W{name}"].reshape(P, 16, 8)
        put(f"L2{name}", np.concatenate([m, np.zeros((P, 16, 24), m.dtype)], 2).reshape(P, 512), 1)
    put("L2v", a["L2_attn_Wv"], 1)
    put("L2o", a["L2_attn_Wo"].reshape(4, 32, P).transpose(1, 0, 2).reshape(32, 512), 1)
    put("gw1", a["L1_ffn_gate_w"])
    put("gb1", a["L1_ffn_gate_b"].reshape(8, 1))
    put("w1", a["L1_ffn_w1"].transpose(1, 0, 2).reshape(P, 4096))
    put("b1", a["L1_ffn_b1"].reshape(32, P).T)
    put("w2", a["L1_ffn_w2"].reshape(32, P, P).transpose(1, 0, 2).reshape(P, 4096))
    put("b2", a["L1_ffn_b2"])
    put("rw", a["L2_ffn_router_w"], 1)
    put("rb", a["L2_ffn_router_b"].reshape(8, 1), 1)
    put("x1", a["L2_ffn_w1"].transpose(1, 0, 2).reshape(P, 4096), 1)
    put("xb1", a["L2_ffn_b1"].reshape(32, P).T, 1)
    put("x2", a["L2_ffn_w2"].reshape(32, P, P).transpose(1, 0, 2).reshape(P, 4096), 1)
    put("xb2", a["L2_ffn_b2"].T, 1)
    put("ow1", a["L2_ffn_ow1"], 1)
    put("ob1", a["L2_ffn_ob1"].reshape(4, P).T, 1)
    put("ow2", a["L2_ffn_ow2"].reshape(4, P, P).transpose(1, 0, 2).reshape(P, 512), 1)
    put("Aconv_w", a["L3_attn_conv_w"].reshape(P, 3), 2)
    for name in ("maa_x", "maa_w", "maa_k", "maa_v", "maa_r", "maa_g", "time_decay", "ln_w", "ln_b", "gate_b"):
        put("A" + name, a["L3_attn_" + name].reshape(P, 1), 2)
    put("Amaa_w1", a["L3_attn_maa_w1"], 2)
    w2 = a["L3_attn_maa_w2"]
    put("Amaa_w2", np.concatenate([np.concatenate([w2[f] if g == f else np.zeros_like(w2[f]) for g in range(4)], 0)
                                   for f in range(4)], 1), 2)
    put("Amaa_w2e", w2[4], 2)
    for name in ("decay_w1", "decay_w2", "Wr", "Wk", "Wg", "Wo", "gate_w"):
        put("A" + name, a["L3_attn_" + name], 2)
    put("AWv8", np.repeat(a["L3_attn_Wv"].reshape(P, 16, 8).transpose(0, 2, 1), 8, axis=2).reshape(P, 1024), 2)
    put("Amean8", np.kron(np.eye(16), np.full((8, 8), 1 / 8)).astype(np.float32), 2)
    put("Apick", np.concatenate([np.kron(np.eye(16), np.ones((8, 1)) * (np.arange(8) == v)[None]) for v in range(8)],
                                1).astype(np.float32), 2)
    rows = np.stack([a["L1_ffn_ln_g"], a["L1_ffn_ln_b"], a["L2_ffn_ob2"]])
    return [np.ascontiguousarray(np.concatenate(c, 1)) for c in cols] + [np.ascontiguousarray(rows)], at


def build(nc, x, wts, rows, out, at, stages="0f1g23h"):
    with ExitStack() as ctx:
        def sb(name, shape, dt=F32):
            return ctx.enter_context(nc.sbuf_tensor(name, shape, dt))

        G = dict(X=sb("X", [P, NT, P]), XNT=sb("XNT", [P, B, TP]), XR=sb("XR", [P, NT, P]),
                 WA=sb("WA", [P, max(wts[0].shape[1], wts[2].shape[1])]), ident=sb("ident", [P, P]),
                 tri=sb("tri", [P, P]), ones=sb("ones", [P, P]), eps=sb("eps", [P, 1]), x_dram=x)
        G["in1"], G["in2"] = nc.alloc_semaphore("in1"), nc.alloc_semaphore("in2")
        inner = ExitStack()
        G["WB"] = inner.enter_context(nc.sbuf_tensor("WB", [P, wts[1].shape[1]], F32))

        def w(name, rows=P):
            part, lo, n = at[name]
            return (G["WA"], G["WB"], G["WA"])[part][0:rows, lo:lo + n]

        constants(nc, G, wts, at["rpe"][1])
        if "0" in stages:
            layernorm(nc, G, "n0")
            channel_mix(nc, G, "l0", w("L0W_r"), w("L0W_k"), w("L0W_v"), w("L0mu_r"), w("L0mu_k"), (w("W0"), w("b0")))

        layernorm(nc, G, "n1", lambda sp: sp.wait_ge(G["in1"], G["in1_n"]))
        tab1 = nc.dram_tensor("tab1", [16, P - 1 + T], F32).ap()
        tab2 = nc.dram_tensor("tab2", [16, P - 1 + T], F32).ap()
        tables(nc, G, w("rpe", 16), w("slopes", 16), tab1, tab2)
        if "f" in stages:
            moe_top2(nc, G, "f1", w("gw1"), w("gb1", 8), w("w1"), w("b1"), w("w2"), w("b2", 8), rows)
        if "1" in stages:
            attention(nc, G, "a1", 64, 16, w("L1q"), w("L1k"), w("L1v"), w("L1o"), tab1, 64 ** -0.5)

        layernorm(nc, G, "n2", lambda sp: sp.wait_ge(G["in2"], G["in2_n"]))
        if "g" in stages:
            buf = nc.dram_tensor("slots", [8 * 160 + N, P], F32).ap()
            ybuf = nc.dram_tensor("slot_out", [8 * 160 + 1, P], F32).ap()
            moe_capacity(nc, G, "f2", w("rw"), w("rb", 8), w("x1"), w("xb1"), w("x2"), w("xb2"), w("ow1"), w("ob1"),
                         w("ow2"), rows, buf, ybuf)
        if "2" in stages:
            attention(nc, G, "a2", 8, 16, w("L2q"), w("L2k"), w("L2v"), w("L2o", 32), tab2, 8 ** -0.5)
        inner.close()

        in3 = nc.alloc_semaphore("in3")
        layernorm(nc, G, "n3", lambda sp: sp.wait_ge(in3, load_columns(sp, in3, G["WA"], wts[2])))
        if "3" in stages:
            names = ("conv_w maa_x maa_w maa_k maa_v maa_r maa_g time_decay ln_w ln_b gate_b maa_w1 maa_w2 decay_w1 decay_w2 "
                     "Wr Wk Wg Wo gate_w Wv8 mean8 pick").split()
            aw = {n: w("A" + n) for n in names}
            aw["maa_w2e"] = w("Amaa_w2e", 32)
            wkv(nc, G, "a3", aw)
        if "h" in stages:
            channel_mix(nc, G, "l3", w("L3W_r"), w("L3W_k"), w("L3W_v"), w("L3mu_r"), w("L3mu_k"))
        store_out(nc, G, out)


def kernel(**inputs):
    import concourse.bacc as bacc
    from concourse.bass_utils import run_bass_kernel_spmd as run

    nc = bacc.Bacc("TRN2", target_bir_lowering=False, num_devices=1)
    packed, at = pack(inputs)
    x = np.ascontiguousarray(np.asarray(inputs["L0_attn_x"]).reshape(N, P))
    arrays = {"in_x": x} | {f"in_w{i}": m for i, m in enumerate(packed)}
    args = {k: nc.dram_tensor(k, list(v.shape), F32, kind="ExternalInput").ap() for k, v in arrays.items()}
    out = nc.dram_tensor("out_x", [N, P], F32, kind="ExternalOutput").ap()
    build(nc, args["in_x"], [args["in_w0"], args["in_w1"], args["in_w2"]], args["in_w3"], out, at)
    result = run(nc, [arrays], core_ids=[0]).results[0]["out_x"]
    return result.reshape(B, T, P)
```

```python
import concourse.bass as bass
from concourse import mybir
from contextlib import ExitStack
import numpy as np

F32 = mybir.dt.float32
BF16 = mybir.dt.bfloat16
U32 = mybir.dt.uint32
I32 = mybir.dt.int32
ALU = mybir.AluOpType
ACT = mybir.ActivationFunctionType
AX = mybir.AxisListType

P = 128
B, T = 4, 1024
N = B * T
NT = N // P
TT = T // P
CH = 512
CT = CH // P
TP = T + 2
LN_EPS = 1e-5


class Phase:

    def __init__(self, nc, tag):
        self.nc, self.tag, self.ctx, self.sems = nc, tag, ExitStack(), []

    def sb(self, name, shape, dt=F32):
        return self.ctx.enter_context(self.nc.sbuf_tensor(f"{self.tag}_{name}", shape, dt))

    def ps(self, name, shape=(P, CH), dt=F32):
        return self.ctx.enter_context(self.nc.psum_tensor(f"{self.tag}_{name}", list(shape), dt))

    def sem(self, name):
        s = self.nc.alloc_semaphore(f"{self.tag}_{name}")
        self.sems.append(s)
        return s

    def end(self):
        self.nc.clear_and_free_semaphores(self.sems)
        self.nc.all_engine_barrier()
        self.ctx.close()


def load_columns(sp, sem, dst, src, lo=0, hi=None):
    hi = hi or src.shape[1]
    cuts = list(range(lo, hi, 2048)) + [hi]
    for a, z in zip(cuts, cuts[1:]):
        sp.dma_start(dst[:, a:z], src[:, a:z]).then_inc(sem, 16)
    return 16 * (len(cuts) - 1)


def constants(nc, G, wts, first):
    ph = Phase(nc, "init")
    loaded, made = ph.sem("loaded"), ph.sem("made")
    with nc.Block() as block:
        @block.sync
        def _(sp):
            sp.dma_start(G["X"][:, :, :], G["x_dram"].rearrange("(n p) d -> p n d", p=P)).then_inc(loaded, 16)
            n = 16 + load_columns(sp, loaded, G["WA"], wts[0], 0, first)
            G["in1_n"] = load_columns(sp, G["in1"], G["WA"], wts[0], first)
            G["in2_n"] = load_columns(sp, G["in2"], G["WB"], wts[1])
            sp.wait_ge(loaded, n)

        @block.gpsimd
        def _(pool):
            pool.memset(G["ident"][:, :], 0.0).then_inc(made, 1)
            pool.memset(G["tri"][:, :], 1.0).then_inc(made, 1)
            pool.memset(G["ones"][:, :], 1.0).then_inc(made, 1)
            pool.memset(G["XNT"][:, :, 0:1], 0.0)
            pool.memset(G["XNT"][:, :, TP - 1:TP], 0.0)
            pool.memset(G["eps"][:, :], LN_EPS)
            pool.wait_ge(made, 3)
            pool.affine_select(out=G["ident"][:, :], in_=G["ident"][:, :], compare_op=ALU.not_equal, fill=1.0,
                               base=0, pattern=[[-1, P]], channel_multiplier=1).then_inc(made, 1)
            pool.affine_select(out=G["tri"][:, :], in_=G["tri"][:, :], compare_op=ALU.is_ge, fill=0.0,
                               base=0, pattern=[[1, P]], channel_multiplier=-1).then_inc(made, 1)
    ph.end()


def layernorm(nc, G, tag, loads=None):
    ph = Phase(nc, tag)
    X, XNT = G["X"], G["XNT"]
    stats = ph.sb("stats", [P, NT, 6])
    mean = ph.sb("mean", [P, NT])
    half = ph.sb("half", [P, NT])
    sq = ph.sb("sq", [P, NT])
    m2 = ph.sb("m2", [P, NT])
    var = ph.sb("var", [P, NT])
    sd = ph.sb("sd", [P, NT])
    rstd = ph.sb("rstd", [P, NT])
    XR = G["XR"]
    pst = [ph.ps(f"t{i}") for i in range(2)]
    stats_done, mv_done, sd_done, rstd_done = (ph.sem(n) for n in ("stats", "mv", "sd", "rstd"))
    xn_done, tr_done, out_done = (ph.sem(n) for n in ("xn", "tr", "out"))
    with nc.Block() as block:
        if loads:
            @block.sync
            def _(sp):
                loads(sp)

        @block.vector
        def _(dve):
            with dve.Fori(0, NT // CT) as c:
                for k in range(CT):
                    ins = dve.bn_stats(stats[:, c * CT + k, :], X[:, c * CT + k, :])
                ins.then_inc(stats_done, 1)
            dve.wait_ge(stats_done, NT // CT)
            dve.tensor_tensor(mean[:, :], stats[:, :, 1], stats[:, :, 4], ALU.add)
            dve.tensor_tensor(half[:, :], stats[:, :, 1], stats[:, :, 4], ALU.subtract)
            dve.tensor_tensor(m2[:, :], stats[:, :, 2], stats[:, :, 5], ALU.add).then_inc(stats_done, 1)
            dve.wait_ge(stats_done, NT // CT + 1)
            dve.tensor_scalar(mean[:, :], mean[:, :], 0.5, None, ALU.mult)
            dve.tensor_tensor(sq[:, :], half[:, :], half[:, :], ALU.mult)
            dve.tensor_scalar(m2[:, :], m2[:, :], 4.0 / P, None, ALU.mult).then_inc(stats_done, 1)
            dve.wait_ge(stats_done, NT // CT + 2)
            dve.tensor_tensor(var[:, :], sq[:, :], m2[:, :], ALU.add).then_inc(mv_done, 1)
            dve.wait_ge(sd_done, 1)
            dve.reciprocal(rstd[:, :], sd[:, :]).then_inc(rstd_done, 1)
            dve.wait_ge(rstd_done, 1)
            with dve.Fori(0, B) as b:
                for h in range(2):
                    for k in range(CT):
                        n = b * TT + (h * CT + k)
                        ins = dve.tensor_scalar(XR[:, n, :], X[:, n, :], mean[:, bass.ds(n, 1)], rstd[:, bass.ds(n, 1)],
                                                ALU.subtract, ALU.mult)
                    ins.then_inc(xn_done, 1)

        @block.scalar
        def _(act):
            act.wait_ge(mv_done, 1)
            act.activation(sd[:, :], var[:, :], ACT.Sqrt, bias=G["eps"][:, 0:1], scale=0.25).then_inc(sd_done, 1)
            with act.Fori(0, B) as b:
                for h in range(2):
                    act.wait_ge(tr_done, b * 2 + h + 1)
                    act.copy(XNT[:, b, 1 + h * CH:1 + (h + 1) * CH], pst[h][:, :]).then_inc(out_done, 1)

        @block.tensor
        def _(pe):
            for c in range(NT // CT):
                pe.wait_ge(xn_done, c + 1)
                if c >= 2:
                    pe.wait_ge(out_done, c - 1)
                for k in range(CT):
                    ins = pe.transpose(pst[c % 2][:, k * P:(k + 1) * P], XR[:, c * CT + k, :], G["ident"][:, :])
                ins.then_inc(tr_done, 1)
    ph.end()


def channel_mix(nc, G, tag, wr, wk, wv, mu_r, mu_k, attn=None):
    ph = Phase(nc, tag)
    X, XNT = G["X"], G["XNT"]
    dx = ph.sb("dx", [P, 2, CH])
    xr = ph.sb("xr", [P, 2, CH])
    xk = ph.sb("xk", [P, 2, CH])
    sig = ph.sb("sig", [P, 2, CH])
    kr = ph.sb("kr", [P, 2, CH])
    k2 = ph.sb("k2", [P, 2, CH])
    prod = ph.sb("prod", [P, 2, CH])
    delta = ph.sb("delta", [P, 2, CH])
    wc = ph.sb("wc", [P, P])
    bc = ph.sb("bc", [P, 1])
    psr = [ph.ps(f"r{i}") for i in range(2)]
    psk = [ph.ps(f"k{i}") for i in range(2)]
    psa = [ph.ps(f"a{i}") for i in range(2)]
    names = ("dx", "mixed", "rk", "relu", "k2", "v", "prod", "delta", "tr", "x", "wcp", "wc")
    dx_done, mixed, rk_done, relu_done, k2_done, v_done, prod_done, delta_done, tr_done, x_done, wc_psum, wc_done = (
        ph.sem(n) for n in names)
    with nc.Block() as block:
        @block.vector
        def _(dve):
            if attn:
                dve.wait_ge(wc_psum, 1)
                dve.tensor_copy(wc[:, :], psa[0][:, 0:P]).then_inc(wc_done, 1)
                dve.tensor_copy(bc[:, :], psa[0][:, P:P + 1]).then_inc(wc_done, 1)
                dve.wait_ge(wc_done, 2)
            with dve.Fori(0, B) as b:
                for h in range(2):
                    c = b * 2 + h
                    cur = XNT[:, b, 1 + h * CH:1 + (h + 1) * CH]
                    prev = XNT[:, b, h * CH:(h + 1) * CH]
                    dve.tensor_tensor(dx[:, h, :], cur, prev, ALU.subtract).then_inc(dx_done, 1)
                    dve.wait_ge(dx_done, c + 1)
                    dve.scalar_tensor_tensor(xr[:, h, :], dx[:, h, :], mu_r, prev, ALU.mult, ALU.add)
                    dve.scalar_tensor_tensor(xk[:, h, :], dx[:, h, :], mu_k, prev, ALU.mult,
                                             ALU.add).then_inc(mixed, 1)
                for h in range(2):
                    c = b * 2 + h
                    dve.wait_ge(v_done, c + 1)
                    if attn:
                        dve.tensor_tensor(prod[:, h, :], sig[:, h, :], psr[h][:, :], ALU.mult).then_inc(prod_done, 1)
                        dve.wait_ge(prod_done, c + 1)
                        dve.scalar_tensor_tensor(delta[:, h, :], psa[h][:, :], bc[:, 0:1], prod[:, h, :], ALU.add,
                                                 ALU.add).then_inc(delta_done, 1)
                    else:
                        dve.tensor_tensor(delta[:, h, :], sig[:, h, :], psr[h][:, :], ALU.mult).then_inc(delta_done, 1)
                for h in range(2):
                    c = b * 2 + h
                    dve.wait_ge(tr_done, c + 1)
                    xv = X[:, bass.ds(b * TT + h * CT, CT), :]
                    dve.tensor_tensor(xv, xv, psk[h][:, :].rearrange("p (k d) -> p k d", k=CT),
                                      ALU.add).then_inc(x_done, 1)

        @block.scalar
        def _(act):
            with act.Fori(0, B) as b:
                for h in range(2):
                    c = b * 2 + h
                    act.wait_ge(rk_done, c + 1)
                    act.activation(sig[:, h, :], psr[h][:, :], ACT.Sigmoid)
                    act.activation(kr[:, h, :], psk[h][:, :], ACT.Relu).then_inc(relu_done, 1)
                    act.wait_ge(relu_done, c + 1)
                    act.activation(k2[:, h, :], kr[:, h, :], ACT.Square).then_inc(k2_done, 1)

        @block.tensor
        def _(pe):
            if attn:
                pe.matmul(psa[0][:, 0:P], attn[0], G["tri"][:, :], start=True, stop=True)
                pe.matmul(psa[0][:, P:P + 1], G["tri"][:, :], attn[1], start=True, stop=True).then_inc(wc_psum, 1)
                pe.wait_ge(wc_done, 2)
            pe.sem_inc(x_done, 2)
            with pe.Fori(0, B) as b:
                for h in range(2):
                    c = b * 2 + h
                    pe.wait_ge(mixed, c + 1)
                    pe.wait_ge(x_done, c + 1)
                    pe.matmul(psr[h][:, :], wr, xr[:, h, :], start=True, stop=True)
                    ins = pe.matmul(psk[h][:, :], wk, xk[:, h, :], start=True, stop=True)
                    ins.then_inc(rk_done, 1)
                    if attn:
                        pe.matmul(psa[h][:, :], wc[:, :], XNT[:, b, 1 + h * CH:1 + (h + 1) * CH], start=True, stop=True)
                for h in range(2):
                    c = b * 2 + h
                    pe.wait_ge(k2_done, c + 1)
                    pe.matmul(psr[h][:, :], wv, k2[:, h, :], start=True, stop=True).then_inc(v_done, 1)
                for h in range(2):
                    c = b * 2 + h
                    pe.wait_ge(delta_done, c + 1)
                    for k in range(CT):
                        ins = pe.transpose(psk[h][:, k * P:(k + 1) * P], delta[:, h, k * P:(k + 1) * P], G["ident"][:, :])
                    ins.then_inc(tr_done, 1)
    ph.end()


def tables(nc, G, rpe, slopes, tab1, qtail, ktail):
    ph = Phase(nc, "tab")
    K = P - 1
    H = 16
    S = 256
    t1 = ph.sb("t1", [H, K + T])
    t2, rest = ph.sb("t2", [H, T]), ph.sb("rest", [H, T])
    tail = ph.sb("tail", [H, 6, T], BF16)
    dist = ph.sb("dist", [H, T])
    zero = ph.sb("zero", [H, T])
    zeros = ph.sb("zeros", [H, T], BF16)
    made, scanned, filled, cut, stored = (ph.sem(n) for n in ("made", "scanned", "filled", "cut", "stored"))
    with nc.Block() as block:
        @block.gpsimd
        def _(pool):
            pool.iota(dist[:, :], [[-1, T]], base=T // 2, channel_multiplier=0, allow_small_or_imprecise_dtypes=True)
            pool.memset(zero[:, :], 0.0)
            pool.memset(zeros[:, :], 0.0)
            pool.memset(tail[:, 0:3, :], 1.0)
            pool.memset(t1[:, 0:K], -30000.0).then_inc(made, 1)

        @block.vector
        def _(dve):
            dve.wait_ge(made, 1)
            dve.tensor_tensor_scan(t1[:, K:K + S], rpe, zero[:, 0:S], 0.0, ALU.add, ALU.add).then_inc(scanned, 1)
            dve.tensor_scalar(t2[:, :], dist[:, :], slopes, None, ALU.mult).then_inc(cut, 1)
            dve.wait_ge(scanned, 1)
            dve.tensor_scalar(t1[:, K + S:K + T], zero[:, S:T], t1[:, K + S - 1:K + S], None,
                              ALU.add).then_inc(filled, 1)
            dve.wait_ge(cut, 1)
            dve.tensor_copy(tail[:, 3, :], t2[:, :]).then_inc(cut, 1)
            dve.wait_ge(cut, 2)
            dve.tensor_tensor(rest[:, :], t2[:, :], tail[:, 3, :], ALU.subtract).then_inc(cut, 1)
            dve.wait_ge(cut, 3)
            dve.tensor_copy(tail[:, 4, :], rest[:, :]).then_inc(cut, 1)
            dve.wait_ge(cut, 4)
            dve.tensor_tensor(tail[:, 5, :], rest[:, :], tail[:, 4, :], ALU.subtract).then_inc(filled, 1)

        @block.sync
        def _(sp):
            sp.wait_ge(filled, 2)
            sp.dma_start(tab1, t1[:, :]).then_inc(stored, 16)
            sp.dma_start(qtail[0:3, :], zeros[0:3, :]).then_inc(stored, 16)
            sp.dma_start(qtail[3:6, :], tail[0:3, 0, :]).then_inc(stored, 16)
            for b in range(B):
                sp.dma_start(ktail[b * H:(b + 1) * H, :, :], tail[:, :, :]).then_inc(stored, 16)
            sp.wait_ge(stored, 16 * (3 + B))
    ph.end()


def attention(nc, G, tag, hd, heads, wq_all, wk_all, wv_all, wo_all, tab, scale):
    ph = Phase(nc, tag)
    X, XNT = G["X"], G["XNT"]
    HG = 2 if hd == 64 else 4
    RS = P // HG
    NG = heads // HG
    MV = HG * hd
    U = HG * TT
    units = [(u, i) for i in range(TT) for u in range(HG)]
    K = P - 1
    wq, wk = ph.sb("wq", [P, P]), ph.sb("wk", [P, P])
    wv, wo = ph.sb("wv", [P, MV]), ph.sb("wo", [MV, P])
    tb = ph.sb("tb", [P, HG, T])
    QT, KT, vT = ph.sb("QT", [P, T]), ph.sb("KT", [P, T]), ph.sb("vT", [MV, T])
    V = ph.sb("V", [P, TT, MV])
    NS = 2
    Sb = ph.sb("S", [P, NS, T])
    Pb = ph.sb("P", [P, NS, T])
    PT = ph.sb("PT", [P, NS, T])
    mix = ph.sb("mix", [P, TT, MV])
    mT = ph.sb("mT", [MV, T])
    nmax, rsum, rinv = (ph.sb(n, [P, U]) for n in ("nmax", "rsum", "rinv"))
    DT = G["XR"][:, :, :].rearrange("p (b k) d -> p b (k d)", b=B)
    pS = [ph.ps(f"S{i}", (P, 2 * CH)) for i in range(2)]
    pT = [ph.ps(f"T{i}") for i in range(2)]
    pO = [ph.ps(f"O{i}") for i in range(2)]
    runs = [(n, r) for n, (u, i) in enumerate(units) for r in range(i // CT + 1)]
    last_run = {n: k for k, (n, r) in enumerate(runs)}
    R = len(runs)
    w_in, w_copied, group_done, dt_zero = (ph.sem(n) for n in ("win", "wcopied", "groupdone", "dtzero"))
    q_ps, k_ps, v_ps, q_sb, k_sb, v_sb = (ph.sem(n) for n in ("qps", "kps", "vps", "qsb", "ksb", "vsb"))
    vt_ps, vt_sb = ph.sem("vtps"), ph.sem("vtsb")
    s_ps, s_sb, p_sb, t_ps, t_sb_a, t_sb_d, o_ps, o_sb, r_inv = (
        ph.sem(n) for n in ("sps", "ssb", "psb", "tps", "tsba", "tsbd", "ops", "osb", "rinv"))
    passed, passed_pe = ph.sem("passed"), ph.sem("passedpe")
    m_ps, m_sb, y_ps, y_sb, f_ps, f_sb = (ph.sem(n) for n in ("mps", "msb", "yps", "ysb", "fps", "fsb"))
    on_act = [n % 3 != 2 for n, r in runs]
    acts = [k for k in range(R) if on_act[k]]
    dves = [k for k in range(R) if not on_act[k]]

    def nth(k):
        return (t_sb_a, len(acts), acts.index(k) + 1) if on_act[k] else (t_sb_d, len(dves), dves.index(k) + 1)

    def length(i):
        return (i + 1) * P

    with nc.Block() as block:
        @block.sync
        def _(sp):
            with sp.Fori(0, NG) as g:
                sp.wait_ge(group_done, g + 1)
                for u in range(HG):
                    src = bass.AP(tab.tensor, (g * HG + u) * (K + T), [[1, P], [1, T]])
                    sp.dma_start(tb[:, u, :], src).then_inc(w_in, 16)

        @block.gpsimd
        def _(pool):
            pool.memset(DT[:, :, :], 0.0).then_inc(dt_zero, 1)
            pool.sem_inc(group_done, 1)
            with pool.Fori(0, NG) as g:
                pool.wait_ge(group_done, g + 1)
                pool.tensor_copy(wq[:, :], wq_all[:, bass.ds(g * P, P)])
                pool.tensor_copy(wk[:, :], wk_all[:, bass.ds(g * P, P)])
                pool.tensor_copy(wv[:, :], wv_all[:, bass.ds(g * MV, MV)])
                pool.tensor_copy(wo[:, :], wo_all[:, bass.ds(g * P, P)]).then_inc(w_copied, 1)

        @block.tensor
        def _(pe):
            def scores(n, it):
                u, i = units[n]
                if n >= 2:
                    pe.wait_ge(s_sb, it * U + n - 1)
                rows = slice(u * RS, u * RS + hd)
                for lo in range(0, length(i), CH):
                    hi = min(lo + CH, length(i))
                    ins = pe.matmul(pS[n % 2][:, lo:hi], QT[rows, i * P:(i + 1) * P], KT[rows, lo:hi],
                                    start=True, stop=True)
                ins.then_inc(s_ps, 1)

            def transposes(n, it):
                u, i = units[n]
                pe.wait_ge(p_sb, it * U + n + 1)
                for k, (m, r) in enumerate(runs):
                    if m != n:
                        continue
                    if k >= 2:
                        s, per, place = nth(k - 2)
                        pe.wait_ge(s, it * per + place)
                    for j in range(r * CT, min(r * CT + CT, i + 1)):
                        ins = pe.transpose(pT[k % 2][:, (j % CT) * P:(j % CT + 1) * P], Pb[:, n % NS, j * P:(j + 1) * P],
                                           G["ident"][:, :])
                    ins.then_inc(t_ps, 1)

            def values(n, it):
                u, i = units[n]
                s, per, place = nth(last_run[n])
                pe.wait_ge(s, it * per + place)
                if n >= 2:
                    pe.wait_ge(o_sb, it * U + n - 1)
                for j in range(i + 1):
                    ins = pe.matmul(pO[n % 2][:, 0:hd], PT[:, n % NS, j * P:(j + 1) * P], V[:, j, u * hd:(u + 1) * hd],
                                    start=(j == 0), stop=(j == i))
                ins.then_inc(o_ps, 1)

            pe.wait_ge(dt_zero, 1)
            with pe.Fori(0, NG) as g:
                with pe.Fori(0, B) as b:
                    it = g * B + b
                    pe.wait_ge(w_copied, g + 1)
                    for half in range(2):
                        x = XNT[:, b, 1 + half * CH:1 + (half + 1) * CH]
                        cut = slice(half * CH, (half + 1) * CH)
                        pe.matmul(pS[0][:, cut], wq[:, :], x, start=True, stop=True)
                        ins = pe.matmul(pS[1][:, cut], wk[:, :], x, start=True, stop=True)
                        ins.then_inc(q_ps, 1)
                    for half in range(2):
                        x = XNT[:, b, 1 + half * CH:1 + (half + 1) * CH]
                        pe.matmul(pT[half][0:MV, :], wv[:, :], x, start=True, stop=True).then_inc(v_ps, 1)
                    pe.wait_ge(v_sb, it + 1)
                    pe.sem_inc(passed_pe, 1)
                    for j in range(TT):
                        ins = pe.transpose(pT[j // CT][:, (j % CT) * MV:(j % CT + 1) * MV], vT[:, j * P:(j + 1) * P],
                                           G["ident"][0:MV, 0:MV])
                    ins.then_inc(vt_ps, 1)
                    pe.wait_ge(q_sb, it + 1)
                    pe.wait_ge(k_sb, it + 1)
                    scores(0, it)
                    pe.wait_ge(vt_sb, it + 1)
                    for n in range(U):
                        if n + 1 < U:
                            scores(n + 1, it)
                        transposes(n, it)
                        if n >= 1:
                            values(n - 1, it)
                    values(U - 1, it)
                    pe.wait_ge(o_sb, it * U + U)
                    for j in range(TT):
                        ins = pe.transpose(pS[0][0:MV, j * P:(j + 1) * P], mix[:, j, :], G["ident"][:, :])
                    ins.then_inc(m_ps, 1)
                    pe.wait_ge(m_sb, it + 1)
                    for half in range(2):
                        cut = slice(half * CH, (half + 1) * CH)
                        ins = pe.matmul(pS[1][:, cut], wo[:, :], mT[:, cut], start=True, stop=True)
                    ins.then_inc(y_ps, 1)
                    pe.wait_ge(y_sb, it + 1)
                pe.sem_inc(group_done, 1)
            for c in range(NT // CT):
                if c >= 2:
                    pe.wait_ge(f_sb, c - 1)
                for j in range(CT):
                    t = c * CT + j
                    ins = pe.transpose(pT[c % 2][:, j * P:(j + 1) * P], DT[:, t // TT, (t % TT) * P:(t % TT + 1) * P],
                                       G["ident"][:, :])
                ins.then_inc(f_ps, 1)

        @block.scalar
        def _(act):
            with act.Fori(0, NG) as g:
                with act.Fori(0, B) as b:
                    it = g * B + b
                    act.wait_ge(q_ps, it * 2 + 2)
                    act.activation(QT[:, :], pS[0][:, :], ACT.Copy, scale=scale).then_inc(q_sb, 1)
                    act.wait_ge(v_ps, it * 2 + 2)
                    act.copy(vT[:, 0:CH], pT[0][0:MV, :])
                    act.copy(vT[:, CH:T], pT[1][0:MV, :]).then_inc(v_sb, 1)
                    act.wait_ge(vt_ps, it + 1)
                    for h in range(2):
                        ins = act.copy(V[:, h * CT:(h + 1) * CT, :],
                                       pT[h][:, 0:CT * MV].rearrange("p (k m) -> p k m", k=CT))
                    ins.then_inc(vt_sb, 1)

                    def copies(n):
                        u, i = units[n]
                        for k, (m, r) in enumerate(runs):
                            if m == n and on_act[k]:
                                act.wait_ge(t_ps, it * R + k + 1)
                                cut = slice(r * CH, min(r * CH + CH, length(i)))
                                act.copy(PT[:, n % NS, cut], pT[k % 2][:, 0:cut.stop - cut.start]).then_inc(t_sb_a, 1)

                    for n in range(U):
                        u, i = units[n]
                        act.wait_ge(s_sb, it * U + n + 1)
                        if n >= NS:
                            act.wait_ge(t_ps, it * R + last_run[n - NS] + 1)
                        act.activation(Pb[:, n % NS, 0:length(i)], Sb[:, n % NS, 0:length(i)], ACT.Exp,
                                       bias=nmax[:, n:n + 1], scale=-1.0, accum_out=rsum[:, n:n + 1]).then_inc(p_sb, 1)
                        if n >= 1:
                            copies(n - 1)
                    copies(U - 1)
                    act.wait_ge(m_ps, it + 1)
                    act.copy(mT[:, :], pS[0][0:MV, :]).then_inc(m_sb, 1)

        @block.vector
        def _(dve):
            with dve.Fori(0, NG) as g:
                with dve.Fori(0, B) as b:
                    it = g * B + b
                    dve.wait_ge(w_in, g * 16 * HG + 16 * HG)
                    dve.wait_ge(q_ps, it * 2 + 2)
                    dve.tensor_copy(KT[:, :], pS[1][:, :]).then_inc(k_sb, 1)

                    def copies(n):
                        u, i = units[n]
                        for k, (m, r) in enumerate(runs):
                            if m == n and not on_act[k]:
                                dve.wait_ge(t_ps, it * R + k + 1)
                                cut = slice(r * CH, min(r * CH + CH, length(i)))
                                dve.tensor_copy(PT[:, n % NS, cut], pT[k % 2][:, 0:cut.stop - cut.start])\
                                   .then_inc(t_sb_d, 1)

                    def normalise(n):
                        u, i = units[n]
                        dve.wait_ge(p_sb, it * U + n + 1)
                        dve.reciprocal(rinv[:, n:n + 1], rsum[:, n:n + 1]).then_inc(r_inv, 1)
                        dve.wait_ge(o_ps, it * U + n + 1)
                        dve.wait_ge(r_inv, it * U + n + 1)
                        dve.tensor_scalar(mix[:, i, u * hd:(u + 1) * hd], pO[n % 2][:, 0:hd], rinv[:, n:n + 1], None,
                                          ALU.mult).then_inc(o_sb, 1)

                    for n in range(U):
                        u, i = units[n]
                        L = length(i)
                        dve.wait_ge(s_ps, it * U + n + 1)
                        if n >= NS:
                            dve.wait_ge(p_sb, it * U + n - NS + 1)
                        dve.sem_inc(passed, 1)
                        dve.tensor_tensor_reduce(out=Sb[:, n % NS, 0:L], in0=pS[n % 2][:, 0:L],
                                                 in1=tb[:, u, L - 1::-1], scale=-1.0, scalar=3.0e38,
                                                 op0=ALU.add, op1=ALU.min, accum_out=nmax[:, n:n + 1]).then_inc(s_sb, 1)
                        if n >= 1:
                            copies(n - 1)
                        if n >= 2:
                            normalise(n - 2)
                    copies(U - 1)
                    normalise(U - 2)
                    normalise(U - 1)
                    dve.wait_ge(y_ps, it + 1)
                    dve.tensor_tensor(DT[:, b, :], DT[:, b, :], pS[1][:, :], ALU.add).then_inc(y_sb, 1)
            for c in range(NT // CT):
                dve.wait_ge(f_ps, c + 1)
                xv = X[:, c * CT:(c + 1) * CT, :]
                dve.tensor_tensor(xv, xv, pT[c % 2][:, :].rearrange("p (k d) -> p k d", k=CT), ALU.add).then_inc(f_sb, 1)
    ph.end()


def alibi_split(nc, G, wq, wk, wv, V9, scr, scale):
    ph = Phase(nc, "a2s")
    XNT = G["XNT"]
    QF, KF, RQ, RK, vT = (ph.sb(n, [P, T]) for n in ("QF", "KF", "RQ", "RK", "vT"))
    parts = ph.sb("parts", [P, 2, 3, T], BF16)
    pQ, pK, pV, pW = (ph.ps(n, (P, T)) for n in ("Q", "K", "V", "W"))
    q_ps, k_ps, v_ps, f_sb, k_sb, v_sb, w_ps, w_sb = (
        ph.sem(n) for n in ("qps", "kps", "vps", "fsb", "ksb", "vsb", "wps", "wsb"))
    high, rest, stored, ones_set, passed = (ph.sem(n) for n in ("high", "rest", "stored", "onesset", "passed"))
    HU = V9.shape[2]

    with nc.Block() as block:
        @block.tensor
        def _(pe):
            with pe.Fori(0, B) as b:
                for ps, w, done in ((pQ, wq, q_ps), (pK, wk, k_ps), (pV, wv, v_ps)):
                    if ps is pQ:
                        pe.wait_ge(rest, b * 6)
                    for half in range(2):
                        ins = pe.matmul(ps[:, half * CH:(half + 1) * CH], w,
                                        XNT[:, b, 1 + half * CH:1 + (half + 1) * CH], start=True, stop=True)
                    ins.then_inc(done, 1)
                pe.wait_ge(v_sb, b + 1)
                pe.wait_ge(w_sb, b)
                for j in range(TT):
                    ins = pe.transpose(pW[:, j * P:(j + 1) * P], vT[:, j * P:(j + 1) * P], G["ident"][:, :])
                ins.then_inc(w_ps, 1)

        @block.scalar
        def _(act):
            with act.Fori(0, B) as b:
                act.wait_ge(q_ps, b + 1)
                act.activation(QF[:, :], pQ[:, :], ACT.Copy, scale=scale).then_inc(f_sb, 1)
                act.wait_ge(k_ps, b + 1)
                act.copy(KF[:, :], pK[:, :]).then_inc(f_sb, 1)
                act.wait_ge(stored, b * 16)
                act.wait_ge(f_sb, b * 2 + 1)
                act.copy(parts[:, 0, 0, :], QF[:, :]).then_inc(high, 1)
                act.wait_ge(f_sb, b * 2 + 2)
                act.copy(parts[:, 1, 0, :], KF[:, :]).then_inc(high, 1)
                act.wait_ge(v_ps, b + 1)
                act.copy(vT[:, :], pV[:, :]).then_inc(v_sb, 1)

        @block.vector
        def _(dve):
            with dve.Fori(0, B) as b:
                for s, F, R in ((0, QF, RQ), (1, KF, RK)):
                    dve.wait_ge(high, b * 2 + s + 1)
                    dve.tensor_tensor(R[:, :], F[:, :], parts[:, s, 0, :], ALU.subtract).then_inc(rest, 1)
                    dve.wait_ge(rest, b * 6 + s * 3 + 1)
                    dve.tensor_copy(parts[:, s, 1, :], R[:, :]).then_inc(rest, 1)
                    dve.wait_ge(rest, b * 6 + s * 3 + 2)
                    dve.tensor_tensor(parts[:, s, 2, :], R[:, :], parts[:, s, 1, :], ALU.subtract).then_inc(rest, 1)
                dve.wait_ge(w_ps, b + 1)
                for h in range(2):
                    for g in range(4):
                        src = pW[:, h * CH:(h + 1) * CH].rearrange("p (t g u d) -> p g u t d", t=CT, g=4, u=HU)
                        ins = dve.tensor_copy(V9[:, bass.ds(b * 4 + g, 1), :, h * CT:(h + 1) * CT, 0:8]
                                              .rearrange("p o u t d -> p (o u) t d"), src[:, g])
                ins.then_inc(w_sb, 1)

        @block.gpsimd
        def _(pool):
            pool.memset(V9[:, :, :, :, 8:9].rearrange("p i u t d -> p (i u t) d"), 1.0).then_inc(ones_set, 1)
            pool.wait_ge(ones_set, 1)

        @block.sync
        def _(sp):
            with sp.Fori(0, B) as b:
                sp.wait_ge(rest, b * 6 + 6)
                dst = bass.AP(scr.tensor, b * P * T, [[T, P], [N * P, 6], [1, T]])
                sp.dma_start(dst, parts[:, :, :, :].rearrange("p s c t -> p (s c) t")).then_inc(stored, 16)
            sp.wait_ge(stored, B * 16)
    ph.end()


def alibi_attention(nc, G, V9, scr, qtail, ktail):
    ph = Phase(nc, "a2")
    HU = V9.shape[2]
    IT = V9.shape[1]
    MR = 72
    mix = G["XR"][:, :, :].rearrange("p a b -> p (a b)").rearrange("p (i t c) -> p i t c", i=IT, t=TT)
    QS = [ph.sb(f"QS{u}", [P, T], BF16) for u in range(HU)]
    KS = [ph.sb(f"KS{u}", [P, T], BF16) for u in range(HU)]
    identb, maskq, maskk = (ph.sb(n, [P, P], BF16) for n in ("identb", "maskq", "maskk"))
    Vg = ph.sb("Vg", [P, HU, TT, 32])
    NP = 4
    PT = ph.sb("PT", [P, NP, CH])
    mx = ph.sb("mx", [P, 2, 12])
    res = ph.sb("res", [8, P])
    mrow = ph.sb("mrow", [8, 2, 3, P], BF16)
    OT = ph.sb("OT", [P, T])
    rinv = ph.sb("rinv", [P, 2, CT, HU])
    pS = [ph.ps(f"S{i}") for i in range(2)]
    pE = [ph.ps(f"E{i}") for i in range(2)]
    pO = [ph.ps(f"O{i}") for i in range(2)]
    pX = [ph.ps(f"X{i}") for i in range(2)]
    sunits = [(i, c) for i in range(TT) for c in range(i // CT + 1)]
    eunits = [(c, j) for c in range(2) for j in range((c + 1) * CT)]
    U = len(sunits)
    HELD = 3
    zeroed, consts = ph.sem("zeroed"), ph.sem("consts")
    stack_in = [ph.sem(f"stackin{u}") for u in range(HU)]
    mrow_in = [ph.sem(f"mrowin{u}") for u in range(HU)]
    LOADS = 16 * 8
    s_ps, s_max, m_all, m_ps, m_part, m_row = (ph.sem(n) for n in ("sps", "smax", "mall", "mps", "mpart", "mrow"))
    e_ps, e_sb, weighed, v_sb = (ph.sem(n) for n in ("eps", "esb", "weighed", "vsb"))
    passed, passed_pe = ph.sem("passed"), ph.sem("passedpe")
    o_sb, t_ps, r_inv, t_used = (ph.sem(n) for n in ("osb", "tps", "rinvs", "tused"))

    def loops(eng, body):
        with eng.Fori(0, IT - 1) as it:
            body(it, False)
        body(IT - 1, True)

    with nc.Block() as block:
        @block.gpsimd
        def _(pool):
            for u in range(HU):
                pool.memset(QS[u][:, :], 0.0)
                pool.memset(KS[u][:, :], 0.0).then_inc(zeroed, 1)
            pool.memset(Vg[:, :, :, :].rearrange("p u t d -> p (u t d)"), 0.0).then_inc(consts, 1)
            pool.tensor_copy(identb[:, :], G["ident"][:, :]).then_inc(consts, 1)
            pool.memset(maskq[:, :], 0.0).then_inc(consts, 1)
            pool.memset(maskk[:, :], 0.0).then_inc(consts, 1)
            pool.wait_ge(consts, 4)
            pool.affine_select(out=maskq[:, :], in_=maskq[:, :], compare_op=ALU.is_ge, fill=-3.0e38,
                               base=0, pattern=[[-1, P]], channel_multiplier=1).then_inc(consts, 1)
            pool.affine_select(out=maskk[:, :], in_=maskk[:, :], compare_op=ALU.is_ge, fill=-3.0e38,
                               base=0, pattern=[[1, P]], channel_multiplier=-1).then_inc(consts, 1)


            def values(it, u):
                pool.tensor_copy(Vg[:, u, :, 0:9], V9[:, bass.ds(it, 1), u, :, :]
                                 .rearrange("p o t d -> p (o t) d")).then_inc(v_sb, 1)

            pool.wait_ge(consts, 6)
            for u in range(HU):
                values(0, u)
            with pool.Fori(0, IT - 1) as it:
                for u in range(HU):
                    pool.wait_ge(weighed, NP + (it * HU + u + 1) * U)
                    pool.sem_inc(passed, 1)
                    values(it + 1, u)

        @block.sync
        def _(sp):
            def load(it, u):
                at = (it * HU + u) * 8 * T
                part = N * P
                for a in range(3):
                    rows = slice(24 * a, 24 * a + 24)
                    sp.dma_start(QS[u][rows, :], bass.AP(scr.tensor, at + a * part, [[0, 3], [T, 8], [1, T]]))\
                      .then_inc(stack_in[u], 16)
                    sp.dma_start(KS[u][rows, :], bass.AP(scr.tensor, at + 3 * part, [[part, 3], [T, 8], [1, T]]))\
                      .then_inc(stack_in[u], 16)
                sp.dma_start(QS[u][MR:MR + 6, :], qtail).then_inc(stack_in[u], 16)
                sp.dma_start(KS[u][MR:MR + 6, :], bass.AP(ktail.tensor, (it * HU + u) * 6 * T, [[T, 6], [1, T]]))\
                  .then_inc(stack_in[u], 16)

            def maxima(h, u):
                sp.wait_ge(m_row, h + 1)
                for a in range(3):
                    sp.dma_start(QS[u][MR + a:MR + a + 1, :].rearrange("o (t q) -> o t q", t=TT), mrow[:, u % 2, a, :])\
                      .then_inc(mrow_in[u], 16)

            sp.wait_ge(zeroed, HU)
            for u in range(HU):
                load(0, u)
            maxima(0, 0)
            with sp.Fori(0, IT - 1) as it:
                for u in range(HU):
                    maxima(it * HU + u + 1, (u + 1) % HU)
                    sp.wait_ge(e_ps, (it * HU + u + 1) * U)
                    load(it + 1, u)
            for u in range(HU - 1):
                maxima((IT - 1) * HU + u + 1, u + 1)

        @block.tensor
        def _(pe):
            def first(it, u, k):
                h = it * HU + u
                i, c = sunits[k]
                if k == 0:
                    pe.wait_ge(stack_in[u], (it + 1) * LOADS)
                pe.wait_ge(s_max, h * U + k + 1)
                n = min((c + 1) * CH, (i + 1) * P) - c * CH
                diag = c == i // CT
                ins = pe.matmul(pS[k % 2][:, 0:n], QS[u][:, i * P:(i + 1) * P], KS[u][:, c * CH:c * CH + n],
                                start=True, stop=not diag)
                if diag:
                    ins = pe.matmul(pS[k % 2][:, n - P:n], identb[:, :], maskq[:, :], start=False, stop=True)
                ins.then_inc(s_ps, 1)

            def turn_maxima(h, s):
                pe.wait_ge(m_all, h + 1)
                pe.transpose(pX[0][0:TT, 0:P], mx[:, s, 0:TT], G["ident"][:, :]).then_inc(m_ps, 1)

            def second(it, u, n):
                h = it * HU + u
                c, j = eunits[n]
                if n == 0:
                    pe.wait_ge(mrow_in[u], (it + 1) * 48)
                pe.wait_ge(e_sb, h * U + n + 1)
                off = max(0, j * P - c * CH)
                diag = j >= c * CT
                ins = pe.matmul(pE[n % 2][:, off:CH], KS[u][:, j * P:(j + 1) * P], QS[u][:, c * CH + off:(c + 1) * CH],
                                start=True, stop=not diag)
                if diag:
                    ins = pe.matmul(pE[n % 2][:, off:off + P], identb[:, :], maskk[:, :], start=False, stop=True)
                ins.then_inc(e_ps, 1)

            def weigh(it, u, n):
                h = it * HU + u
                c, j = eunits[n]
                if n == 0:
                    pe.wait_ge(v_sb, h + 1)
                if u == 0 and j == 0:
                    pe.wait_ge(o_sb, 2 * it + c + 1)
                pe.wait_ge(e_sb, h * U + n + 3)
                off = max(0, j * P - c * CH)
                pe.matmul(pO[c][32 * u:32 * u + 32, off:CH], Vg[:, u, j, :], PT[:, n % NP, off:CH],
                          start=(j == 0), stop=(j == (c + 1) * CT - 1)).then_inc(weighed, 1)

            def body(it, last):
                before = None
                for u in range(HU):
                    ahead = (it, u + 2) if u + 2 < HU else None if last else (it + 1, u + 2 - HU)
                    held = HELD if u == HU - 1 else 0
                    for n in range(U):
                        second(it, u, n)
                        if ahead and n < U - held:
                            first(*ahead, n)
                        if before:
                            weigh(*before)
                        before = (it, u, n)
                        if n == 1 and not (last and u == HU - 1):
                            if u == 0:
                                pe.wait_ge(t_used, 2 * it + 2)
                            pe.wait_ge(m_row, it * HU + u + 1)
                            pe.sem_inc(passed_pe, 1)
                            turn_maxima(it * HU + u + 1, (u + 1) % 2)
                for k in range(U - HELD, U):
                    if ahead:
                        first(*ahead, k)
                    if k == U - HELD:
                        weigh(*before)
                for c in range(2):
                    pe.wait_ge(o_sb, 2 * it + c + 3)
                    pe.wait_ge(t_used, 2 * it + c + 1)
                    for t in range(CT):
                        ins = pe.transpose(pX[1 - c][:, t * P:(t + 1) * P], OT[:, (c * CT + t) * P:(c * CT + t + 1) * P],
                                           G["ident"][:, :])
                    ins.then_inc(t_ps, 1)

            pe.wait_ge(consts, 6)
            pe.sem_inc(weighed, NP)
            for u in range(2):
                for k in range(U):
                    first(0, u, k)
            turn_maxima(0, 0)
            loops(pe, body)

        @block.scalar
        def _(act):
            act.sem_inc(e_sb, 2)

            def body(it, last):
                for u in range(HU):
                    for n, (c, j) in enumerate(eunits):
                        at = (it * HU + u) * U + n
                        off = max(0, j * P - c * CH)
                        act.wait_ge(e_ps, at + 1)
                        act.wait_ge(weighed, at + 1)
                        act.activation(PT[:, n % NP, off:CH], pE[n % 2][:, off:CH], ACT.Exp).then_inc(e_sb, 1)
            loops(act, body)

        @block.vector
        def _(dve):
            dve.sem_inc(s_max, 2)
            dve.sem_inc(o_sb, 2)
            dve.sem_inc(t_used, 2)

            def maximum(h, s, k):
                i, c = sunits[k]
                n = min((c + 1) * CH, (i + 1) * P) - c * CH
                slot = i + CT * c
                dve.wait_ge(s_ps, h * U + k + 1)
                dve.tensor_reduce(mx[:, s, slot:slot + 1], pS[k % 2][:, 0:n], AX.X, ALU.max).then_inc(s_max, 1)

            def join(h, s):
                dve.wait_ge(s_max, (h + 1) * U + 2)
                dve.tensor_tensor(mx[:, s, CT:TT], mx[:, s, CT:TT], mx[:, s, TT:TT + CT], ALU.max).then_inc(m_all, 1)

            def split(h, s):
                x = pX[0][0:TT, 0:P]
                dve.wait_ge(m_ps, h + 1)
                dve.tensor_scalar(mrow[:, s, 0, :], x, -1.0, None, ALU.mult).then_inc(m_part, 1)
                dve.wait_ge(m_part, h * 3 + 1)
                dve.scalar_tensor_tensor(res[:, :], x, -1.0, mrow[:, s, 0, :], ALU.mult, ALU.subtract).then_inc(m_part, 1)
                dve.wait_ge(m_part, h * 3 + 2)
                dve.tensor_copy(mrow[:, s, 1, :], res[:, :]).then_inc(m_part, 1)
                dve.wait_ge(m_part, h * 3 + 3)
                dve.tensor_tensor(mrow[:, s, 2, :], res[:, :], mrow[:, s, 1, :], ALU.subtract).then_inc(m_row, 1)

            def empty(it, c, n):
                dve.wait_ge(weighed, NP + (it * HU + HU - 1) * U + n)
                dve.tensor_copy(OT[:, c * CH:(c + 1) * CH], pO[c][:, :]).then_inc(o_sb, 1)

            def normalise(it, c):
                v = pX[1 - c][:, :].rearrange("p (t u d) -> p t u d", t=CT, u=HU)
                dve.wait_ge(t_ps, 2 * it + c + 1)
                dve.reciprocal(rinv[:, c, :, :], v[:, :, :, 8]).then_inc(r_inv, 1)
                dve.wait_ge(r_inv, 2 * it + c + 1)
                out = (mix[:, it, c * CT:(c + 1) * CT, :] if isinstance(it, int) else
                       mix[:, bass.ds(it, 1), c * CT:(c + 1) * CT, :].rearrange("p o t c -> p (o t) c"))
                dve.tensor_tensor(out.rearrange("p t (u d) -> p t u d", u=HU), v[:, :, :, 0:8],
                                  rinv[:, c, :, :].unsqueeze(3).to_broadcast([P, CT, HU, 8]), ALU.mult).then_inc(t_used, 1)

            def body(it, last):
                for u in range(HU):
                    h = it * HU + u
                    ahead = not (last and u + 2 >= HU)
                    for k in range(U):
                        if ahead:
                            maximum(h + 2, u % 2, k)
                        if k == 1 and not (last and u == HU - 1):
                            split(h + 1, (u + 1) % 2)
                        if u == HU - 1 and k == 6:
                            empty(it, 0, CT)
                        if u == HU - 1 and k == U - HELD:
                            empty(it, 1, U)
                    if ahead:
                        join(h + 2, u % 2)
                for c in range(2):
                    normalise(it, c)

            for h in range(2):
                for k in range(U):
                    maximum(h, h, k)
                join(h, h)
            split(0, 0)
            loops(dve, body)
    ph.end()


def alibi_out(nc, G, wo):
    ph = Phase(nc, "a2o")
    X = G["X"]
    mix = G["XR"][:, :, :].rearrange("p a b -> p (a b)").rearrange("p (i t c) -> p i t c", i=4 * B, t=TT)
    rows = ph.sb("rows", [P, 2, CT, 4, 32])
    mT = ph.sb("mT", [P, 2, CH])
    pT = [ph.ps(f"T{i}") for i in range(2)]
    pY = [ph.ps(f"Y{i}") for i in range(2)]
    r_sb, t_ps, t_sb, y_ps, y_sb = (ph.sem(n) for n in ("rsb", "tps", "tsb", "yps", "ysb"))
    chunks = NT // CT
    with nc.Block() as block:
        @block.tensor
        def _(pe):
            def turn(c):
                if c >= 2:
                    pe.wait_ge(t_sb, c - 1)
                pe.wait_ge(r_sb, c + 1)
                for j in range(CT):
                    ins = pe.transpose(pT[c % 2][:, j * P:(j + 1) * P],
                                       rows[:, c % 2, j, :, :].rearrange("p g d -> p (g d)"), G["ident"][:, :])
                ins.then_inc(t_ps, 1)

            turn(0)
            for c in range(chunks):
                if c + 1 < chunks:
                    turn(c + 1)
                pe.wait_ge(t_sb, c + 1)
                if c >= 2:
                    pe.wait_ge(y_sb, c - 1)
                for j in range(CT):
                    ins = pe.matmul(pY[c % 2][:, j * P:(j + 1) * P], mT[:, c % 2, j * P:(j + 1) * P], wo,
                                    start=True, stop=True)
                ins.then_inc(y_ps, 1)

        @block.scalar
        def _(act):
            for c in range(chunks):
                act.wait_ge(t_ps, c + 1)
                if c >= 2:
                    act.wait_ge(y_ps, c - 1)
                act.copy(mT[:, c % 2, :], pT[c % 2][:, :]).then_inc(t_sb, 1)

        @block.vector
        def _(dve):
            def gather(c):
                b, h = divmod(c, TT // CT)
                if c >= 2:
                    dve.wait_ge(t_ps, c - 1)
                dve.tensor_copy(rows[:, c % 2, :, :, :].rearrange("p t g d -> p g t d"),
                                mix[:, 4 * b:4 * b + 4, h * CT:(h + 1) * CT, :]).then_inc(r_sb, 1)

            gather(0)
            for c in range(chunks):
                if c + 1 < chunks:
                    gather(c + 1)
                dve.wait_ge(y_ps, c + 1)
                xv = X[:, c * CT:(c + 1) * CT, :]
                dve.tensor_tensor(xv, xv, pY[c % 2][:, :].rearrange("p (k d) -> p k d", k=CT), ALU.add).then_inc(y_sb, 1)
    ph.end()


def moe_top2(nc, G, tag, gw, gb, w1, b1, w2, b2, rows):
    ph = Phase(nc, tag)
    X, XNT = G["X"], G["XNT"]
    E, FC = 8, 4
    lng, lnb = ph.sb("lng", [P, P]), ph.sb("lnb", [P, P])
    lg = ph.sb("lg", [P, CH])
    lgt, ex, pr = (ph.sb(n, [P, CT, E]) for n in ("lgt", "ex", "pr"))
    mx = ph.sb("mx", [P, CT, E])
    mi = ph.sb("mi", [P, CT, E], U32)
    mf, keep1, keep = (ph.sb(n, [P, CT, E]) for n in ("mf", "keep1", "keep"))
    io = ph.sb("io", [P, CT, E])
    sm, ri = ph.sb("sm", [P, CT]), ph.sb("ri", [P, CT])
    prT = ph.sb("prT", [E, CH])
    h = ph.sb("h", [P, 2, FC, CH])
    acc = ph.sb("acc", [P, CT, P])
    st, mv = ph.sb("st", [P, CT, 6]), ph.sb("mv", [P, CT, 2])
    sd, rs = ph.sb("sd", [P, CT]), ph.sb("rs", [P, CT])
    on = ph.sb("on", [P, CT, P])
    pU = [ph.ps(f"U{i}") for i in range(3)]
    pY = [ph.ps(f"Y{i}") for i in range(2)]
    pR = ph.ps("R")
    rows_in, io_done = ph.sem("rowsin"), ph.sem("iodone")
    names = ("lg_ps", "lg_sb", "lgt_ps", "lgt_sb", "mx_done", "mi_done", "mf_done", "keep1_done", "keep_done", "sub_done",
             "exp_done", "mask_done", "sum_done", "ri_done", "pr_done", "prT_ps", "prT_sb", "bias_ps", "acc0", "st_done",
             "mv_done", "sd_done", "rs_done", "on_done", "aff_done", "x_done")
    S = {n: ph.sem(n) for n in names}
    up, gelu, down, added = (ph.sem(n) for n in ("up", "gelu", "down", "added"))
    with nc.Block() as block:
        @block.sync
        def _(sp):
            sp.dma_start(lng[:, :], bass.AP(rows.tensor, 0, [[0, P], [1, P]])).then_inc(rows_in, 16)
            sp.dma_start(lnb[:, :], bass.AP(rows.tensor, P, [[0, P], [1, P]])).then_inc(rows_in, 16)
            sp.wait_ge(rows_in, 32)

        @block.gpsimd
        def _(pool):
            pool.iota(io[:, :, :], [[0, CT], [1, E]], base=0, channel_multiplier=0,
                      allow_small_or_imprecise_dtypes=True).then_inc(io_done, 1)
            pool.memset(lg[:, :], 0.0).then_inc(io_done, 1)

        @block.tensor
        def _(pe):
            with pe.Fori(0, B) as b:
                with pe.Fori(0, 2) as half:
                    c = b * 2 + half
                    x = XNT[:, b, bass.ds(half * CH + 1, CH)]

                    def ups(e):
                        for f in range(FC):
                            n = e * FC + f
                            if n >= 3:
                                pe.wait_ge(gelu, c * (E * FC) + n - 2)
                            pe.matmul(pU[n % 3][:, :], w1[:, n * P:(n + 1) * P], x, start=True, stop=True).then_inc(up, 1)

                    def downs(e):
                        pe.wait_ge(gelu, c * (E * FC) + (e + 1) * FC)
                        if e >= 2:
                            pe.wait_ge(added, c * E + e - 1)
                        for k in range(CT):
                            for f in range(FC):
                                ins = pe.matmul(pY[e % 2][:, k * P:(k + 1) * P], h[:, e % 2, f, k * P:(k + 1) * P],
                                                w2[:, (e * FC + f) * P:(e * FC + f + 1) * P],
                                                start=(f == 0), stop=(f == FC - 1))
                        ins.then_inc(down, 1)

                    pe.matmul(pR[0:E, :], gw, x, start=True, stop=True).then_inc(S["lg_ps"], 1)
                    ups(0)
                    pe.wait_ge(S["lg_sb"], c + 1)
                    for k in range(CT):
                        ins = pe.transpose(pR[:, k * P:(k + 1) * P], lg[:, k * P:(k + 1) * P], G["ident"][:, :])
                    ins.then_inc(S["lgt_ps"], 1)
                    ups(1)
                    pe.wait_ge(S["pr_done"], c + 1)
                    for k in range(CT):
                        ins = pe.transpose(pR[0:E, k * P:(k + 1) * P], pr[:, k, :], G["ident"][:, :])
                    ins.then_inc(S["prT_ps"], 1)
                    pe.wait_ge(S["prT_sb"], c + 1)
                    for k in range(CT):
                        ins = pe.matmul(pR[:, k * P:(k + 1) * P], prT[:, k * P:(k + 1) * P], b2, start=True, stop=True)
                    ins.then_inc(S["bias_ps"], 1)
                    for e in range(E):
                        downs(e)
                        if e + 2 < E:
                            ups(e + 2)
                    pe.wait_ge(added, c * E + E)
                    pe.wait_ge(S["acc0"], c + 1)

        @block.scalar
        def _(act):
            with act.Fori(0, B) as b:
                with act.Fori(0, 2) as half:
                    c = b * 2 + half

                    def gelus(e):
                        if e >= 2:
                            act.wait_ge(down, c * E + e - 1)
                        for f in range(FC):
                            n = e * FC + f
                            act.wait_ge(up, c * (E * FC) + n + 1)
                            act.activation(h[:, e % 2, f, :], pU[n % 3][:, :], ACT.Gelu, bias=b1[:, n:n + 1]).then_inc(gelu, 1)

                    gelus(0)
                    act.wait_ge(S["sub_done"], c + 1)
                    act.activation(ex[:, :, :], ex[:, :, :], ACT.Exp).then_inc(S["exp_done"], 1)
                    for e in range(1, E):
                        gelus(e)
                    act.wait_ge(S["mv_done"], c + 1)
                    act.activation(sd[:, :], mv[:, :, 1], ACT.Sqrt, bias=G["eps"][:, 0:1]).then_inc(S["sd_done"], 1)

        @block.vector
        def _(dve):
            dve.wait_ge(io_done, 2)
            dve.wait_ge(rows_in, 32)
            with dve.Fori(0, B) as b:
                with dve.Fori(0, 2) as half:
                    c = b * 2 + half

                    def step(name, ins):
                        ins.then_inc(S[name], 1)
                        dve.wait_ge(io_done, 1)
                        dve.wait_ge(S[name], c + 1)

                    dve.wait_ge(S["lg_ps"], c + 1)
                    dve.tensor_scalar(lg[0:E, :], pR[0:E, :], gb, 1.0 / 0.9, ALU.add, ALU.mult).then_inc(S["lg_sb"], 1)
                    dve.wait_ge(S["lgt_ps"], c + 1)
                    step("lgt_sb", dve.tensor_copy(lgt[:, :, :], pR[:, :].rearrange("p (k e) -> p k e", k=CT)[:, :, 0:E]))
                    for k in range(CT):
                        ins = dve.max(mx[:, k, :], lgt[:, k, :])
                    step("mx_done", ins)
                    for k in range(CT):
                        ins = dve.max_index(mi[:, k, :], mx[:, k, :], lgt[:, k, :])
                    ins.then_inc(S["mi_done"], 1)
                    dve.tensor_tensor(ex[:, :, :], lgt[:, :, :], mx[:, :, 0:1].to_broadcast([P, CT, E]),
                                      ALU.subtract).then_inc(S["sub_done"], 1)
                    dve.wait_ge(S["mi_done"], c + 1)
                    step("mf_done", dve.tensor_copy(mf[:, :, :], mi[:, :, :]))
                    dve.tensor_tensor(keep1[:, :, :], io[:, :, :], mf[:, :, 0:1].to_broadcast([P, CT, E]), ALU.is_equal)
                    step("keep1_done", dve.tensor_tensor(keep[:, :, :], io[:, :, :],
                                                         mf[:, :, 1:2].to_broadcast([P, CT, E]), ALU.is_equal))
                    step("keep_done", dve.tensor_tensor(keep[:, :, :], keep[:, :, :], keep1[:, :, :], ALU.add))
                    dve.wait_ge(S["exp_done"], c + 1)
                    step("mask_done", dve.tensor_tensor(keep1[:, :, :], ex[:, :, :], keep[:, :, :], ALU.mult))
                    step("sum_done", dve.tensor_reduce(sm[:, :], keep1[:, :, :], AX.X, ALU.add))
                    step("ri_done", dve.reciprocal(ri[:, :], sm[:, :]))
                    step("pr_done", dve.tensor_tensor(pr[:, :, :], keep1[:, :, :],
                                                      ri[:, :].rearrange("p (k o) -> p k o", o=1).to_broadcast([P, CT, E]), ALU.mult))
                    dve.wait_ge(S["prT_ps"], c + 1)
                    dve.tensor_copy(prT[:, :], pR[0:E, :]).then_inc(S["prT_sb"], 1)
                    dve.wait_ge(S["bias_ps"], c + 1)
                    step("acc0", dve.tensor_copy(acc[:, :, :], pR[:, :].rearrange("p (k d) -> p k d", k=CT)))
                    for e in range(E):
                        dve.wait_ge(down, c * E + e + 1)
                        if e:
                            dve.wait_ge(added, c * E + e)
                        for k in range(CT):
                            ins = dve.scalar_tensor_tensor(acc[:, k, :], pY[e % 2][:, k * P:(k + 1) * P], pr[:, k, e:e + 1],
                                                           acc[:, k, :], ALU.mult, ALU.add)
                        ins.then_inc(added, 1)
                    dve.wait_ge(added, c * E + E)
                    for k in range(CT):
                        ins = dve.bn_stats(st[:, k, :], acc[:, k, :])
                    step("st_done", ins)
                    for k in range(CT):
                        ins = dve.bn_aggr(mv[:, k, :], st[:, k, :])
                    step("mv_done", ins)
                    dve.wait_ge(S["sd_done"], c + 1)
                    step("rs_done", dve.reciprocal(rs[:, :], sd[:, :]))
                    for k in range(CT):
                        ins = dve.tensor_scalar(on[:, k, :], acc[:, k, :], mv[:, k, 0:1], rs[:, k:k + 1], ALU.subtract, ALU.mult)
                    step("on_done", ins)
                    wide = [P, CT, P]
                    step("aff_done", dve.tensor_tensor(acc[:, :, :], on[:, :, :],
                                                       lng[:, :].rearrange("p (o d) -> p o d", o=1).to_broadcast(wide), ALU.mult))
                    step("x_done", dve.tensor_tensor(on[:, :, :], acc[:, :, :],
                                                     lnb[:, :].rearrange("p (o d) -> p o d", o=1).to_broadcast(wide), ALU.add))
                    xv = X[:, bass.ds(c * CT, CT), :]
                    dve.tensor_tensor(xv, xv, on[:, :, :], ALU.add)
    ph.end()


def moe_capacity(nc, G, tag, rw, rb, w1, b1, w2, b2, ow1, ob1, ow2, rows, buf, ybuf):
    ph = Phase(nc, tag)
    X, XNT, XR = G["X"], G["XNT"], G["XR"]
    E, FC, CAP = 8, 4, 160
    SL = E * CAP
    ST = SL // P
    lg = ph.sb("lg", [E, 2, CH])
    lgt, mx, oh, cum, tot, run, sel = (ph.sb(n, [P, NT, E]) for n in ("lgt", "mx", "oh", "cum", "tot", "run", "sel"))
    mi = ph.sb("mi", [P, NT, E], U32)
    io = ph.sb("io", [P, NT, E])
    zero = ph.sb("zero", [P, NT])
    eid, rank, valid, inval, spare, slot, sc_f, ga_f, tmp = (
        ph.sb(n, [P, NT]) for n in ("eid", "rank", "valid", "inval", "spare", "slot", "scf", "gaf", "tmp"))
    sc_i, ga_i = ph.sb("sci", [P, NT], U32), ph.sb("gai", [P, NT], U32)
    zrow = ph.sb("zrow", [P, P])
    bt = ph.sb("bt", [P, ST, P])
    bT = ph.sb("bT", [P, SL])
    he = ph.sb("he", [P, 2, FC, CAP])
    yT = ph.sb("yT", [P, SL])
    yr = ph.sb("yr", [P, ST, P])
    ob2 = ph.sb("ob2", [1, P])
    h = ph.sb("h", [P, 2, FC, CH])
    yg = ph.sb("yg", [P, 8, P])
    pU = [ph.ps(f"U{i}") for i in range(3)]
    pY = [ph.ps(f"Y{i}") for i in range(2)]
    pR = [ph.ps(f"R{i}") for i in range(2)]
    const, zeroed, scattered, loaded, stored, ob_in = (
        ph.sem(n) for n in ("const", "zeroed", "scattered", "loaded", "stored", "obin"))
    gathered = [ph.sem(f"gathered{i}") for i in range(8)]
    lg_ps, lg_sb, lgt_ps, lgt_sb, cnt_ps, own = (ph.sem(n) for n in ("lgps", "lgsb", "lgtps", "lgtsb", "cntps", "own"))
    slots_done, bt_ps, bt_sb, up, act_up, down, act_down, yt_ps, yt_sb, valid_done = (
        ph.sem(n) for n in ("slots", "btps", "btsb", "up", "actup", "down", "actdown", "ytps", "ytsb", "valid"))
    o_up, o_relu, o_down, o_add, g_add = (ph.sem(n) for n in ("oup", "orelu", "odown", "oadd", "gadd"))
    with nc.Block() as block:
        @block.sync
        def _(sp):
            sp.dma_start(ob2[:, :], rows[2:3, :]).then_inc(ob_in, 16)
            sp.wait_ge(const, 1)
            for t in range(ST):
                sp.dma_start(buf[t * P:(t + 1) * P, :], zrow[:, :]).then_inc(zeroed, 16)
            sp.dma_start(ybuf[SL:SL + 1, :], zrow[0:1, :]).then_inc(zeroed, 16)
            sp.wait_ge(scattered, 16 * NT)
            sp.dma_start(bt[:, :, :], buf[0:SL, :].rearrange("(t p) d -> p t d", p=P)).then_inc(loaded, 16)
            sp.wait_ge(yt_sb, ST)
            sp.dma_start(ybuf[0:SL, :].rearrange("(t p) d -> p t d", p=P), yr[:, :, :]).then_inc(stored, 16)
            sp.wait_ge(ob_in, 16)

        @block.gpsimd
        def _(pool):
            pool.memset(zrow[:, :], 0.0).then_inc(const, 1)
            pool.iota(io[:, :, :], [[0, NT], [1, E]], base=0, channel_multiplier=0,
                      allow_small_or_imprecise_dtypes=True).then_inc(const, 1)
            pool.iota(spare[:, :], [[P, NT]], base=SL, channel_multiplier=1,
                      allow_small_or_imprecise_dtypes=True).then_inc(const, 1)
            pool.memset(zero[:, :], 0.0).then_inc(const, 1)
            pool.wait_ge(slots_done, 1)
            pool.wait_ge(zeroed, 16 * (ST + 1))
            for t in range(NT):
                pool.indirect_dma_start(out=buf[:, :], out_offset=bass.IndirectOffsetOnAxis(ap=sc_i[:, t:t + 1], axis=0),
                                        in_=XR[:, t, :], in_offset=None).then_inc(scattered, 16)
            pool.wait_ge(stored, 16)
            for t in range(NT):
                if t >= 8:
                    pool.wait_ge(g_add, t - 7)
                pool.indirect_dma_start(out=yg[:, t % 8, :], out_offset=None, in_=ybuf[:, :],
                                        in_offset=bass.IndirectOffsetOnAxis(ap=ga_i[:, t:t + 1], axis=0)).then_inc(gathered[t % 8], 16)

        @block.tensor
        def _(pe):
            pe.wait_ge(ob_in, 16)
            for c in range(NT // CT):
                x = XNT[:, c // 2, 1 + (c % 2) * CH:1 + (c % 2 + 1) * CH]
                if c >= 2:
                    pe.wait_ge(lgt_sb, c - 1)
                pe.matmul(pR[c % 2][0:E, :], rw, x, start=True, stop=True).then_inc(lg_ps, 1)
                pe.wait_ge(lg_sb, c + 1)
                for k in range(CT):
                    ins = pe.transpose(pR[c % 2][:, k * E:(k + 1) * E], lg[:, c % 2, k * P:(k + 1) * P], G["ident"][0:E, 0:E])
                ins.then_inc(lgt_ps, 1)
            pe.wait_ge(own, 3)
            flat = oh[:, :, :].rearrange("p n e -> p (n e)")
            pe.matmul(pR[0][:, 0:NT * E], G["tri"][:, :], flat, start=True, stop=True)
            pe.matmul(pR[1][:, 0:NT * E], G["ones"][:, :], flat, start=True, stop=True).then_inc(cnt_ps, 1)

            with pe.Fori(0, B) as b:
                with pe.Fori(0, 2) as half:
                    c = b * 2 + half
                    x = XNT[:, b, bass.ds(half * CH + 1, CH)]
                    for f in range(FC):
                        if f >= 3:
                            pe.wait_ge(o_relu, c * FC + f - 2)
                        pe.matmul(pU[f % 3][:, :], ow1[:, f * P:(f + 1) * P], x, start=True, stop=True).then_inc(o_up, 1)
                    pe.wait_ge(o_relu, c * FC + FC)
                    for k in range(CT):
                        for f in range(FC):
                            pe.matmul(pY[0][:, k * P:(k + 1) * P], h[:, 0, f, k * P:(k + 1) * P], ow2[:, f * P:(f + 1) * P],
                                      start=(f == 0), stop=False)
                        ins = pe.matmul(pY[0][:, k * P:(k + 1) * P], G["ones"][0:1, :], ob2[:, :], start=False, stop=True)
                    ins.then_inc(o_down, 1)
                    pe.wait_ge(o_add, c + 1)
            pe.wait_ge(loaded, 16)
            for t in range(ST):
                if t >= 2:
                    pe.wait_ge(bt_sb, t - 1)
                pe.transpose(pR[t % 2][:, 0:P], bt[:, t, :], G["ident"][:, :]).then_inc(bt_ps, 1)
            pe.wait_ge(bt_sb, ST)

            def ups(e):
                for f in range(FC):
                    n = e * FC + f
                    if n >= 3:
                        pe.wait_ge(act_up, n - 2)
                    pe.matmul(pU[n % 3][:, 0:CAP], w1[:, n * P:(n + 1) * P], bT[:, e * CAP:(e + 1) * CAP],
                              start=True, stop=True).then_inc(up, 1)

            def downs(e):
                pe.wait_ge(act_up, (e + 1) * FC)
                if e >= 2:
                    pe.wait_ge(act_down, e - 1)
                for f in range(FC):
                    n = e * FC + f
                    ins = pe.matmul(pY[e % 2][:, 0:CAP], w2[:, n * P:(n + 1) * P], he[:, e % 2, f, :],
                                    start=(f == 0), stop=(f == FC - 1))
                ins.then_inc(down, 1)

            ups(0)
            for e in range(E):
                if e + 1 < E:
                    ups(e + 1)
                downs(e)
            pe.wait_ge(act_down, E)
            for t in range(ST):
                if t >= 2:
                    pe.wait_ge(yt_sb, t - 1)
                pe.transpose(pR[t % 2][:, 0:P], yT[:, t * P:(t + 1) * P], G["ident"][:, :]).then_inc(yt_ps, 1)

        @block.scalar
        def _(act):
            with act.Fori(0, B) as b:
                with act.Fori(0, 2) as half:
                    c = b * 2 + half
                    for f in range(FC):
                        act.wait_ge(o_up, c * FC + f + 1)
                        act.activation(h[:, 0, f, :], pU[f % 3][:, :], ACT.Relu, bias=ob1[:, f:f + 1]).then_inc(o_relu, 1)
            def outputs(e):
                act.wait_ge(down, e + 1)
                act.activation(yT[:, e * CAP:(e + 1) * CAP], pY[e % 2][:, 0:CAP], ACT.Identity,
                               bias=b2[:, e:e + 1]).then_inc(act_down, 1)

            for e in range(E):
                for f in range(FC):
                    n = e * FC + f
                    if e >= 2:
                        act.wait_ge(down, e - 1)
                    act.wait_ge(up, n + 1)
                    act.activation(he[:, e % 2, f, :], pU[n % 3][:, 0:CAP], ACT.Relu, bias=b1[:, n:n + 1]).then_inc(act_up, 1)
                if e >= 1:
                    outputs(e - 1)
            outputs(E - 1)

        @block.vector
        def _(dve):
            done = [0]

            def chain(ins):
                done[0] += 1
                ins.then_inc(own, 1)
                dve.wait_ge(own, done[0])

            for c in range(NT // CT):
                dve.wait_ge(lg_ps, c + 1)
                dve.tensor_scalar(lg[:, c % 2, :], pR[c % 2][0:E, :], rb, None, ALU.add).then_inc(lg_sb, 1)
                dve.wait_ge(lgt_ps, c + 1)
                dve.tensor_copy(lgt[:, c * CT:(c + 1) * CT, :],
                                pR[c % 2][:, 0:CT * E].rearrange("p (k e) -> p k e", k=CT)).then_inc(lgt_sb, 1)
            dve.wait_ge(lgt_sb, NT // CT)
            dve.wait_ge(const, 4)
            for t in range(NT):
                ins = dve.max(mx[:, t, :], lgt[:, t, :])
            chain(ins)
            for t in range(NT):
                ins = dve.max_index(mi[:, t, :], mx[:, t, :], lgt[:, t, :])
            chain(ins)
            dve.tensor_copy(eid[:, :], mi[:, :, 0]).then_inc(valid_done, 1)
            dve.wait_ge(valid_done, 1)
            wide = [P, NT, E]
            chain(dve.tensor_tensor(oh[:, :, :], io[:, :, :],
                                    eid[:, :].rearrange("p (n o) -> p n o", o=1).to_broadcast(wide), ALU.is_equal))
            dve.wait_ge(cnt_ps, 1)
            dve.tensor_copy(cum[:, :, :], pR[0][:, 0:NT * E].rearrange("p (n e) -> p n e", e=E))
            chain(dve.tensor_copy(tot[:, :, :], pR[1][:, 0:NT * E].rearrange("p (n e) -> p n e", e=E)))
            for e in range(E):
                ins = dve.tensor_tensor_scan(run[:, :, e], tot[:, :, e], zero[:, :], 0.0, ALU.add, ALU.add)
            chain(ins)
            chain(dve.tensor_tensor(run[:, :, :], run[:, :, :], tot[:, :, :], ALU.subtract))
            chain(dve.tensor_tensor(cum[:, :, :], cum[:, :, :], run[:, :, :], ALU.add))
            chain(dve.tensor_tensor(sel[:, :, :], cum[:, :, :], oh[:, :, :], ALU.mult))
            chain(dve.tensor_reduce(rank[:, :], sel[:, :, :], AX.X, ALU.add))
            chain(dve.tensor_scalar(valid[:, :], rank[:, :], float(CAP), None, ALU.is_le))
            dve.tensor_scalar(inval[:, :], valid[:, :], -1.0, 1.0, ALU.mult, ALU.add)
            chain(dve.tensor_scalar(tmp[:, :], eid[:, :], float(CAP), -1.0, ALU.mult, ALU.add))
            chain(dve.tensor_tensor(slot[:, :], tmp[:, :], rank[:, :], ALU.add))
            chain(dve.tensor_tensor(slot[:, :], slot[:, :], valid[:, :], ALU.mult))
            dve.tensor_tensor(tmp[:, :], spare[:, :], inval[:, :], ALU.mult)
            chain(dve.tensor_scalar(ga_f[:, :], inval[:, :], float(SL), None, ALU.mult))
            chain(dve.tensor_tensor(sc_f[:, :], slot[:, :], tmp[:, :], ALU.add))
            chain(dve.tensor_tensor(ga_f[:, :], slot[:, :], ga_f[:, :], ALU.add))
            dve.tensor_copy(sc_i[:, :], sc_f[:, :])
            dve.tensor_copy(ga_i[:, :], ga_f[:, :]).then_inc(slots_done, 1)
            for c in range(NT // CT):
                dve.wait_ge(o_down, c + 1)
                for k in range(CT):
                    t = c * CT + k
                    ins = dve.scalar_tensor_tensor(X[:, t, :], pY[0][:, k * P:(k + 1) * P], inval[:, t:t + 1], X[:, t, :],
                                                   ALU.mult, ALU.add)
                ins.then_inc(o_add, 1)
            for t in range(ST):
                dve.wait_ge(bt_ps, t + 1)
                dve.tensor_copy(bT[:, t * P:(t + 1) * P], pR[t % 2][:, 0:P]).then_inc(bt_sb, 1)
            for t in range(ST):
                dve.wait_ge(yt_ps, t + 1)
                dve.tensor_copy(yr[:, t, :], pR[t % 2][:, 0:P]).then_inc(yt_sb, 1)
            for t in range(NT):
                dve.wait_ge(gathered[t % 8], 16 * (t // 8 + 1))
                dve.tensor_tensor(X[:, t, :], X[:, t, :], yg[:, t % 8, :], ALU.add).then_inc(g_add, 1)
    ph.end()


def wkv(nc, G, tag, w):
    ph = Phase(nc, tag)
    X, XNT = G["X"], G["XNT"]
    HK = 8
    GN_EPS = 1e-5 * 64
    dx, x5, t5a, xa, xb = (ph.sb(n, [P, T]) for n in ("dx", "x5", "t5a", "xa", "xb"))
    t5b = ph.sb("t5b", [32, T])
    td = ph.sb("td", [64, T])
    r, k, dec, g, gate = (ph.sb(n, [P, T]) for n in ("r", "k", "dec", "g", "gate"))
    kv, Sf, Ss, Sr = (ph.sb(n, [P, 2, T]) for n in ("kv", "Sf", "Ss", "Sr"))
    Sb = ph.sb("Sb", [P, 2, T + 1])
    eps = ph.sb("geps", [P, 1])
    pA, pB, pC, pD = (ph.ps(n, (P, 2 * CH)) for n in "ABCD")
    setup = ph.sem("setup")
    made = {}

    def S(name):
        if name not in made:
            made[name] = ph.sem(name)
        return made[name]

    def halves():
        return (slice(0, CH), slice(CH, T))

    mixes = ["w", "k", "v", "r", "g"]
    with nc.Block() as block:
        @block.gpsimd
        def _(pool):
            pool.memset(eps[:, :], GN_EPS)
            pool.memset(Sb[:, :, T:T + 1], 0.0).then_inc(setup, 1)
            with pool.Fori(0, B) as b:
                for v in range(HK):
                    n = b * HK + v
                    pool.wait_ge(S("bwd"), n + 1)
                    if v >= 2:
                        pool.wait_ge(S("y_mm"), n - 1)
                    pool.tensor_tensor(Ss[:, v % 2, :], Sf[:, v % 2, :], Sb[:, v % 2, 1:T + 1], ALU.add).then_inc(S("ssum"), 1)
                    pool.wait_ge(S("ssum"), n + 1)
                    pool.tensor_tensor(Sr[:, v % 2, :], Ss[:, v % 2, :], r[:, :], ALU.mult).then_inc(S("sr"), 1)

        @block.tensor
        def _(pe):
            def product(out, lhsT, rhs, name):
                for cut in halves():
                    ins = pe.matmul(out[:, cut], lhsT, rhs[:, cut], start=True, stop=True)
                ins.then_inc(S(name), 1)

            def reduce(pe, b, v):
                n = b * HK + v
                if v == 0:
                    pe.wait_ge(S("g_sb"), b + 1)
                pe.wait_ge(S("sr"), n + 1)
                for cut in halves():
                    ins = pe.matmul(pD[:, cut], w["pick"][:, v * P:(v + 1) * P], Sr[:, v % 2, cut],
                                    start=(v == 0), stop=(v == HK - 1), skip_group_check=True)
                ins.then_inc(S("y_mm"), 1)

            def projection(pe, b, product, name):
                if name == "v":
                    return
                pe.wait_ge(S("mix2_" + name), b + 1)
                src = {"w": xa, "k": xb, "r": xb, "g": xa}[name]
                if name == "w":
                    pe.wait_ge(S("gate"), b + 1)
                    product(pC[0:64, :], w["decay_w1"], src, "d1_ps")
                    pe.wait_ge(S("td"), b + 1)
                    product(pC, w["decay_w2"][0:64, :], td, "d2_ps")
                else:
                    last = {"k": "dec", "r": "k", "g": "r"}[name]
                    bank = {"k": pD, "r": pC, "g": pD}[name]
                    pe.wait_ge(S(last + "_sb"), b + 1)
                    product(bank, w["W" + name], src, name + "_ps")

            with pe.Fori(0, B) as b:
                pe.wait_ge(S("x5"), b + 1)
                product(pA, w["maa_w1"][:, 0:P], x5, "t5a_ps")
                product(pB[0:32, :], w["maa_w1"][:, P:P + 32], x5, "t5b_ps")
                pe.wait_ge(S("dx"), b + 1)
                product(pC, w["gate_w"], dx, "gate_ps")
                pe.wait_ge(S("t5"), b + 1)
                for n, name in enumerate(mixes):
                    bank = (pA, pB)[n % 2]
                    if n >= 2:
                        pe.wait_ge(S("mix_" + mixes[n - 2]), b + 1)
                    if n < 4:
                        product(bank, w["maa_w2"][:, n * P:(n + 1) * P], t5a, "m_" + name)
                    else:
                        product(bank, w["maa_w2e"], t5b, "m_" + name)
                    if n >= 1:
                        projection(pe, b, product, mixes[n - 1])
                projection(pe, b, product, "g")
                pe.wait_ge(S("mix_g"), b + 1)
                for v in range(HK):
                    n = b * HK + v
                    bank = (pA, pB)[v % 2]
                    if v >= 2:
                        pe.wait_ge(S("kv"), n - 1)
                    if v == 0:
                        pe.wait_ge(S("mix2_v"), b + 1)
                    for cut in halves():
                        ins = pe.matmul(bank[:, cut], w["Wv8"][:, v * P:(v + 1) * P], x5[:, cut], start=True, stop=True)
                    ins.then_inc(S("v_ps"), 1)
                    if v >= 2:
                        reduce(pe, b, v - 2)
                reduce(pe, b, HK - 2)
                reduce(pe, b, HK - 1)
                pe.wait_ge(S("yg"), b + 1)
                product(pA, w["mean8"], xa, "mu_ps")
                pe.wait_ge(S("sq"), b + 1)
                product(pB, w["mean8"], dx, "var_ps")
                pe.wait_ge(S("gn"), b + 1)
                product(pC, w["Wo"], xa, "o_ps")
                pe.wait_ge(S("o_sb"), b + 1)
                for t in range(TT):
                    ins = pe.transpose(pA[:, t * P:(t + 1) * P], xb[:, t * P:(t + 1) * P], G["ident"][:, :])
                ins.then_inc(S("tr"), 1)
                pe.wait_ge(S("x"), b + 1)

        @block.scalar
        def _(act):
            act.wait_ge(setup, 1)
            with act.Fori(0, B) as b:
                act.wait_ge(S("t5a_ps"), b + 1)
                act.activation(t5a[:, :], pA[:, :], ACT.Tanh)
                act.wait_ge(S("t5b_ps"), b + 1)
                act.activation(t5b[:, :], pB[0:32, :], ACT.Tanh).then_inc(S("t5"), 1)
                act.wait_ge(S("gate_ps"), b + 1)
                act.activation(gate[:, :], pC[:, :], ACT.Sigmoid, bias=w["gate_b"]).then_inc(S("gate"), 1)
                act.wait_ge(S("d1_ps"), b + 1)
                act.activation(td[:, :], pC[0:64, :], ACT.Tanh).then_inc(S("td"), 1)
                act.wait_ge(S("d2_ps"), b + 1)
                act.activation(dec[:, :], pC[:, :], ACT.Exp, bias=w["time_decay"]).then_inc(S("dec_e"), 1)
                act.wait_ge(S("dec_e"), b + 1)
                act.activation(dec[:, :], dec[:, :], ACT.Exp, scale=-1.0).then_inc(S("dec_sb"), 1)
                act.wait_ge(S("k_ps"), b + 1)
                act.copy(k[:, :], pD[:, :]).then_inc(S("k_sb"), 1)
                act.wait_ge(S("r_ps"), b + 1)
                act.copy(r[:, :], pC[:, :]).then_inc(S("r_sb"), 1)
                act.wait_ge(S("g_ps"), b + 1)
                act.activation(g[:, :], pD[:, :], ACT.Silu).then_inc(S("g_sb"), 1)
                act.wait_ge(S("yc"), b + 1)
                act.activation(dx[:, :], xb[:, :], ACT.Square).then_inc(S("sq"), 1)
                act.wait_ge(S("var_ps"), b + 1)
                act.activation(Ss[:, 0, :], pB[:, :], ACT.Sqrt, bias=eps[:, 0:1]).then_inc(S("gsd"), 1)
                act.wait_ge(S("o_ps"), b + 1)
                act.copy(xb[:, :], pC[:, :]).then_inc(S("o_sb"), 1)

        @block.vector
        def _(dve):
            with dve.Fori(0, B) as b:
                def step(name, ins):
                    ins.then_inc(S(name), 1)
                    dve.wait_ge(S(name), b + 1)

                cur, prev, nxt = (XNT[:, b, a:a + T] for a in (1, 0, 2))
                cw = w["conv_w"]
                step("c1", dve.tensor_scalar(dx[:, :], prev, cw[:, 0:1], None, ALU.mult))
                step("c2", dve.scalar_tensor_tensor(xa[:, :], cur, cw[:, 1:2], dx[:, :], ALU.mult, ALU.add))
                step("c3", dve.scalar_tensor_tensor(dx[:, :], nxt, cw[:, 2:3], xa[:, :], ALU.mult, ALU.add))
                step("dx", dve.tensor_tensor(dx[:, :], dx[:, :], cur, ALU.subtract))
                step("x5", dve.scalar_tensor_tensor(x5[:, :], dx[:, :], w["maa_x"], cur, ALU.mult, ALU.add))
                for n, name in enumerate(mixes):
                    dst = {"w": xa, "k": xb, "v": x5, "r": xb, "g": xa}[name]
                    bank = (pA, pB)[n % 2]
                    dve.wait_ge(S("m_" + name), b + 1)
                    if name == "r":
                        dve.wait_ge(S("k_ps"), b + 1)
                    if name == "g":
                        dve.wait_ge(S("d1_ps"), b + 1)
                    step("mix_" + name, dve.scalar_tensor_tensor(dst[:, :], bank[:, :], w["maa_" + name], dx[:, :],
                                                                 ALU.add, ALU.mult))
                    step("mix2_" + name, dve.tensor_tensor(dst[:, :], dst[:, :], cur, ALU.add))
                dve.wait_ge(S("k_sb"), b + 1)
                dve.wait_ge(S("r_sb"), b + 1)
                for v in range(HK):
                    n = b * HK + v
                    bank = (pA, pB)[v % 2]
                    dve.wait_ge(S("v_ps"), n + 1)
                    dve.tensor_tensor(kv[:, v % 2, :], bank[:, :], k[:, :], ALU.mult).then_inc(S("kv"), 1)
                    if v >= 2:
                        dve.wait_ge(S("ssum"), n - 1)
                    dve.wait_ge(S("kv"), n + 1)
                    dve.tensor_tensor_scan(Sf[:, v % 2, :], dec[:, :], kv[:, v % 2, :], 0.0, ALU.mult, ALU.add)
                    dve.tensor_tensor_scan(Sb[:, v % 2, T - 1::-1], kv[:, v % 2, ::-1], dec[:, ::-1], 0.0,
                                           ALU.add, ALU.mult).then_inc(S("bwd"), 1)
                dve.wait_ge(S("g_sb"), b + 1)
                dve.wait_ge(S("y_mm"), b * HK + HK)
                step("yg", dve.tensor_tensor(xa[:, :], pD[:, :], gate[:, :], ALU.mult))
                dve.wait_ge(S("mu_ps"), b + 1)
                step("yc", dve.tensor_tensor(xb[:, :], xa[:, :], pA[:, :], ALU.subtract))
                dve.wait_ge(S("gsd"), b + 1)
                step("grs", dve.reciprocal(Ss[:, 1, :], Ss[:, 0, :]))
                step("g1", dve.tensor_tensor(xa[:, :], xb[:, :], Ss[:, 1, :], ALU.mult))
                step("g2", dve.tensor_scalar(xb[:, :], xa[:, :], w["ln_w"], w["ln_b"], ALU.mult, ALU.add))
                step("gn", dve.tensor_tensor(xa[:, :], xb[:, :], g[:, :], ALU.mult))
                dve.wait_ge(S("tr"), b + 1)
                xv = X[:, bass.ds(b * TT, TT), :]
                dve.tensor_tensor(xv, xv, pA[:, :].rearrange("p (k d) -> p k d", k=TT), ALU.add).then_inc(S("x"), 1)
    ph.end()


def store_out(nc, G, out):
    ph = Phase(nc, "fin")
    stored = ph.sem("stored")
    with nc.Block() as block:
        @block.sync
        def _(sp):
            sp.dma_start(out.rearrange("(n p) d -> p n d", p=P), G["X"][:, :, :]).then_inc(stored, 16)
            sp.wait_ge(stored, 16)
    ph.end()


def pack(inputs):
    a = {k: np.asarray(v) for k, v in inputs.items()}
    cols, at = [[], [], []], {}

    def put(name, m, part=0):
        m = np.asarray(m)
        if m.shape[0] < P:
            m = np.concatenate([m, np.zeros((P - m.shape[0], m.shape[1]), m.dtype)], 0)
        at[name] = (part, sum(c.shape[1] for c in cols[part]), m.shape[1])
        cols[part].append(m)

    put("W0", a["L0_attn_W"])
    put("b0", a["L0_attn_bias"].reshape(P, 1))
    for layer in ("L0", "L3"):
        for w in ("W_r", "W_k", "W_v"):
            put(f"{layer}{w}", a[f"{layer}_ffn_{w}"].T, 2 if layer == "L3" else 0)
        for w in ("mu_r", "mu_k"):
            put(f"{layer}{w}", a[f"{layer}_ffn_{w}"].reshape(P, 1), 2 if layer == "L3" else 0)
    put("rpe", a["L1_attn_rpe_bias"][:, :256])
    put("slopes", np.asarray([[-(2.0 ** (-0.5 * (h + 1)))] for h in range(16)], np.float32))
    for m, name in enumerate("qkv"):
        put(f"L1{name}", a["L1_attn_qkv"][:, m].reshape(P, 1024))
    put("L1o", a["L1_attn_out_w"].reshape(8, P, P).transpose(1, 0, 2).reshape(P, 1024))
    for name in "qkvo":
        put(f"L2{name}", a[f"L2_attn_W{name}"], 1)
    put("gw1", a["L1_ffn_gate_w"])
    put("gb1", a["L1_ffn_gate_b"].reshape(8, 1))
    put("w1", a["L1_ffn_w1"].transpose(1, 0, 2).reshape(P, 4096))
    put("b1", a["L1_ffn_b1"].reshape(32, P).T)
    put("w2", a["L1_ffn_w2"].reshape(32, P, P).transpose(1, 0, 2).reshape(P, 4096))
    put("b2", a["L1_ffn_b2"])
    put("rw", a["L2_ffn_router_w"], 1)
    put("rb", a["L2_ffn_router_b"].reshape(8, 1), 1)
    put("x1", a["L2_ffn_w1"].transpose(1, 0, 2).reshape(P, 4096), 1)
    put("xb1", a["L2_ffn_b1"].reshape(32, P).T, 1)
    put("x2", a["L2_ffn_w2"].reshape(32, P, P).transpose(1, 0, 2).reshape(P, 4096), 1)
    put("xb2", a["L2_ffn_b2"].T, 1)
    put("ow1", a["L2_ffn_ow1"], 1)
    put("ob1", a["L2_ffn_ob1"].reshape(4, P).T, 1)
    put("ow2", a["L2_ffn_ow2"].reshape(4, P, P).transpose(1, 0, 2).reshape(P, 512), 1)
    put("Aconv_w", a["L3_attn_conv_w"].reshape(P, 3), 2)
    for name in ("maa_x", "maa_w", "maa_k", "maa_v", "maa_r", "maa_g", "time_decay", "ln_w", "ln_b", "gate_b"):
        put("A" + name, a["L3_attn_" + name].reshape(P, 1), 2)
    put("Amaa_w1", a["L3_attn_maa_w1"], 2)
    w2 = a["L3_attn_maa_w2"]
    put("Amaa_w2", np.concatenate([np.concatenate([w2[f] if g == f else np.zeros_like(w2[f]) for g in range(4)], 0)
                                   for f in range(4)], 1), 2)
    put("Amaa_w2e", w2[4], 2)
    for name in ("decay_w1", "decay_w2", "Wr", "Wk", "Wg", "Wo", "gate_w"):
        put("A" + name, a["L3_attn_" + name], 2)
    put("AWv8", np.repeat(a["L3_attn_Wv"].reshape(P, 16, 8).transpose(0, 2, 1), 8, axis=2).reshape(P, 1024), 2)
    put("Amean8", np.kron(np.eye(16), np.full((8, 8), 1 / 8)).astype(np.float32), 2)
    put("Apick", np.concatenate([np.kron(np.eye(16), np.ones((8, 1)) * (np.arange(8) == v)[None]) for v in range(8)],
                                1).astype(np.float32), 2)
    rows = np.stack([a["L1_ffn_ln_g"], a["L1_ffn_ln_b"], a["L2_ffn_ob2"]])
    return [np.ascontiguousarray(np.concatenate(c, 1)) for c in cols] + [np.ascontiguousarray(rows)], at


def build(nc, x, wts, rows, out, at, stages="0f1g23h"):
    with ExitStack() as ctx:
        def sb(name, shape, dt=F32):
            return ctx.enter_context(nc.sbuf_tensor(name, shape, dt))

        G = dict(X=sb("X", [P, NT, P]), XNT=sb("XNT", [P, B, TP]), XR=sb("XR", [P, NT, P]),
                 WA=sb("WA", [P, max(wts[0].shape[1], wts[2].shape[1])]), ident=sb("ident", [P, P]),
                 tri=sb("tri", [P, P]), ones=sb("ones", [P, P]), eps=sb("eps", [P, 1]), x_dram=x)
        G["in1"], G["in2"] = nc.alloc_semaphore("in1"), nc.alloc_semaphore("in2")
        inner = ExitStack()
        G["WB"] = inner.enter_context(nc.sbuf_tensor("WB", [P, wts[1].shape[1]], F32))

        def w(name, rows=P):
            part, lo, n = at[name]
            return (G["WA"], G["WB"], G["WA"])[part][0:rows, lo:lo + n]

        constants(nc, G, wts, at["rpe"][1])
        if "0" in stages:
            layernorm(nc, G, "n0")
            channel_mix(nc, G, "l0", w("L0W_r"), w("L0W_k"), w("L0W_v"), w("L0mu_r"), w("L0mu_k"), (w("W0"), w("b0")))

        layernorm(nc, G, "n1", lambda sp: sp.wait_ge(G["in1"], G["in1_n"]))
        tab1 = nc.dram_tensor("tab1", [16, P - 1 + T], F32).ap()
        qtail = nc.dram_tensor("qtail", [6, T], BF16).ap()
        ktail = nc.dram_tensor("ktail", [B * 16, 6, T], BF16).ap()
        tables(nc, G, w("rpe", 16), w("slopes", 16), tab1, qtail, ktail)
        if "f" in stages:
            moe_top2(nc, G, "f1", w("gw1"), w("gb1", 8), w("w1"), w("b1"), w("w2"), w("b2", 8), rows)
        if "1" in stages:
            attention(nc, G, "a1", 64, 16, w("L1q"), w("L1k"), w("L1v"), w("L1o"), tab1, 64 ** -0.5)

        layernorm(nc, G, "n2", lambda sp: sp.wait_ge(G["in2"], G["in2_n"]))
        if "g" in stages:
            buf = nc.dram_tensor("slots", [8 * 160 + N, P], F32).ap()
            ybuf = nc.dram_tensor("slot_out", [8 * 160 + 1, P], F32).ap()
            moe_capacity(nc, G, "f2", w("rw"), w("rb", 8), w("x1"), w("xb1"), w("x2"), w("xb2"), w("ow1"), w("ob1"),
                         w("ow2"), rows, buf, ybuf)
        if "2" in stages:
            parts = nc.dram_tensor("parts", [6, B * P, T], BF16).ap()
            with nc.sbuf_tensor("V9", [P, 4 * B, 4, TT, 9], F32) as V9:
                alibi_split(nc, G, w("L2q"), w("L2k"), w("L2v"), V9, parts, 8 ** -0.5)
                alibi_attention(nc, G, V9, parts, qtail, ktail)
                alibi_out(nc, G, w("L2o"))
        inner.close()

        in3 = nc.alloc_semaphore("in3")
        layernorm(nc, G, "n3", lambda sp: sp.wait_ge(in3, load_columns(sp, in3, G["WA"], wts[2])))
        if "3" in stages:
            names = ("conv_w maa_x maa_w maa_k maa_v maa_r maa_g time_decay ln_w ln_b gate_b maa_w1 maa_w2 decay_w1 decay_w2 "
                     "Wr Wk Wg Wo gate_w Wv8 mean8 pick").split()
            aw = {n: w("A" + n) for n in names}
            aw["maa_w2e"] = w("Amaa_w2e", 32)
            wkv(nc, G, "a3", aw)
        if "h" in stages:
            channel_mix(nc, G, "l3", w("L3W_r"), w("L3W_k"), w("L3W_v"), w("L3mu_r"), w("L3mu_k"))
        store_out(nc, G, out)


def kernel(**inputs):
    import concourse.bacc as bacc
    from concourse.bass_utils import run_bass_kernel_spmd as run

    nc = bacc.Bacc("TRN2", target_bir_lowering=False, num_devices=1)
    packed, at = pack(inputs)
    x = np.ascontiguousarray(np.asarray(inputs["L0_attn_x"]).reshape(N, P))
    arrays = {"in_x": x} | {f"in_w{i}": m for i, m in enumerate(packed)}
    args = {k: nc.dram_tensor(k, list(v.shape), F32, kind="ExternalInput").ap() for k, v in arrays.items()}
    out = nc.dram_tensor("out_x", [N, P], F32, kind="ExternalOutput").ap()
    build(nc, args["in_x"], [args["in_w0"], args["in_w1"], args["in_w2"]], args["in_w3"], out, at)
    result = run(nc, [arrays], core_ids=[0]).results[0]["out_x"]
    return result.reshape(B, T, P)
```

```python
import concourse.bass as bass
from concourse import mybir
from contextlib import ExitStack
import numpy as np

F32 = mybir.dt.float32
BF16 = mybir.dt.bfloat16
U32 = mybir.dt.uint32
I32 = mybir.dt.int32
ALU = mybir.AluOpType
ACT = mybir.ActivationFunctionType
AX = mybir.AxisListType

P = 128
B, T = 4, 1024
N = B * T
NT = N // P
TT = T // P
CH = 512
CT = CH // P
TP = T + 2
LN_EPS = 1e-5


class Phase:

    def __init__(self, nc, tag):
        self.nc, self.tag, self.ctx, self.sems = nc, tag, ExitStack(), []

    def sb(self, name, shape, dt=F32):
        return self.ctx.enter_context(self.nc.sbuf_tensor(f"{self.tag}_{name}", shape, dt))

    def ps(self, name, shape=(P, CH), dt=F32):
        return self.ctx.enter_context(self.nc.psum_tensor(f"{self.tag}_{name}", list(shape), dt))

    def sem(self, name):
        s = self.nc.alloc_semaphore(f"{self.tag}_{name}")
        self.sems.append(s)
        return s

    def end(self):
        self.nc.clear_and_free_semaphores(self.sems)
        self.nc.all_engine_barrier()
        self.ctx.close()


def load_columns(sp, sem, dst, src, lo=0, hi=None):
    hi = hi or src.shape[1]
    cuts = list(range(lo, hi, 2048)) + [hi]
    for a, z in zip(cuts, cuts[1:]):
        sp.dma_start(dst[:, a:z], src[:, a:z]).then_inc(sem, 16)
    return 16 * (len(cuts) - 1)


def constants(nc, G, wts, first):
    ph = Phase(nc, "init")
    loaded, made = ph.sem("loaded"), ph.sem("made")
    with nc.Block() as block:
        @block.sync
        def _(sp):
            sp.dma_start(G["X"][:, :, :], G["x_dram"].rearrange("(n p) d -> p n d", p=P)).then_inc(loaded, 16)
            n = 16 + load_columns(sp, loaded, G["WA"], wts[0], 0, first)
            G["in1_n"] = load_columns(sp, G["in1"], G["WA"], wts[0], first)
            G["in2_n"] = load_columns(sp, G["in2"], G["WB"], wts[1])
            sp.wait_ge(loaded, n)

        @block.gpsimd
        def _(pool):
            pool.memset(G["ident"][:, :], 0.0).then_inc(made, 1)
            pool.memset(G["tri"][:, :], 1.0).then_inc(made, 1)
            pool.memset(G["ones"][:, :], 1.0).then_inc(made, 1)
            pool.memset(G["XNT"][:, :, 0:1], 0.0)
            pool.memset(G["XNT"][:, :, TP - 1:TP], 0.0)
            pool.memset(G["eps"][:, :], LN_EPS)
            pool.wait_ge(made, 3)
            pool.affine_select(out=G["ident"][:, :], in_=G["ident"][:, :], compare_op=ALU.not_equal, fill=1.0,
                               base=0, pattern=[[-1, P]], channel_multiplier=1).then_inc(made, 1)
            pool.affine_select(out=G["tri"][:, :], in_=G["tri"][:, :], compare_op=ALU.is_ge, fill=0.0,
                               base=0, pattern=[[1, P]], channel_multiplier=-1).then_inc(made, 1)
    ph.end()


def layernorm(nc, G, tag, loads=None):
    ph = Phase(nc, tag)
    X, XNT = G["X"], G["XNT"]
    stats = ph.sb("stats", [P, NT, 6])
    mean = ph.sb("mean", [P, NT])
    half = ph.sb("half", [P, NT])
    sq = ph.sb("sq", [P, NT])
    m2 = ph.sb("m2", [P, NT])
    var = ph.sb("var", [P, NT])
    sd = ph.sb("sd", [P, NT])
    rstd = ph.sb("rstd", [P, NT])
    XR = G["XR"]
    pst = [ph.ps(f"t{i}") for i in range(2)]
    stats_done, mv_done, sd_done, rstd_done = (ph.sem(n) for n in ("stats", "mv", "sd", "rstd"))
    xn_done, tr_done, out_done = (ph.sem(n) for n in ("xn", "tr", "out"))
    with nc.Block() as block:
        if loads:
            @block.sync
            def _(sp):
                loads(sp)

        @block.vector
        def _(dve):
            with dve.Fori(0, NT // CT) as c:
                for k in range(CT):
                    ins = dve.bn_stats(stats[:, c * CT + k, :], X[:, c * CT + k, :])
                ins.then_inc(stats_done, 1)
            dve.wait_ge(stats_done, NT // CT)
            dve.tensor_tensor(mean[:, :], stats[:, :, 1], stats[:, :, 4], ALU.add)
            dve.tensor_tensor(half[:, :], stats[:, :, 1], stats[:, :, 4], ALU.subtract)
            dve.tensor_tensor(m2[:, :], stats[:, :, 2], stats[:, :, 5], ALU.add).then_inc(stats_done, 1)
            dve.wait_ge(stats_done, NT // CT + 1)
            dve.tensor_scalar(mean[:, :], mean[:, :], 0.5, None, ALU.mult)
            dve.tensor_tensor(sq[:, :], half[:, :], half[:, :], ALU.mult)
            dve.tensor_scalar(m2[:, :], m2[:, :], 4.0 / P, None, ALU.mult).then_inc(stats_done, 1)
            dve.wait_ge(stats_done, NT // CT + 2)
            dve.tensor_tensor(var[:, :], sq[:, :], m2[:, :], ALU.add).then_inc(mv_done, 1)
            dve.wait_ge(sd_done, 1)
            dve.reciprocal(rstd[:, :], sd[:, :]).then_inc(rstd_done, 1)
            dve.wait_ge(rstd_done, 1)
            with dve.Fori(0, B) as b:
                for h in range(2):
                    for k in range(CT):
                        n = b * TT + (h * CT + k)
                        ins = dve.tensor_scalar(XR[:, n, :], X[:, n, :], mean[:, bass.ds(n, 1)], rstd[:, bass.ds(n, 1)],
                                                ALU.subtract, ALU.mult)
                    ins.then_inc(xn_done, 1)

        @block.scalar
        def _(act):
            act.wait_ge(mv_done, 1)
            act.activation(sd[:, :], var[:, :], ACT.Sqrt, bias=G["eps"][:, 0:1], scale=0.25).then_inc(sd_done, 1)
            with act.Fori(0, B) as b:
                for h in range(2):
                    act.wait_ge(tr_done, b * 2 + h + 1)
                    act.copy(XNT[:, b, 1 + h * CH:1 + (h + 1) * CH], pst[h][:, :]).then_inc(out_done, 1)

        @block.tensor
        def _(pe):
            for c in range(NT // CT):
                pe.wait_ge(xn_done, c + 1)
                if c >= 2:
                    pe.wait_ge(out_done, c - 1)
                for k in range(CT):
                    ins = pe.transpose(pst[c % 2][:, k * P:(k + 1) * P], XR[:, c * CT + k, :], G["ident"][:, :])
                ins.then_inc(tr_done, 1)
    ph.end()


def channel_mix(nc, G, tag, wr, wk, wv, mu_r, mu_k, attn=None):
    ph = Phase(nc, tag)
    X, XNT = G["X"], G["XNT"]
    dx = ph.sb("dx", [P, 2, CH])
    xr = ph.sb("xr", [P, 2, CH])
    xk = ph.sb("xk", [P, 2, CH])
    sig = ph.sb("sig", [P, 2, CH])
    kr = ph.sb("kr", [P, 2, CH])
    k2 = ph.sb("k2", [P, 2, CH])
    prod = ph.sb("prod", [P, 2, CH])
    delta = ph.sb("delta", [P, 2, CH])
    wc = ph.sb("wc", [P, P])
    bc = ph.sb("bc", [P, 1])
    psr = [ph.ps(f"r{i}") for i in range(2)]
    psk = [ph.ps(f"k{i}") for i in range(2)]
    psa = [ph.ps(f"a{i}") for i in range(2)]
    names = ("dx", "mixed", "rk", "relu", "k2", "v", "prod", "delta", "tr", "x", "wcp", "wc")
    dx_done, mixed, rk_done, relu_done, k2_done, v_done, prod_done, delta_done, tr_done, x_done, wc_psum, wc_done = (
        ph.sem(n) for n in names)
    with nc.Block() as block:
        @block.vector
        def _(dve):
            if attn:
                dve.wait_ge(wc_psum, 1)
                dve.tensor_copy(wc[:, :], psa[0][:, 0:P]).then_inc(wc_done, 1)
                dve.tensor_copy(bc[:, :], psa[0][:, P:P + 1]).then_inc(wc_done, 1)
                dve.wait_ge(wc_done, 2)
            with dve.Fori(0, B) as b:
                for h in range(2):
                    c = b * 2 + h
                    cur = XNT[:, b, 1 + h * CH:1 + (h + 1) * CH]
                    prev = XNT[:, b, h * CH:(h + 1) * CH]
                    dve.tensor_tensor(dx[:, h, :], cur, prev, ALU.subtract).then_inc(dx_done, 1)
                    dve.wait_ge(dx_done, c + 1)
                    dve.scalar_tensor_tensor(xr[:, h, :], dx[:, h, :], mu_r, prev, ALU.mult, ALU.add)
                    dve.scalar_tensor_tensor(xk[:, h, :], dx[:, h, :], mu_k, prev, ALU.mult,
                                             ALU.add).then_inc(mixed, 1)
                for h in range(2):
                    c = b * 2 + h
                    dve.wait_ge(v_done, c + 1)
                    if attn:
                        dve.tensor_tensor(prod[:, h, :], sig[:, h, :], psr[h][:, :], ALU.mult).then_inc(prod_done, 1)
                        dve.wait_ge(prod_done, c + 1)
                        dve.scalar_tensor_tensor(delta[:, h, :], psa[h][:, :], bc[:, 0:1], prod[:, h, :], ALU.add,
                                                 ALU.add).then_inc(delta_done, 1)
                    else:
                        dve.tensor_tensor(delta[:, h, :], sig[:, h, :], psr[h][:, :], ALU.mult).then_inc(delta_done, 1)
                for h in range(2):
                    c = b * 2 + h
                    dve.wait_ge(tr_done, c + 1)
                    xv = X[:, bass.ds(b * TT + h * CT, CT), :]
                    dve.tensor_tensor(xv, xv, psk[h][:, :].rearrange("p (k d) -> p k d", k=CT),
                                      ALU.add).then_inc(x_done, 1)

        @block.scalar
        def _(act):
            with act.Fori(0, B) as b:
                for h in range(2):
                    c = b * 2 + h
                    act.wait_ge(rk_done, c + 1)
                    act.activation(sig[:, h, :], psr[h][:, :], ACT.Sigmoid)
                    act.activation(kr[:, h, :], psk[h][:, :], ACT.Relu).then_inc(relu_done, 1)
                    act.wait_ge(relu_done, c + 1)
                    act.activation(k2[:, h, :], kr[:, h, :], ACT.Square).then_inc(k2_done, 1)

        @block.tensor
        def _(pe):
            if attn:
                pe.matmul(psa[0][:, 0:P], attn[0], G["tri"][:, :], start=True, stop=True)
                pe.matmul(psa[0][:, P:P + 1], G["tri"][:, :], attn[1], start=True, stop=True).then_inc(wc_psum, 1)
                pe.wait_ge(wc_done, 2)
            pe.sem_inc(x_done, 2)
            with pe.Fori(0, B) as b:
                for h in range(2):
                    c = b * 2 + h
                    pe.wait_ge(mixed, c + 1)
                    pe.wait_ge(x_done, c + 1)
                    pe.matmul(psr[h][:, :], wr, xr[:, h, :], start=True, stop=True)
                    ins = pe.matmul(psk[h][:, :], wk, xk[:, h, :], start=True, stop=True)
                    ins.then_inc(rk_done, 1)
                    if attn:
                        pe.matmul(psa[h][:, :], wc[:, :], XNT[:, b, 1 + h * CH:1 + (h + 1) * CH], start=True, stop=True)
                for h in range(2):
                    c = b * 2 + h
                    pe.wait_ge(k2_done, c + 1)
                    pe.matmul(psr[h][:, :], wv, k2[:, h, :], start=True, stop=True).then_inc(v_done, 1)
                for h in range(2):
                    c = b * 2 + h
                    pe.wait_ge(delta_done, c + 1)
                    for k in range(CT):
                        ins = pe.transpose(psk[h][:, k * P:(k + 1) * P], delta[:, h, k * P:(k + 1) * P], G["ident"][:, :])
                    ins.then_inc(tr_done, 1)
    ph.end()


def tables(nc, G, rpe, slopes, tab1, qstack, ktail):
    ph = Phase(nc, "tab")
    K = P - 1
    H = 16
    S = 256
    t1 = ph.sb("t1", [H, K + T])
    t2, rest = ph.sb("t2", [H, T]), ph.sb("rest", [H, T])
    tail = ph.sb("tail", [H, 6, T], BF16)
    dist = ph.sb("dist", [H, T])
    zero = ph.sb("zero", [H, T])
    qtail = ph.sb("qtail", [H, 6, T], BF16)
    made, scanned, filled, cut, stored = (ph.sem(n) for n in ("made", "scanned", "filled", "cut", "stored"))
    with nc.Block() as block:
        @block.gpsimd
        def _(pool):
            pool.iota(dist[:, :], [[-1, T]], base=T // 2, channel_multiplier=0, allow_small_or_imprecise_dtypes=True)
            pool.memset(zero[:, :], 0.0)
            pool.memset(qtail[:, 0:3, :], 0.0)
            pool.memset(qtail[:, 3:6, :], 1.0)
            pool.memset(tail[:, 0:3, :], 1.0)
            pool.memset(t1[:, 0:K], -30000.0).then_inc(made, 1)

        @block.vector
        def _(dve):
            dve.wait_ge(made, 1)
            dve.tensor_tensor_scan(t1[:, K:K + S], rpe, zero[:, 0:S], 0.0, ALU.add, ALU.add).then_inc(scanned, 1)
            dve.tensor_scalar(t2[:, :], dist[:, :], slopes, None, ALU.mult).then_inc(cut, 1)
            dve.wait_ge(scanned, 1)
            dve.tensor_scalar(t1[:, K + S:K + T], zero[:, S:T], t1[:, K + S - 1:K + S], None,
                              ALU.add).then_inc(filled, 1)
            dve.wait_ge(cut, 1)
            dve.tensor_copy(tail[:, 3, :], t2[:, :]).then_inc(cut, 1)
            dve.wait_ge(cut, 2)
            dve.tensor_tensor(rest[:, :], t2[:, :], tail[:, 3, :], ALU.subtract).then_inc(cut, 1)
            dve.wait_ge(cut, 3)
            dve.tensor_copy(tail[:, 4, :], rest[:, :]).then_inc(cut, 1)
            dve.wait_ge(cut, 4)
            dve.tensor_tensor(tail[:, 5, :], rest[:, :], tail[:, 4, :], ALU.subtract).then_inc(filled, 1)

        @block.sync
        def _(sp):
            sp.wait_ge(filled, 2)
            sp.dma_start(tab1, t1[:, :]).then_inc(stored, 16)
            for b in range(B):
                sp.dma_start(qstack[b * H:(b + 1) * H, 72:78, :], qtail[:, :, :]).then_inc(stored, 16)
                sp.dma_start(ktail[b * H:(b + 1) * H, :, :], tail[:, :, :]).then_inc(stored, 16)
            sp.wait_ge(stored, 16 * (1 + 2 * B))
    ph.end()


def attention(nc, G, wq_all, wk_all, wv_all, wo_all, tab, scale, scratch):
    ph = Phase(nc, "a1")
    X, XNT = G["X"], G["XNT"]
    HG = 2
    D = P // HG
    NG = wq_all.shape[1] // P
    IT = NG * B
    U = HG * TT
    K = P - 1
    units = [(u, i) for u in range(HG) for i in range(TT)]
    chunks = [(n, c) for n, (u, i) in enumerate(units) for c in range(i // CT + 1)]
    R = len(chunks)
    last = {n: k for k, (n, c) in enumerate(chunks)}
    joined = [n for n, (u, i) in enumerate(units) if i >= CT]
    NB = 3
    wq, wk, wv, wo = ph.sb("wq", [P, P]), ph.sb("wk", [P, P]), ph.sb("wv", [P, P]), ph.sb("wo", [P, P])
    tb = ph.sb("tb", [P, HG, T])
    xb = ph.sb("xb", [P, T])
    Q = [ph.sb(f"Q{s}", [P, T]) for s in range(2)]
    Kt = ph.sb("Kt", [P, T])
    Kh = [ph.sb(f"K{u}", [P, T]) for u in range(HG)]
    V = [ph.sb(f"V{s}", [P, TT, P]) for s in range(2)]
    PT = ph.sb("PT", [P, 2, T])
    mU = [ph.sb(f"mU{s}", [P, T]) for s in range(2)]
    NPB = 4
    Pb = G["XR"][:, :, :].rearrange("p (s k) d -> p s (k d)", s=NPB)
    Sb = scratch[:, 0:2 * T].rearrange("p (s t) -> p s t", s=2)
    nmax, half_max = ph.sb("nmax", [P, U]), ph.sb("halfmax", [P, 2, U])
    rsum, rinv = ph.sb("rsum", [P, U]), ph.sb("rinv", [P, U])
    pS = [ph.ps(f"S{i}") for i in range(NB)]
    pT = [ph.ps(f"T{i}") for i in range(2)]
    pO = [ph.ps(f"O{i}") for i in range(2)]
    pP = ph.ps("P")
    zeroed, x_ok, wo_ok, k0_ok, k1_ok, passed = (ph.sem(n) for n in ("zeroed", "xok", "wook", "k0ok", "k1ok", "passed"))
    k_ok = (k0_ok, k1_ok)
    tb_in, tb_ok = [ph.sem(f"tbin{u}") for u in range(HG)], [ph.sem(f"tbok{u}") for u in range(HG)]
    q_ps, k_ps, v_ps, q_sb, k_sb, v_sb = (ph.sem(n) for n in ("qps", "kps", "vps", "qsb", "ksb", "vsb"))
    s_ps, s_sb, m_ok, p_sb, t_ps, t_sb_a, t_sb_d = (
        ph.sem(n) for n in ("sps", "ssb", "mok", "psb", "tps", "tsba", "tsbd"))
    pv_ps, o_sb, y_ps, x_sb, r_inv, n_sb = (ph.sem(n) for n in ("pvps", "osb", "yps", "xsb", "rinvs", "nsb"))
    passed_dve = ph.sem("passeddve")
    on_act = [n % 3 != 2 for n, c in chunks]
    acts = [k for k in range(R) if on_act[k]]
    dves = [k for k in range(R) if not on_act[k]]

    OUT = {1: 0, 2: 1}
    EARLY = {6: 1, 7: 2, 14: 4}
    LATE = {3: 0, 8: 3, 15: 5}
    TAKE_OUT = {n + 1: j for n, j in OUT.items()}
    TAKE = EARLY | {n + 1: j for n, j in LATE.items()}

    def copied(k):
        return (t_sb_a, len(acts), acts.index(k) + 1) if on_act[k] else (t_sb_d, len(dves), dves.index(k) + 1)

    def length(i):
        return (i + 1) * P

    def span(n, c):
        return c * CH, min((c + 1) * CH, length(units[n][1]))

    def place(it, n):
        return it + n // U, n % U

    def loops(eng, body):
        with eng.Fori(0, NG) as g:
            with eng.Fori(0, B // 2) as h:
                body(g * B + h * 2, 0, 3 - h * 2)
                body(g * B + h * 2 + 1, 1, h * 2)

    with nc.Block() as block:
        @block.sync
        def _(sp):
            def load(g, u):
                src = bass.AP(tab.tensor, (g * HG + u) * (K + T), [[1, P], [1, T]])
                sp.dma_start(tb[:, u, :], src).then_inc(tb_in[u], 16)

            for u in range(HG):
                load(0, u)
            for u in range(HG):
                sp.wait_ge(tb_in[u], 16)
                sp.sem_inc(tb_ok[u], B)
            with sp.Fori(0, NG - 1) as g:
                for u in range(HG):
                    sp.wait_ge(s_sb, NB + (g * B + B - 1) * R + R // HG * (u + 1))
                    load(g + 1, u)
                for u in range(HG):
                    sp.wait_ge(tb_in[u], g * 16 + 32)
                    sp.sem_inc(tb_ok[u], B)
            sp.sem_inc(tb_ok[0], B)

        @block.gpsimd
        def _(pool):
            def weights(g):
                for w, w_all in ((wq, wq_all), (wk, wk_all), (wv, wv_all)):
                    pool.tensor_copy(w[:, :], w_all[:, bass.ds(g * P, P)])

            def sequence(b):
                pool.tensor_copy(xb[:, :], XNT[:, b, 1:1 + T]).then_inc(x_ok, 1)

            def keys(p):
                for u in range(HG):
                    pool.wait_ge(k_sb, 2 * p + 2)
                    pool.wait_ge(s_ps, p * R + R // HG * (u + 1))
                    pool.sem_inc(passed, 1)
                    pool.tensor_copy(Kh[u][u * D:(u + 1) * D, :], Kt[u * D:(u + 1) * D, :]).then_inc(k_ok[u], 1)
                    pool.wait_ge(k_ok[u], p + 1)

            def group(g, end):
                for b in range(1, B + 1):
                    p = g * B + b
                    pool.wait_ge(v_ps, p * 2)
                    pool.sem_inc(passed, 1)
                    if b == B and not end:
                        weights(g + 1)
                    sequence(b % B)
                    if b == 1:
                        pool.wait_ge(y_ps, (g * B + 1) * 2)
                        pool.sem_inc(passed, 1)
                        pool.tensor_copy(wo[:, :], wo_all[:, bass.ds(g * P, P)]).then_inc(wo_ok, B)
                    keys(p)

            for u in range(HG):
                pool.memset(Kh[u][:, :], 0.0)
            pool.memset(wo[:, :], 0.0)
            pool.memset(mU[1][:, :], 0.0).then_inc(zeroed, 1)
            pool.wait_ge(zeroed, 1)
            pool.sem_inc(wo_ok, 1)
            weights(0)
            sequence(0)
            keys(0)
            with pool.Fori(0, NG - 1) as g:
                group(g, False)
            group(NG - 1, True)

        @block.tensor
        def _(pe):
            def project(p, s, job):
                kind, half = divmod(job, 2)
                x = xb[:, half * CH:(half + 1) * CH]
                if kind < 2:
                    if kind == 0 and half == 0:
                        pe.wait_ge(x_ok, p + 1)
                        pe.wait_ge(x_sb, p * 2 + 2)
                    else:
                        pe.wait_ge(k_sb if job == 3 else q_sb, 2 * p + (1 if half else 2))
                    pe.matmul(pP[:, :], (wq, wk)[kind][:, :], x, start=True, stop=True)\
                      .then_inc((q_ps, k_ps)[kind], 1)
                else:
                    pe.wait_ge(v_sb if half else k_sb, 2 * p + (1 if half else 2))
                    for t in range(CT):
                        ins = pe.matmul(pP[:, t * P:(t + 1) * P], x[:, t * P:(t + 1) * P], wv[:, :], start=True, stop=True)
                    ins.then_inc(v_ps, 1)

            def output(it, s, j):
                if j == 0:
                    pe.wait_ge(v_sb, it * 2 + 2)
                    pe.wait_ge(wo_ok, it + 1)
                    pe.wait_ge(o_sb, it * 2 + 2)
                else:
                    pe.wait_ge(x_sb, it * 2 + j + 2)
                for t in range(CT):
                    ins = pe.matmul(pP[:, t * P:(t + 1) * P], mU[1 - s][:, (j * CT + t) * P:(j * CT + t + 1) * P], wo[:, :],
                                    start=True, stop=True)
                ins.then_inc(y_ps, 1)

            def scores(it, n, s):
                at, n0 = place(it, n)
                s = (s + n // U) % 2
                u, i = units[n0]
                if n0 == 0:
                    pe.wait_ge(q_sb, at * 2 + 2)
                if i == 0:
                    pe.wait_ge(k_ok[u], at + 1)
                for k, (m, c) in enumerate(chunks):
                    if m == n0:
                        lo, hi = span(m, c)
                        pe.wait_ge(s_sb, at * R + k + 1)
                        pe.matmul(pS[k % NB][:, 0:hi - lo], Q[s][:, i * P:(i + 1) * P], Kh[u][:, lo:hi],
                                  start=True, stop=True).then_inc(s_ps, 1)

            def transposes(it, n):
                pe.wait_ge(n_sb, it * U + n + 1)
                for k, (m, c) in enumerate(chunks):
                    if m == n:
                        sem, per, nth = copied((k - 2) % R)
                        pe.wait_ge(sem, it * per + nth + (per if k >= 2 else 0))
                        lo, hi = span(n, c)
                        for j in range(lo // P, hi // P):
                            ins = pe.transpose(pT[k % 2][:, j * P - lo:(j + 1) * P - lo], Pb[:, n % NPB, j * P:(j + 1) * P],
                                               G["ident"][:, :])
                        ins.then_inc(t_ps, 1)

            def values(it, n, s):
                u, i = units[n]
                sem, per, nth = copied(last[n])
                pe.wait_ge(sem, it * per + nth + per)
                if n == 0:
                    pe.wait_ge(v_sb, it * 2 + 2)
                if n in (0, CT):
                    pe.wait_ge(o_sb, it * 2 + n // CT + 1)
                for j in range(i + 1):
                    ins = pe.matmul(pO[i // CT][u * D:(u + 1) * D, i % CT * P:(i % CT + 1) * P],
                                    V[s][:, j, u * D:(u + 1) * D], PT[:, n % 2, j * P:(j + 1) * P],
                                    start=(j == 0), stop=(j == i))
                ins.then_inc(pv_ps, 1)


            def body(it, s, b_before):
                for n in range(U):
                    scores(it, n + 2, s)
                    if n in EARLY:
                        project(it + 1, 1 - s, EARLY[n])
                    transposes(it, n)
                    if n >= 1:
                        values(it, n - 1, s)
                    if n in OUT:
                        output(it, s, OUT[n])
                    if n in LATE:
                        project(it + 1, 1 - s, LATE[n])
                values(it, U - 1, s)

            pe.sem_inc(s_ps, R)
            pe.sem_inc(t_ps, R)
            pe.wait_ge(zeroed, 1)
            for job in range(6):
                project(0, 0, job)
            for n in range(2):
                scores(0, n, 0)
            loops(pe, body)
            for j in range(2):
                output(IT, 0, j)

        @block.scalar
        def _(act):
            def project_v(p, s, half):
                act.wait_ge(v_ps, 2 * p + half + 1)
                act.copy(V[s][:, half * CT:(half + 1) * CT, :], pP[:, :].rearrange("p (k d) -> p k d", k=CT))\
                   .then_inc(v_sb, 1)

            def project_k(p, half):
                act.wait_ge(k_ps, 2 * p + half + 1)
                act.copy(Kt[:, half * CH:(half + 1) * CH], pP[:, :]).then_inc(k_sb, 1)

            def exponentials(it, n):
                at, n0 = place(it, n)
                u, i = units[n0]
                if i < CT:
                    act.wait_ge(s_sb, NB + at * R + last[n0] + 1)
                else:
                    act.wait_ge(m_ok, at * len(joined) + joined.index(n0) + 1)
                act.wait_ge(t_ps, at * R + last[(n0 - NPB) % U] + 1 + (R if n0 >= NPB else 0))
                act.activation(Pb[:, n0 % NPB, 0:length(i)], Sb[:, n0 % 2, 0:length(i)], ACT.Exp,
                               bias=nmax[:, n0:n0 + 1], scale=-1.0, accum_out=rsum[:, n0:n0 + 1]).then_inc(p_sb, 1)

            def copies(it, n):
                for k, (m, c) in enumerate(chunks):
                    if m == n and on_act[k]:
                        lo, hi = span(n, c)
                        act.wait_ge(t_ps, it * R + R + k + 1)
                        act.copy(PT[:, n % 2, lo:hi], pT[k % 2][:, 0:hi - lo]).then_inc(t_sb_a, 1)

            def empty(it, s, c):
                act.wait_ge(pv_ps, it * U + U - CT + CT * c)
                act.copy(mU[s][:, c * CH:(c + 1) * CH], pO[c][:, :]).then_inc(o_sb, 1)

            def body(it, s, b_before):
                for n in range(U):
                    if TAKE.get(n) in (2, 3):
                        project_k(it + 1, TAKE[n] - 2)
                    if TAKE.get(n) in (4, 5):
                        project_v(it + 1, 1 - s, TAKE[n] - 4)
                    copies(it, n)
                    exponentials(it, n + 2)
                    if n == U - CT + 1:
                        empty(it, s, 0)
                project_v(it + 1, 1 - s, 1)
                empty(it, s, 1)

            act.sem_inc(p_sb, 2)
            act.sem_inc(t_sb_a, len(acts))
            act.sem_inc(o_sb, 2)
            act.wait_ge(zeroed, 1)
            for half in range(2):
                project_k(0, half)
            for half in range(2):
                project_v(0, 0, half)
            for n in range(2):
                exponentials(0, n)
            loops(act, body)

        @block.vector
        def _(dve):
            def project_q(p, s, half):
                dve.wait_ge(q_ps, 2 * p + half + 1)
                dve.tensor_scalar(Q[s][:, half * CH:(half + 1) * CH], pP[:, :], scale, None, ALU.mult).then_inc(q_sb, 1)

            def bias(it, n):
                at, n0 = place(it, n)
                u, i = units[n0]
                L = length(i)
                for k, (m, c) in enumerate(chunks):
                    if m != n0:
                        continue
                    if i == 0:
                        dve.wait_ge(tb_ok[u], at + 1)
                    if c == 0:
                        dve.wait_ge(p_sb, at * U + n0 + 1)
                    dve.wait_ge(s_ps, at * R + R + k + 1)
                    dve.sem_inc(passed_dve, 1)
                    lo, hi = span(n0, c)
                    peak = nmax[:, n0:n0 + 1] if i < CT else half_max[:, c, n0:n0 + 1]
                    first, end = L - 1 - lo, L - hi - 1
                    dve.tensor_tensor_reduce(out=Sb[:, n0 % 2, lo:hi], in0=pS[k % NB][:, 0:hi - lo],
                                             in1=tb[:, u, first:(end if end >= 0 else None):-1], scale=-1.0,
                                             scalar=3.0e38, op0=ALU.add, op1=ALU.min, accum_out=peak).then_inc(s_sb, 1)
                if i >= CT:
                    dve.wait_ge(s_sb, NB + at * R + last[n0] + 1)
                    dve.tensor_tensor(nmax[:, n0:n0 + 1], half_max[:, 0, n0:n0 + 1], half_max[:, 1, n0:n0 + 1],
                                      ALU.min).then_inc(m_ok, 1)

            def copies(it, n):
                for k, (m, c) in enumerate(chunks):
                    if m == n and not on_act[k]:
                        lo, hi = span(n, c)
                        dve.wait_ge(t_ps, it * R + R + k + 1)
                        dve.tensor_copy(PT[:, n % 2, lo:hi], pT[k % 2][:, 0:hi - lo]).then_inc(t_sb_d, 1)

            def normalise(it, n):
                at, n0 = place(it, n)
                x = Pb[:, n0 % NPB, 0:length(units[n0][1])]
                dve.wait_ge(p_sb, at * U + n0 + 3)
                dve.reciprocal(rinv[:, n0:n0 + 1], rsum[:, n0:n0 + 1]).then_inc(r_inv, 1)
                dve.wait_ge(r_inv, at * U + n0 + 1)
                dve.tensor_scalar(x, x, rinv[:, n0:n0 + 1], None, ALU.mult).then_inc(n_sb, 1)

            def add(it, b, j):
                dve.wait_ge(y_ps, it * 2 + j + 1)
                dve.sem_inc(passed_dve, 1)
                i = b * TT + j * CT
                xv = X[:, i:i + CT, :] if isinstance(b, int) else X[:, bass.ds(i, CT), :]
                dve.tensor_tensor(xv, xv, pP[:, :].rearrange("p (k d) -> p k d", k=CT), ALU.add).then_inc(x_sb, 1)

            def body(it, s, b_before):
                for n in range(U):
                    if n in TAKE_OUT:
                        add(it, b_before, TAKE_OUT[n])
                    if TAKE.get(n) in (0, 1):
                        project_q(it + 1, 1 - s, TAKE[n])
                    bias(it, n + 2)
                    normalise(it, n + 1)
                    copies(it, n)

            dve.sem_inc(s_sb, NB)
            dve.sem_inc(t_sb_d, len(dves))
            dve.sem_inc(x_sb, 2)
            dve.wait_ge(zeroed, 1)
            for half in range(2):
                project_q(0, 0, half)
            for n in range(2):
                bias(0, n)
            normalise(0, 0)
            loops(dve, body)
            for j in range(2):
                add(IT, B - 1, j)
    ph.end()


def alibi_split(nc, G, wq, wk, wv, V9, qstack, kparts, scale):
    ph = Phase(nc, "a2s")
    XNT = G["XNT"]
    QF, KF, RQ, RK, vT = (ph.sb(n, [P, T]) for n in ("QF", "KF", "RQ", "RK", "vT"))
    parts = ph.sb("parts", [P, 2, 3, T], BF16)
    pQ, pK, pV, pW = (ph.ps(n, (P, T)) for n in ("Q", "K", "V", "W"))
    q_ps, k_ps, v_ps, f_sb, k_sb, v_sb, w_ps, w_sb = (
        ph.sem(n) for n in ("qps", "kps", "vps", "fsb", "ksb", "vsb", "wps", "wsb"))
    high, rest, stored, ones_set, passed = (ph.sem(n) for n in ("high", "rest", "stored", "onesset", "passed"))
    HU = V9.shape[2]
    STORES = 16 * 12
    QR, KR = qstack.shape[1], kparts.shape[1]

    with nc.Block() as block:
        @block.tensor
        def _(pe):
            with pe.Fori(0, B) as b:
                for ps, w, done in ((pQ, wq, q_ps), (pK, wk, k_ps), (pV, wv, v_ps)):
                    if ps is pQ:
                        pe.wait_ge(rest, b * 6 + 6)
                    for half in range(2):
                        ins = pe.matmul(ps[:, half * CH:(half + 1) * CH], w,
                                        XNT[:, b, 1 + half * CH:1 + (half + 1) * CH], start=True, stop=True)
                    ins.then_inc(done, 1)
                pe.wait_ge(v_sb, b + 1)
                pe.wait_ge(w_sb, b + 1)
                for j in range(TT):
                    ins = pe.transpose(pW[:, j * P:(j + 1) * P], vT[:, j * P:(j + 1) * P], G["ident"][:, :])
                ins.then_inc(w_ps, 1)

        @block.scalar
        def _(act):
            with act.Fori(0, B) as b:
                act.wait_ge(q_ps, b + 1)
                act.activation(QF[:, :], pQ[:, :], ACT.Copy, scale=scale).then_inc(f_sb, 1)
                act.wait_ge(k_ps, b + 1)
                act.copy(KF[:, :], pK[:, :]).then_inc(f_sb, 1)
                act.wait_ge(stored, (b + 1) * STORES)
                act.wait_ge(f_sb, b * 2 + 1)
                act.copy(parts[:, 0, 0, :], QF[:, :]).then_inc(high, 1)
                act.wait_ge(f_sb, b * 2 + 2)
                act.copy(parts[:, 1, 0, :], KF[:, :]).then_inc(high, 1)
                act.wait_ge(v_ps, b + 1)
                act.copy(vT[:, :], pV[:, :]).then_inc(v_sb, 1)

        @block.vector
        def _(dve):
            dve.sem_inc(rest, 6)
            dve.sem_inc(w_sb, 1)
            with dve.Fori(0, B) as b:
                for s, F, R in ((0, QF, RQ), (1, KF, RK)):
                    dve.wait_ge(high, b * 2 + s + 1)
                    dve.tensor_tensor(R[:, :], F[:, :], parts[:, s, 0, :], ALU.subtract).then_inc(rest, 1)
                    dve.wait_ge(rest, b * 6 + s * 3 + 7)
                    dve.tensor_copy(parts[:, s, 1, :], R[:, :]).then_inc(rest, 1)
                    dve.wait_ge(rest, b * 6 + s * 3 + 8)
                    dve.tensor_tensor(parts[:, s, 2, :], R[:, :], parts[:, s, 1, :], ALU.subtract).then_inc(rest, 1)
                dve.wait_ge(w_ps, b + 1)
                for h in range(2):
                    for g in range(4):
                        src = pW[:, h * CH:(h + 1) * CH].rearrange("p (t g u d) -> p g u t d", t=CT, g=4, u=HU)
                        ins = dve.tensor_copy(V9[:, bass.ds(b * 4 + g, 1), :, h * CT:(h + 1) * CT, 0:8]
                                              .rearrange("p o u t d -> p (o u) t d"), src[:, g])
                ins.then_inc(w_sb, 1)

        @block.gpsimd
        def _(pool):
            pool.memset(V9[:, :, :, :, 8:9].rearrange("p i u t d -> p (i u t) d"), 1.0).then_inc(ones_set, 1)
            pool.wait_ge(ones_set, 1)

        @block.sync
        def _(sp):
            sp.sem_inc(stored, STORES)
            with sp.Fori(0, B) as b:
                sp.wait_ge(rest, b * 6 + 12)
                for a in range(3):
                    for c in range(3):
                        dst = bass.AP(qstack.tensor, (b * 16 * QR + a * 24 + c * 8) * T, [[QR * T, 16], [T, 8], [1, T]])
                        sp.dma_start(dst, parts[:, 0, a, :]).then_inc(stored, 16)
                    dst = bass.AP(kparts.tensor, (b * 16 * KR + a * 8) * T, [[KR * T, 16], [T, 8], [1, T]])
                    sp.dma_start(dst, parts[:, 1, a, :]).then_inc(stored, 16)
            sp.wait_ge(stored, (B + 1) * STORES)
    ph.end()


def alibi_attention(nc, G, V9, qstack, kparts, ktail):
    ph = Phase(nc, "a2")
    HU = V9.shape[2]
    IT = V9.shape[1]
    MR = 72
    mix = G["XR"][:, :, :].rearrange("p a b -> p (a b)").rearrange("p (i t c) -> p i t c", i=IT, t=TT)
    QS = [ph.sb(f"QS{u}", [P, T], BF16) for u in range(HU)]
    KS = [ph.sb(f"KS{u}", [P, T], BF16) for u in range(HU)]
    identb, maskq, maskk = (ph.sb(n, [P, P], BF16) for n in ("identb", "maskq", "maskk"))
    Vg = ph.sb("Vg", [P, HU, TT, 32])
    NP = 4
    PT = ph.sb("PT", [P, NP, CH])
    mx = ph.sb("mx", [P, 2, 12])
    minus, res = ph.sb("minus", [TT, P]), ph.sb("res", [TT, P])
    mrow = ph.sb("mrow", [TT, 2, 3, P], BF16)
    OT = ph.sb("OT", [P, T])
    rinv = ph.sb("rinv", [P, 2, CT, HU])
    pS = [ph.ps(f"S{i}") for i in range(2)]
    pE = [ph.ps(f"E{i}") for i in range(2)]
    pO = [ph.ps(f"O{i}") for i in range(2)]
    pX = [ph.ps(f"X{i}") for i in range(2)]
    sunits = [(i, 0) for i in (3, 2, 1, 0, 4, 5, 6, 7)] + [(i, 1) for i in (7, 6, 5, 4)]
    eunits = [(c, j) for c in range(2) for j in range((c + 1) * CT)]
    U = len(sunits)
    HELD = 3
    zeroed, consts = ph.sem("zeroed"), ph.sem("consts")
    stack_in = [ph.sem(f"stackin{u}") for u in range(HU)]
    mrow_in = [ph.sem(f"mrowin{u}") for u in range(HU)]
    LOADS = 16 * 3
    s_ps, s_max, m_all, m_ps, m_sb, m_part, m_row = (
        ph.sem(n) for n in ("sps", "smax", "mall", "mps", "msb", "mpart", "mrow"))
    e_ps, e_sb, weighed, v_sb = (ph.sem(n) for n in ("eps", "esb", "weighed", "vsb"))
    passed, passed_pe = ph.sem("passed"), ph.sem("passedpe")
    o_sb, t_ps, r_inv, t_used = (ph.sem(n) for n in ("osb", "tps", "rinvs", "tused"))

    def loops(eng, body):
        with eng.Fori(0, IT - 1) as it:
            body(it, False)
        body(IT - 1, True)

    with nc.Block() as block:
        @block.gpsimd
        def _(pool):
            for u in range(HU):
                pool.memset(QS[u][:, :], 0.0)
                pool.memset(KS[u][:, :], 0.0).then_inc(zeroed, 1)
            pool.memset(Vg[:, :, :, :].rearrange("p u t d -> p (u t d)"), 0.0).then_inc(consts, 1)
            pool.tensor_copy(identb[:, :], G["ident"][:, :]).then_inc(consts, 1)
            pool.memset(maskq[:, :], 0.0).then_inc(consts, 1)
            pool.memset(maskk[:, :], 0.0).then_inc(consts, 1)
            pool.wait_ge(consts, 4)
            pool.affine_select(out=maskq[:, :], in_=maskq[:, :], compare_op=ALU.is_ge, fill=-3.0e38,
                               base=0, pattern=[[-1, P]], channel_multiplier=1).then_inc(consts, 1)
            pool.affine_select(out=maskk[:, :], in_=maskk[:, :], compare_op=ALU.is_ge, fill=-3.0e38,
                               base=0, pattern=[[1, P]], channel_multiplier=-1).then_inc(consts, 1)


            def values(it, u):
                pool.tensor_copy(Vg[:, u, :, 0:9], V9[:, bass.ds(it, 1), u, :, :]
                                 .rearrange("p o t d -> p (o t) d")).then_inc(v_sb, 1)

            def split(h, s):
                pool.wait_ge(m_sb, h + 1)
                pool.sem_inc(passed, 1)
                pool.tensor_copy(mrow[:, s, 0, :], minus[:, :]).then_inc(m_part, 1)
                pool.wait_ge(m_part, h * 3 + 1)
                pool.tensor_tensor(res[:, :], minus[:, :], mrow[:, s, 0, :], ALU.subtract).then_inc(m_part, 1)
                pool.wait_ge(m_part, h * 3 + 2)
                pool.sem_inc(passed, 1)
                pool.tensor_copy(mrow[:, s, 1, :], res[:, :]).then_inc(m_part, 1)
                pool.wait_ge(m_part, h * 3 + 3)
                pool.tensor_tensor(mrow[:, s, 2, :], res[:, :], mrow[:, s, 1, :], ALU.subtract).then_inc(m_row, 1)

            pool.wait_ge(consts, 6)
            for u in range(HU):
                values(0, u)
            split(0, 0)
            with pool.Fori(0, IT - 1) as it:
                for u in range(HU):
                    split(it * HU + u + 1, (u + 1) % 2)
                    pool.wait_ge(weighed, NP + (it * HU + u + 1) * U)
                    pool.sem_inc(passed, 1)
                    values(it + 1, u)
            for u in range(HU - 1):
                split((IT - 1) * HU + u + 1, (u + 1) % 2)

        @block.sync
        def _(sp):
            def load(it, u):
                h = it * HU + u
                sp.dma_start(QS[u][0:MR + 6, :], bass.AP(qstack.tensor, h * (MR + 6) * T, [[T, MR + 6], [1, T]]))\
                  .then_inc(stack_in[u], 16)
                sp.dma_start(KS[u][0:MR, :], bass.AP(kparts.tensor, h * 24 * T, [[0, 3], [T, 24], [1, T]]))\
                  .then_inc(stack_in[u], 16)
                sp.dma_start(KS[u][MR:MR + 6, :], bass.AP(ktail.tensor, h * 6 * T, [[T, 6], [1, T]]))\
                  .then_inc(stack_in[u], 16)

            def maxima(h, u):
                for a in range(3):
                    if a < 2:
                        sp.wait_ge(m_part, h * 3 + (1, 3)[a])
                    else:
                        sp.wait_ge(m_row, h + 1)
                    sp.dma_start(QS[u][MR + a:MR + a + 1, :].rearrange("o (t q) -> o t q", t=TT), mrow[:, u % 2, a, :])\
                      .then_inc(mrow_in[u], 16)

            sp.wait_ge(zeroed, HU)
            for u in range(HU):
                load(0, u)
            maxima(0, 0)
            with sp.Fori(0, IT - 1) as it:
                for u in range(HU):
                    maxima(it * HU + u + 1, (u + 1) % HU)
                    sp.wait_ge(e_ps, (it * HU + u + 1) * U)
                    load(it + 1, u)
            for u in range(HU - 1):
                maxima((IT - 1) * HU + u + 1, u + 1)

        @block.tensor
        def _(pe):
            def first(it, u, k):
                h = it * HU + u
                i, c = sunits[k]
                if k == 0:
                    pe.wait_ge(stack_in[u], (it + 1) * LOADS)
                pe.wait_ge(s_max, h * U + k + 1)
                n = min((c + 1) * CH, (i + 1) * P) - c * CH
                diag = c == i // CT
                ins = pe.matmul(pS[k % 2][:, 0:n], QS[u][:, i * P:(i + 1) * P], KS[u][:, c * CH:c * CH + n],
                                start=True, stop=not diag)
                if diag:
                    ins = pe.matmul(pS[k % 2][:, n - P:n], identb[:, :], maskq[:, :], start=False, stop=True)
                ins.then_inc(s_ps, 1)

            def turn_maxima(h, s):
                pe.wait_ge(m_all, h + 1)
                pe.transpose(pX[0][0:TT, 0:P], mx[:, s, 0:TT], G["ident"][:, :]).then_inc(m_ps, 1)

            def second(it, u, n):
                h = it * HU + u
                c, j = eunits[n]
                if n == 0:
                    pe.wait_ge(mrow_in[u], (it + 1) * 48)
                pe.wait_ge(e_sb, h * U + n + 1)
                off = max(0, j * P - c * CH)
                diag = j >= c * CT
                ins = pe.matmul(pE[n % 2][:, off:CH], KS[u][:, j * P:(j + 1) * P], QS[u][:, c * CH + off:(c + 1) * CH],
                                start=True, stop=not diag)
                if diag:
                    ins = pe.matmul(pE[n % 2][:, off:off + P], identb[:, :], maskk[:, :], start=False, stop=True)
                ins.then_inc(e_ps, 1)

            def weigh(it, u, n):
                h = it * HU + u
                c, j = eunits[n]
                if n == 0:
                    pe.wait_ge(v_sb, h + 1)
                if u == 0 and j == 0:
                    pe.wait_ge(o_sb, 2 * it + c + 1)
                pe.wait_ge(e_sb, h * U + n + 3)
                off = max(0, j * P - c * CH)
                pe.matmul(pO[c][32 * u:32 * u + 32, off:CH], Vg[:, u, j, :], PT[:, n % NP, off:CH],
                          start=(j == 0), stop=(j == (c + 1) * CT - 1)).then_inc(weighed, 1)

            def body(it, last):
                before = None
                for u in range(HU):
                    ahead = (it, u + 2) if u + 2 < HU else None if last else (it + 1, u + 2 - HU)
                    held = HELD if u == HU - 1 else 0
                    for n in range(U):
                        second(it, u, n)
                        if ahead and n < U - held:
                            first(*ahead, n)
                        if before:
                            weigh(*before)
                        before = (it, u, n)
                        if n == (1 if u == 0 else 0) and not (last and u == HU - 1):
                            if u == 0:
                                pe.wait_ge(t_used, 2 * it + 2)
                            pe.wait_ge(m_row, it * HU + u + 1)
                            pe.sem_inc(passed_pe, 1)
                            turn_maxima(it * HU + u + 1, (u + 1) % 2)
                for k in range(U - HELD, U):
                    if ahead:
                        first(*ahead, k)
                    if k == U - HELD:
                        weigh(*before)
                for c in range(2):
                    pe.wait_ge(o_sb, 2 * it + c + 3)
                    pe.wait_ge(t_used, 2 * it + c + 1)
                    for t in range(CT):
                        ins = pe.transpose(pX[1 - c][:, t * P:(t + 1) * P], OT[:, (c * CT + t) * P:(c * CT + t + 1) * P],
                                           G["ident"][:, :])
                    ins.then_inc(t_ps, 1)

            pe.wait_ge(consts, 6)
            pe.sem_inc(weighed, NP)
            for u in range(2):
                for k in range(U):
                    first(0, u, k)
            turn_maxima(0, 0)
            loops(pe, body)

        @block.scalar
        def _(act):
            def rows(h):
                act.wait_ge(m_ps, h + 1)
                act.activation(minus[:, :], pX[0][0:TT, 0:P], ACT.Copy, scale=-1.0).then_inc(m_sb, 1)

            act.sem_inc(e_sb, 2)
            rows(0)

            def body(it, last):
                for u in range(HU):
                    for n, (c, j) in enumerate(eunits):
                        at = (it * HU + u) * U + n
                        off = max(0, j * P - c * CH)
                        act.wait_ge(e_ps, at + 1)
                        act.wait_ge(weighed, at + 1)
                        act.activation(PT[:, n % NP, off:CH], pE[n % 2][:, off:CH], ACT.Exp).then_inc(e_sb, 1)
                        if n == (1 if u == 0 else 0) and not (last and u == HU - 1):
                            rows(it * HU + u + 1)
            loops(act, body)

        @block.vector
        def _(dve):
            dve.sem_inc(s_max, 2)
            dve.sem_inc(o_sb, 2)
            dve.sem_inc(t_used, 2)

            def maximum(h, s, k):
                i, c = sunits[k]
                n = min((c + 1) * CH, (i + 1) * P) - c * CH
                slot = i + CT * c
                dve.wait_ge(s_ps, h * U + k + 1)
                dve.tensor_reduce(mx[:, s, slot:slot + 1], pS[k % 2][:, 0:n], AX.X, ALU.max).then_inc(s_max, 1)

            def join(h, s):
                dve.wait_ge(s_max, (h + 1) * U + 2)
                dve.tensor_tensor(mx[:, s, CT:TT], mx[:, s, CT:TT], mx[:, s, TT:TT + CT], ALU.max).then_inc(m_all, 1)

            def empty(it, c, n):
                dve.wait_ge(weighed, NP + (it * HU + HU - 1) * U + n)
                dve.tensor_copy(OT[:, c * CH:(c + 1) * CH], pO[c][:, :]).then_inc(o_sb, 1)

            def normalise(it, c):
                v = pX[1 - c][:, :].rearrange("p (t u d) -> p t u d", t=CT, u=HU)
                dve.wait_ge(t_ps, 2 * it + c + 1)
                dve.reciprocal(rinv[:, c, :, :], v[:, :, :, 8]).then_inc(r_inv, 1)
                dve.wait_ge(r_inv, 2 * it + c + 1)
                out = (mix[:, it, c * CT:(c + 1) * CT, :] if isinstance(it, int) else
                       mix[:, bass.ds(it, 1), c * CT:(c + 1) * CT, :].rearrange("p o t c -> p (o t) c"))
                dve.tensor_tensor(out.rearrange("p t (u d) -> p t u d", u=HU), v[:, :, :, 0:8],
                                  rinv[:, c, :, :].unsqueeze(3).to_broadcast([P, CT, HU, 8]), ALU.mult).then_inc(t_used, 1)

            def body(it, last):
                for u in range(HU):
                    h = it * HU + u
                    ahead = not (last and u + 2 >= HU)
                    for k in range(U):
                        if ahead:
                            maximum(h + 2, u % 2, k)
                        if u == HU - 1 and k == 6:
                            empty(it, 0, CT)
                        if u == HU - 1 and k == U - HELD:
                            empty(it, 1, U)
                    if ahead:
                        join(h + 2, u % 2)
                for c in range(2):
                    normalise(it, c)

            for h in range(2):
                for k in range(U):
                    maximum(h, h, k)
                join(h, h)
            loops(dve, body)
    ph.end()


def alibi_out(nc, G, wo):
    ph = Phase(nc, "a2o")
    X = G["X"]
    mix = G["XR"][:, :, :].rearrange("p a b -> p (a b)").rearrange("p (i t c) -> p i t c", i=4 * B, t=TT)
    rows = ph.sb("rows", [P, 2, CT, 4, 32])
    mT = ph.sb("mT", [P, 2, CH])
    pT = [ph.ps(f"T{i}") for i in range(2)]
    pY = [ph.ps(f"Y{i}") for i in range(2)]
    r_sb, t_ps, t_sb, y_ps, y_sb = (ph.sem(n) for n in ("rsb", "tps", "tsb", "yps", "ysb"))
    chunks = NT // CT
    with nc.Block() as block:
        @block.tensor
        def _(pe):
            def turn(c):
                if c >= 2:
                    pe.wait_ge(t_sb, c - 1)
                pe.wait_ge(r_sb, c + 1)
                for j in range(CT):
                    ins = pe.transpose(pT[c % 2][:, j * P:(j + 1) * P],
                                       rows[:, c % 2, j, :, :].rearrange("p g d -> p (g d)"), G["ident"][:, :])
                ins.then_inc(t_ps, 1)

            turn(0)
            for c in range(chunks):
                if c + 1 < chunks:
                    turn(c + 1)
                pe.wait_ge(t_sb, c + 1)
                if c >= 2:
                    pe.wait_ge(y_sb, c - 1)
                for j in range(CT):
                    ins = pe.matmul(pY[c % 2][:, j * P:(j + 1) * P], mT[:, c % 2, j * P:(j + 1) * P], wo,
                                    start=True, stop=True)
                ins.then_inc(y_ps, 1)

        @block.scalar
        def _(act):
            for c in range(chunks):
                act.wait_ge(t_ps, c + 1)
                if c >= 2:
                    act.wait_ge(y_ps, c - 1)
                act.copy(mT[:, c % 2, :], pT[c % 2][:, :]).then_inc(t_sb, 1)

        @block.vector
        def _(dve):
            def gather(c):
                b, h = divmod(c, TT // CT)
                if c >= 2:
                    dve.wait_ge(t_ps, c - 1)
                dve.tensor_copy(rows[:, c % 2, :, :, :].rearrange("p t g d -> p g t d"),
                                mix[:, 4 * b:4 * b + 4, h * CT:(h + 1) * CT, :]).then_inc(r_sb, 1)

            gather(0)
            for c in range(chunks):
                if c + 1 < chunks:
                    gather(c + 1)
                dve.wait_ge(y_ps, c + 1)
                xv = X[:, c * CT:(c + 1) * CT, :]
                dve.tensor_tensor(xv, xv, pY[c % 2][:, :].rearrange("p (k d) -> p k d", k=CT), ALU.add).then_inc(y_sb, 1)
    ph.end()


def moe_top2(nc, G, tag, gw, gb, w1, b1, w2, b2, rows):
    ph = Phase(nc, tag)
    X, XNT = G["X"], G["XNT"]
    E, FC = 8, 4
    lng, lnb = ph.sb("lng", [P, P]), ph.sb("lnb", [P, P])
    lg = ph.sb("lg", [P, CH])
    lgt, ex, pr = (ph.sb(n, [P, CT, E]) for n in ("lgt", "ex", "pr"))
    mx = ph.sb("mx", [P, CT, E])
    mi = ph.sb("mi", [P, CT, E], U32)
    mf, keep1, keep = (ph.sb(n, [P, CT, E]) for n in ("mf", "keep1", "keep"))
    io = ph.sb("io", [P, CT, E])
    sm, ri = ph.sb("sm", [P, CT]), ph.sb("ri", [P, CT])
    prT = ph.sb("prT", [E, CH])
    h = ph.sb("h", [P, 2, FC, CH])
    acc = ph.sb("acc", [P, CT, P])
    st, mv = ph.sb("st", [P, CT, 6]), ph.sb("mv", [P, CT, 2])
    sd, rs = ph.sb("sd", [P, CT]), ph.sb("rs", [P, CT])
    on = ph.sb("on", [P, CT, P])
    pU = [ph.ps(f"U{i}") for i in range(3)]
    pY = [ph.ps(f"Y{i}") for i in range(2)]
    pR = ph.ps("R")
    rows_in, io_done = ph.sem("rowsin"), ph.sem("iodone")
    names = ("lg_ps", "lg_sb", "lgt_ps", "lgt_sb", "mx_done", "mi_done", "mf_done", "keep1_done", "keep_done", "sub_done",
             "exp_done", "mask_done", "sum_done", "ri_done", "pr_done", "prT_ps", "prT_sb", "bias_ps", "acc0", "st_done",
             "mv_done", "sd_done", "rs_done", "on_done", "aff_done", "x_done")
    S = {n: ph.sem(n) for n in names}
    up, gelu, down, added = (ph.sem(n) for n in ("up", "gelu", "down", "added"))
    with nc.Block() as block:
        @block.sync
        def _(sp):
            sp.dma_start(lng[:, :], bass.AP(rows.tensor, 0, [[0, P], [1, P]])).then_inc(rows_in, 16)
            sp.dma_start(lnb[:, :], bass.AP(rows.tensor, P, [[0, P], [1, P]])).then_inc(rows_in, 16)
            sp.wait_ge(rows_in, 32)

        @block.gpsimd
        def _(pool):
            pool.iota(io[:, :, :], [[0, CT], [1, E]], base=0, channel_multiplier=0,
                      allow_small_or_imprecise_dtypes=True).then_inc(io_done, 1)
            pool.memset(lg[:, :], 0.0).then_inc(io_done, 1)

        @block.tensor
        def _(pe):
            with pe.Fori(0, B) as b:
                with pe.Fori(0, 2) as half:
                    c = b * 2 + half
                    x = XNT[:, b, bass.ds(half * CH + 1, CH)]

                    def ups(e):
                        for f in range(FC):
                            n = e * FC + f
                            if n >= 3:
                                pe.wait_ge(gelu, c * (E * FC) + n - 2)
                            pe.matmul(pU[n % 3][:, :], w1[:, n * P:(n + 1) * P], x, start=True, stop=True).then_inc(up, 1)

                    def downs(e):
                        pe.wait_ge(gelu, c * (E * FC) + (e + 1) * FC)
                        if e >= 2:
                            pe.wait_ge(added, c * E + e - 1)
                        for k in range(CT):
                            for f in range(FC):
                                ins = pe.matmul(pY[e % 2][:, k * P:(k + 1) * P], h[:, e % 2, f, k * P:(k + 1) * P],
                                                w2[:, (e * FC + f) * P:(e * FC + f + 1) * P],
                                                start=(f == 0), stop=(f == FC - 1))
                        ins.then_inc(down, 1)

                    pe.matmul(pR[0:E, :], gw, x, start=True, stop=True).then_inc(S["lg_ps"], 1)
                    ups(0)
                    pe.wait_ge(S["lg_sb"], c + 1)
                    for k in range(CT):
                        ins = pe.transpose(pR[:, k * P:(k + 1) * P], lg[:, k * P:(k + 1) * P], G["ident"][:, :])
                    ins.then_inc(S["lgt_ps"], 1)
                    ups(1)
                    pe.wait_ge(S["pr_done"], c + 1)
                    for k in range(CT):
                        ins = pe.transpose(pR[0:E, k * P:(k + 1) * P], pr[:, k, :], G["ident"][:, :])
                    ins.then_inc(S["prT_ps"], 1)
                    pe.wait_ge(S["prT_sb"], c + 1)
                    for k in range(CT):
                        ins = pe.matmul(pR[:, k * P:(k + 1) * P], prT[:, k * P:(k + 1) * P], b2, start=True, stop=True)
                    ins.then_inc(S["bias_ps"], 1)
                    for e in range(E):
                        downs(e)
                        if e + 2 < E:
                            ups(e + 2)
                    pe.wait_ge(added, c * E + E)
                    pe.wait_ge(S["acc0"], c + 1)

        @block.scalar
        def _(act):
            with act.Fori(0, B) as b:
                with act.Fori(0, 2) as half:
                    c = b * 2 + half

                    def gelus(e):
                        if e >= 2:
                            act.wait_ge(down, c * E + e - 1)
                        for f in range(FC):
                            n = e * FC + f
                            act.wait_ge(up, c * (E * FC) + n + 1)
                            act.activation(h[:, e % 2, f, :], pU[n % 3][:, :], ACT.Gelu, bias=b1[:, n:n + 1]).then_inc(gelu, 1)

                    gelus(0)
                    act.wait_ge(S["sub_done"], c + 1)
                    act.activation(ex[:, :, :], ex[:, :, :], ACT.Exp).then_inc(S["exp_done"], 1)
                    for e in range(1, E):
                        gelus(e)
                    act.wait_ge(S["mv_done"], c + 1)
                    act.activation(sd[:, :], mv[:, :, 1], ACT.Sqrt, bias=G["eps"][:, 0:1]).then_inc(S["sd_done"], 1)

        @block.vector
        def _(dve):
            dve.wait_ge(io_done, 2)
            dve.wait_ge(rows_in, 32)
            with dve.Fori(0, B) as b:
                with dve.Fori(0, 2) as half:
                    c = b * 2 + half

                    def step(name, ins):
                        ins.then_inc(S[name], 1)
                        dve.wait_ge(io_done, 1)
                        dve.wait_ge(S[name], c + 1)

                    dve.wait_ge(S["lg_ps"], c + 1)
                    dve.tensor_scalar(lg[0:E, :], pR[0:E, :], gb, 1.0 / 0.9, ALU.add, ALU.mult).then_inc(S["lg_sb"], 1)
                    dve.wait_ge(S["lgt_ps"], c + 1)
                    step("lgt_sb", dve.tensor_copy(lgt[:, :, :], pR[:, :].rearrange("p (k e) -> p k e", k=CT)[:, :, 0:E]))
                    for k in range(CT):
                        ins = dve.max(mx[:, k, :], lgt[:, k, :])
                    step("mx_done", ins)
                    for k in range(CT):
                        ins = dve.max_index(mi[:, k, :], mx[:, k, :], lgt[:, k, :])
                    ins.then_inc(S["mi_done"], 1)
                    dve.tensor_tensor(ex[:, :, :], lgt[:, :, :], mx[:, :, 0:1].to_broadcast([P, CT, E]),
                                      ALU.subtract).then_inc(S["sub_done"], 1)
                    dve.wait_ge(S["mi_done"], c + 1)
                    step("mf_done", dve.tensor_copy(mf[:, :, :], mi[:, :, :]))
                    dve.tensor_tensor(keep1[:, :, :], io[:, :, :], mf[:, :, 0:1].to_broadcast([P, CT, E]), ALU.is_equal)
                    step("keep1_done", dve.tensor_tensor(keep[:, :, :], io[:, :, :],
                                                         mf[:, :, 1:2].to_broadcast([P, CT, E]), ALU.is_equal))
                    step("keep_done", dve.tensor_tensor(keep[:, :, :], keep[:, :, :], keep1[:, :, :], ALU.add))
                    dve.wait_ge(S["exp_done"], c + 1)
                    step("mask_done", dve.tensor_tensor(keep1[:, :, :], ex[:, :, :], keep[:, :, :], ALU.mult))
                    step("sum_done", dve.tensor_reduce(sm[:, :], keep1[:, :, :], AX.X, ALU.add))
                    step("ri_done", dve.reciprocal(ri[:, :], sm[:, :]))
                    step("pr_done", dve.tensor_tensor(pr[:, :, :], keep1[:, :, :],
                                                      ri[:, :].rearrange("p (k o) -> p k o", o=1).to_broadcast([P, CT, E]), ALU.mult))
                    dve.wait_ge(S["prT_ps"], c + 1)
                    dve.tensor_copy(prT[:, :], pR[0:E, :]).then_inc(S["prT_sb"], 1)
                    dve.wait_ge(S["bias_ps"], c + 1)
                    step("acc0", dve.tensor_copy(acc[:, :, :], pR[:, :].rearrange("p (k d) -> p k d", k=CT)))
                    for e in range(E):
                        dve.wait_ge(down, c * E + e + 1)
                        if e:
                            dve.wait_ge(added, c * E + e)
                        for k in range(CT):
                            ins = dve.scalar_tensor_tensor(acc[:, k, :], pY[e % 2][:, k * P:(k + 1) * P], pr[:, k, e:e + 1],
                                                           acc[:, k, :], ALU.mult, ALU.add)
                        ins.then_inc(added, 1)
                    dve.wait_ge(added, c * E + E)
                    for k in range(CT):
                        ins = dve.bn_stats(st[:, k, :], acc[:, k, :])
                    step("st_done", ins)
                    for k in range(CT):
                        ins = dve.bn_aggr(mv[:, k, :], st[:, k, :])
                    step("mv_done", ins)
                    dve.wait_ge(S["sd_done"], c + 1)
                    step("rs_done", dve.reciprocal(rs[:, :], sd[:, :]))
                    for k in range(CT):
                        ins = dve.tensor_scalar(on[:, k, :], acc[:, k, :], mv[:, k, 0:1], rs[:, k:k + 1], ALU.subtract, ALU.mult)
                    step("on_done", ins)
                    wide = [P, CT, P]
                    step("aff_done", dve.tensor_tensor(acc[:, :, :], on[:, :, :],
                                                       lng[:, :].rearrange("p (o d) -> p o d", o=1).to_broadcast(wide), ALU.mult))
                    step("x_done", dve.tensor_tensor(on[:, :, :], acc[:, :, :],
                                                     lnb[:, :].rearrange("p (o d) -> p o d", o=1).to_broadcast(wide), ALU.add))
                    xv = X[:, bass.ds(c * CT, CT), :]
                    dve.tensor_tensor(xv, xv, on[:, :, :], ALU.add)
    ph.end()


def moe_capacity(nc, G, tag, rw, rb, w1, b1, w2, b2, ow1, ob1, ow2, rows, buf, ybuf):
    ph = Phase(nc, tag)
    X, XNT, XR = G["X"], G["XNT"], G["XR"]
    E, FC, CAP = 8, 4, 160
    SL = E * CAP
    ST = SL // P
    lg = ph.sb("lg", [E, 2, CH])
    lgt, mx, oh, cum, tot, run, sel = (ph.sb(n, [P, NT, E]) for n in ("lgt", "mx", "oh", "cum", "tot", "run", "sel"))
    mi = ph.sb("mi", [P, NT, E], U32)
    io = ph.sb("io", [P, NT, E])
    zero = ph.sb("zero", [P, NT])
    eid, rank, valid, inval, spare, slot, sc_f, ga_f, tmp = (
        ph.sb(n, [P, NT]) for n in ("eid", "rank", "valid", "inval", "spare", "slot", "scf", "gaf", "tmp"))
    sc_i, ga_i = ph.sb("sci", [P, NT], U32), ph.sb("gai", [P, NT], U32)
    zrow = ph.sb("zrow", [P, P])
    bt = ph.sb("bt", [P, ST, P])
    bT = ph.sb("bT", [P, SL])
    he = ph.sb("he", [P, 2, FC, CAP])
    yT = ph.sb("yT", [P, SL])
    yr = ph.sb("yr", [P, ST, P])
    ob2 = ph.sb("ob2", [1, P])
    h = ph.sb("h", [P, 2, FC, CH])
    yg = ph.sb("yg", [P, 8, P])
    pU = [ph.ps(f"U{i}") for i in range(3)]
    pY = [ph.ps(f"Y{i}") for i in range(2)]
    pR = [ph.ps(f"R{i}") for i in range(2)]
    const, zeroed, scattered, loaded, stored, ob_in = (
        ph.sem(n) for n in ("const", "zeroed", "scattered", "loaded", "stored", "obin"))
    gathered = [ph.sem(f"gathered{i}") for i in range(8)]
    lg_ps, lg_sb, lgt_ps, lgt_sb, cnt_ps, own = (ph.sem(n) for n in ("lgps", "lgsb", "lgtps", "lgtsb", "cntps", "own"))
    slots_done, bt_ps, bt_sb, up, act_up, down, act_down, yt_ps, yt_sb, valid_done = (
        ph.sem(n) for n in ("slots", "btps", "btsb", "up", "actup", "down", "actdown", "ytps", "ytsb", "valid"))
    o_up, o_relu, o_down, o_add, g_add = (ph.sem(n) for n in ("oup", "orelu", "odown", "oadd", "gadd"))
    with nc.Block() as block:
        @block.sync
        def _(sp):
            sp.dma_start(ob2[:, :], rows[2:3, :]).then_inc(ob_in, 16)
            sp.wait_ge(const, 1)
            for t in range(ST):
                sp.dma_start(buf[t * P:(t + 1) * P, :], zrow[:, :]).then_inc(zeroed, 16)
            sp.dma_start(ybuf[SL:SL + 1, :], zrow[0:1, :]).then_inc(zeroed, 16)
            sp.wait_ge(scattered, 16 * NT)
            sp.dma_start(bt[:, :, :], buf[0:SL, :].rearrange("(t p) d -> p t d", p=P)).then_inc(loaded, 16)
            sp.wait_ge(yt_sb, ST)
            sp.dma_start(ybuf[0:SL, :].rearrange("(t p) d -> p t d", p=P), yr[:, :, :]).then_inc(stored, 16)
            sp.wait_ge(ob_in, 16)

        @block.gpsimd
        def _(pool):
            pool.memset(zrow[:, :], 0.0).then_inc(const, 1)
            pool.iota(io[:, :, :], [[0, NT], [1, E]], base=0, channel_multiplier=0,
                      allow_small_or_imprecise_dtypes=True).then_inc(const, 1)
            pool.iota(spare[:, :], [[P, NT]], base=SL, channel_multiplier=1,
                      allow_small_or_imprecise_dtypes=True).then_inc(const, 1)
            pool.memset(zero[:, :], 0.0).then_inc(const, 1)
            pool.wait_ge(slots_done, 1)
            pool.wait_ge(zeroed, 16 * (ST + 1))
            for t in range(NT):
                pool.indirect_dma_start(out=buf[:, :], out_offset=bass.IndirectOffsetOnAxis(ap=sc_i[:, t:t + 1], axis=0),
                                        in_=XR[:, t, :], in_offset=None).then_inc(scattered, 16)
            pool.wait_ge(stored, 16)
            for t in range(NT):
                if t >= 8:
                    pool.wait_ge(g_add, t - 7)
                pool.indirect_dma_start(out=yg[:, t % 8, :], out_offset=None, in_=ybuf[:, :],
                                        in_offset=bass.IndirectOffsetOnAxis(ap=ga_i[:, t:t + 1], axis=0)).then_inc(gathered[t % 8], 16)

        @block.tensor
        def _(pe):
            pe.wait_ge(ob_in, 16)
            for c in range(NT // CT):
                x = XNT[:, c // 2, 1 + (c % 2) * CH:1 + (c % 2 + 1) * CH]
                if c >= 2:
                    pe.wait_ge(lgt_sb, c - 1)
                pe.matmul(pR[c % 2][0:E, :], rw, x, start=True, stop=True).then_inc(lg_ps, 1)
                pe.wait_ge(lg_sb, c + 1)
                for k in range(CT):
                    ins = pe.transpose(pR[c % 2][:, k * E:(k + 1) * E], lg[:, c % 2, k * P:(k + 1) * P], G["ident"][0:E, 0:E])
                ins.then_inc(lgt_ps, 1)
            pe.wait_ge(own, 3)
            flat = oh[:, :, :].rearrange("p n e -> p (n e)")
            pe.matmul(pR[0][:, 0:NT * E], G["tri"][:, :], flat, start=True, stop=True)
            pe.matmul(pR[1][:, 0:NT * E], G["ones"][:, :], flat, start=True, stop=True).then_inc(cnt_ps, 1)

            with pe.Fori(0, B) as b:
                with pe.Fori(0, 2) as half:
                    c = b * 2 + half
                    x = XNT[:, b, bass.ds(half * CH + 1, CH)]
                    for f in range(FC):
                        if f >= 3:
                            pe.wait_ge(o_relu, c * FC + f - 2)
                        pe.matmul(pU[f % 3][:, :], ow1[:, f * P:(f + 1) * P], x, start=True, stop=True).then_inc(o_up, 1)
                    pe.wait_ge(o_relu, c * FC + FC)
                    for k in range(CT):
                        for f in range(FC):
                            pe.matmul(pY[0][:, k * P:(k + 1) * P], h[:, 0, f, k * P:(k + 1) * P], ow2[:, f * P:(f + 1) * P],
                                      start=(f == 0), stop=False)
                        ins = pe.matmul(pY[0][:, k * P:(k + 1) * P], G["ones"][0:1, :], ob2[:, :], start=False, stop=True)
                    ins.then_inc(o_down, 1)
                    pe.wait_ge(o_add, c + 1)
            pe.wait_ge(loaded, 16)
            for t in range(ST):
                if t >= 2:
                    pe.wait_ge(bt_sb, t - 1)
                pe.transpose(pR[t % 2][:, 0:P], bt[:, t, :], G["ident"][:, :]).then_inc(bt_ps, 1)
            pe.wait_ge(bt_sb, ST)

            def ups(e):
                for f in range(FC):
                    n = e * FC + f
                    if n >= 3:
                        pe.wait_ge(act_up, n - 2)
                    pe.matmul(pU[n % 3][:, 0:CAP], w1[:, n * P:(n + 1) * P], bT[:, e * CAP:(e + 1) * CAP],
                              start=True, stop=True).then_inc(up, 1)

            def downs(e):
                pe.wait_ge(act_up, (e + 1) * FC)
                if e >= 2:
                    pe.wait_ge(act_down, e - 1)
                for f in range(FC):
                    n = e * FC + f
                    ins = pe.matmul(pY[e % 2][:, 0:CAP], w2[:, n * P:(n + 1) * P], he[:, e % 2, f, :],
                                    start=(f == 0), stop=(f == FC - 1))
                ins.then_inc(down, 1)

            ups(0)
            for e in range(E):
                if e + 1 < E:
                    ups(e + 1)
                downs(e)
            pe.wait_ge(act_down, E)
            for t in range(ST):
                if t >= 2:
                    pe.wait_ge(yt_sb, t - 1)
                pe.transpose(pR[t % 2][:, 0:P], yT[:, t * P:(t + 1) * P], G["ident"][:, :]).then_inc(yt_ps, 1)

        @block.scalar
        def _(act):
            with act.Fori(0, B) as b:
                with act.Fori(0, 2) as half:
                    c = b * 2 + half
                    for f in range(FC):
                        act.wait_ge(o_up, c * FC + f + 1)
                        act.activation(h[:, 0, f, :], pU[f % 3][:, :], ACT.Relu, bias=ob1[:, f:f + 1]).then_inc(o_relu, 1)
            def outputs(e):
                act.wait_ge(down, e + 1)
                act.activation(yT[:, e * CAP:(e + 1) * CAP], pY[e % 2][:, 0:CAP], ACT.Identity,
                               bias=b2[:, e:e + 1]).then_inc(act_down, 1)

            for e in range(E):
                for f in range(FC):
                    n = e * FC + f
                    if e >= 2:
                        act.wait_ge(down, e - 1)
                    act.wait_ge(up, n + 1)
                    act.activation(he[:, e % 2, f, :], pU[n % 3][:, 0:CAP], ACT.Relu, bias=b1[:, n:n + 1]).then_inc(act_up, 1)
                if e >= 1:
                    outputs(e - 1)
            outputs(E - 1)

        @block.vector
        def _(dve):
            done = [0]

            def chain(ins):
                done[0] += 1
                ins.then_inc(own, 1)
                dve.wait_ge(own, done[0])

            for c in range(NT // CT):
                dve.wait_ge(lg_ps, c + 1)
                dve.tensor_scalar(lg[:, c % 2, :], pR[c % 2][0:E, :], rb, None, ALU.add).then_inc(lg_sb, 1)
                dve.wait_ge(lgt_ps, c + 1)
                dve.tensor_copy(lgt[:, c * CT:(c + 1) * CT, :],
                                pR[c % 2][:, 0:CT * E].rearrange("p (k e) -> p k e", k=CT)).then_inc(lgt_sb, 1)
            dve.wait_ge(lgt_sb, NT // CT)
            dve.wait_ge(const, 4)
            for t in range(NT):
                ins = dve.max(mx[:, t, :], lgt[:, t, :])
            chain(ins)
            for t in range(NT):
                ins = dve.max_index(mi[:, t, :], mx[:, t, :], lgt[:, t, :])
            chain(ins)
            dve.tensor_copy(eid[:, :], mi[:, :, 0]).then_inc(valid_done, 1)
            dve.wait_ge(valid_done, 1)
            wide = [P, NT, E]
            chain(dve.tensor_tensor(oh[:, :, :], io[:, :, :],
                                    eid[:, :].rearrange("p (n o) -> p n o", o=1).to_broadcast(wide), ALU.is_equal))
            dve.wait_ge(cnt_ps, 1)
            dve.tensor_copy(cum[:, :, :], pR[0][:, 0:NT * E].rearrange("p (n e) -> p n e", e=E))
            chain(dve.tensor_copy(tot[:, :, :], pR[1][:, 0:NT * E].rearrange("p (n e) -> p n e", e=E)))
            for e in range(E):
                ins = dve.tensor_tensor_scan(run[:, :, e], tot[:, :, e], zero[:, :], 0.0, ALU.add, ALU.add)
            chain(ins)
            chain(dve.tensor_tensor(run[:, :, :], run[:, :, :], tot[:, :, :], ALU.subtract))
            chain(dve.tensor_tensor(cum[:, :, :], cum[:, :, :], run[:, :, :], ALU.add))
            chain(dve.tensor_tensor(sel[:, :, :], cum[:, :, :], oh[:, :, :], ALU.mult))
            chain(dve.tensor_reduce(rank[:, :], sel[:, :, :], AX.X, ALU.add))
            chain(dve.tensor_scalar(valid[:, :], rank[:, :], float(CAP), None, ALU.is_le))
            dve.tensor_scalar(inval[:, :], valid[:, :], -1.0, 1.0, ALU.mult, ALU.add)
            chain(dve.tensor_scalar(tmp[:, :], eid[:, :], float(CAP), -1.0, ALU.mult, ALU.add))
            chain(dve.tensor_tensor(slot[:, :], tmp[:, :], rank[:, :], ALU.add))
            chain(dve.tensor_tensor(slot[:, :], slot[:, :], valid[:, :], ALU.mult))
            dve.tensor_tensor(tmp[:, :], spare[:, :], inval[:, :], ALU.mult)
            chain(dve.tensor_scalar(ga_f[:, :], inval[:, :], float(SL), None, ALU.mult))
            chain(dve.tensor_tensor(sc_f[:, :], slot[:, :], tmp[:, :], ALU.add))
            chain(dve.tensor_tensor(ga_f[:, :], slot[:, :], ga_f[:, :], ALU.add))
            dve.tensor_copy(sc_i[:, :], sc_f[:, :])
            dve.tensor_copy(ga_i[:, :], ga_f[:, :]).then_inc(slots_done, 1)
            for c in range(NT // CT):
                dve.wait_ge(o_down, c + 1)
                for k in range(CT):
                    t = c * CT + k
                    ins = dve.scalar_tensor_tensor(X[:, t, :], pY[0][:, k * P:(k + 1) * P], inval[:, t:t + 1], X[:, t, :],
                                                   ALU.mult, ALU.add)
                ins.then_inc(o_add, 1)
            for t in range(ST):
                dve.wait_ge(bt_ps, t + 1)
                dve.tensor_copy(bT[:, t * P:(t + 1) * P], pR[t % 2][:, 0:P]).then_inc(bt_sb, 1)
            for t in range(ST):
                dve.wait_ge(yt_ps, t + 1)
                dve.tensor_copy(yr[:, t, :], pR[t % 2][:, 0:P]).then_inc(yt_sb, 1)
            for t in range(NT):
                dve.wait_ge(gathered[t % 8], 16 * (t // 8 + 1))
                dve.tensor_tensor(X[:, t, :], X[:, t, :], yg[:, t % 8, :], ALU.add).then_inc(g_add, 1)
    ph.end()


def wkv(nc, G, tag, w):
    ph = Phase(nc, tag)
    X, XNT = G["X"], G["XNT"]
    HK = 8
    GN_EPS = 1e-5 * 64
    dx, x5, t5a, xa, xb = (ph.sb(n, [P, T]) for n in ("dx", "x5", "t5a", "xa", "xb"))
    t5b = ph.sb("t5b", [32, T])
    td = ph.sb("td", [64, T])
    r, k, dec, g, gate = (ph.sb(n, [P, T]) for n in ("r", "k", "dec", "g", "gate"))
    kv, Sf, Ss, Sr = (ph.sb(n, [P, 2, T]) for n in ("kv", "Sf", "Ss", "Sr"))
    Sb = ph.sb("Sb", [P, 2, T + 1])
    eps = ph.sb("geps", [P, 1])
    pA, pB, pC, pD = (ph.ps(n, (P, 2 * CH)) for n in "ABCD")
    setup = ph.sem("setup")
    made = {}

    def S(name):
        if name not in made:
            made[name] = ph.sem(name)
        return made[name]

    def loops(eng, body):
        with eng.Fori(0, B - 1) as b:
            body(b, False)
        body(B - 1, True)

    ODD = [v for v in range(HK) if v % 2]

    def halves():
        return (slice(0, CH), slice(CH, T))

    mixes = ["w", "k", "v", "r", "g"]
    with nc.Block() as block:
        @block.gpsimd
        def _(pool):
            pool.memset(eps[:, :], GN_EPS)
            pool.memset(Sb[:, :, T:T + 1], 0.0).then_inc(setup, 1)
            with pool.Fori(0, B) as b:
                for v in range(HK):
                    n = b * HK + v
                    if v >= 2:
                        pool.wait_ge(S("y_mm"), n - 1)
                    if v in ODD:
                        pool.wait_ge(S("ssum_d"), b * len(ODD) + v // 2 + 1)
                    else:
                        pool.wait_ge(S("bwd"), n + 1)
                        pool.tensor_tensor(Ss[:, v % 2, :], Sf[:, v % 2, :], Sb[:, v % 2, 1:T + 1], ALU.add)\
                            .then_inc(S("ssum"), 1)
                        pool.wait_ge(S("ssum"), b * (HK - len(ODD)) + v // 2 + 1)
                    pool.tensor_tensor(Sr[:, v % 2, :], Ss[:, v % 2, :], r[:, :], ALU.mult).then_inc(S("sr"), 1)

        @block.tensor
        def _(pe):
            def product(out, lhsT, rhs, name):
                for cut in halves():
                    ins = pe.matmul(out[:, cut], lhsT, rhs[:, cut], start=True, stop=True)
                ins.then_inc(S(name), 1)

            def reduce(pe, b, v):
                n = b * HK + v
                if v == 0:
                    pe.wait_ge(S("g_sb"), b + 1)
                pe.wait_ge(S("sr"), n + 1)
                for cut in halves():
                    ins = pe.matmul(pD[:, cut], w["pick"][:, v * P:(v + 1) * P], Sr[:, v % 2, cut],
                                    start=(v == 0), stop=(v == HK - 1), skip_group_check=True)
                ins.then_inc(S("y_mm"), 1)

            def projection(pe, b, product, name):
                if name == "v":
                    return
                src = {"w": xa, "k": xb, "r": xb, "g": xa}[name]
                bank, weights, done = {"w": (pC[0:64, :], w["decay_w1"], "d1_ps"), "k": (pD, w["Wk"], "k_ps"),
                                       "r": (pC, w["Wr"], "r_ps"), "g": (pD, w["Wg"], "g_ps")}[name]
                pe.wait_ge(S({"w": "gate", "k": "dec_sb", "r": "dec_sb", "g": "k_sb"}[name]), b + 1)
                for half, cut in enumerate(halves()):
                    pe.matmul(bank[:, cut], weights, XNT[:, b, 1 + half * CH:1 + (half + 1) * CH], start=True, stop=False)
                pe.wait_ge(S("mix_" + name), b + 1)
                for cut in halves():
                    ins = pe.matmul(bank[:, cut], weights, src[:, cut], start=False, stop=True)
                ins.then_inc(S(done), 1)
                if name == "w":
                    pe.wait_ge(S("td"), b + 1)
                    product(pC, w["decay_w2"][0:64, :], td, "d2_ps")

            def begin(b, part):
                pe.wait_ge(S("x5"), b + 1)
                if part == 0:
                    product(pA, w["maa_w1"][:, 0:P], x5, "t5a_ps")
                else:
                    product(pB[0:32, :], w["maa_w1"][:, P:P + 32], x5, "t5b_ps")

            begin(0, 0)
            begin(0, 1)

            def body(b, last):
                pe.wait_ge(S("dx"), b + 1)
                product(pC, w["gate_w"], dx, "gate_ps")
                pe.wait_ge(S("t5"), b + 1)
                for n, name in enumerate(mixes):
                    bank = (pA, pB)[n % 2]
                    if n >= 2:
                        pe.wait_ge(S("mix_" + mixes[n - 2]), b + 1)
                    if n < 4:
                        product(bank, w["maa_w2"][:, n * P:(n + 1) * P], t5a, "m_" + name)
                    else:
                        product(bank, w["maa_w2e"], t5b, "m_" + name)
                    if n >= 1:
                        projection(pe, b, product, mixes[n - 1])
                projection(pe, b, product, "g")
                for v in range(HK):
                    n = b * HK + v
                    bank = (pA, pB)[v % 2]
                    if v >= 2:
                        pe.wait_ge(S("kv"), n - 1)
                    if v == 0:
                        pe.wait_ge(S("mix2_v"), b + 1)
                    for cut in halves():
                        ins = pe.matmul(bank[:, cut], w["Wv8"][:, v * P:(v + 1) * P], x5[:, cut], start=True, stop=True)
                    ins.then_inc(S("v_ps"), 1)
                    if v >= 2:
                        reduce(pe, b, v - 2)
                reduce(pe, b, HK - 2)
                reduce(pe, b, HK - 1)
                pe.wait_ge(S("yg"), b + 1)
                product(pC, w["mean8"], xa, "mu_ps")
                if not last:
                    pe.wait_ge(S("kv"), (b + 1) * HK)
                    begin(b + 1, 0)
                pe.wait_ge(S("sq"), b + 1)
                product(pD, w["mean8"], Sf[:, 0, :], "var_ps")
                if not last:
                    begin(b + 1, 1)
                pe.wait_ge(S("gn"), b + 1)
                for t in range(TT):
                    ins = pe.matmul(pC[:, t * P:(t + 1) * P], xa[:, t * P:(t + 1) * P], w["Wo"], start=True, stop=True)
                ins.then_inc(S("o_ps"), 1)
                pe.wait_ge(S("x"), b + 1)

            loops(pe, body)

        @block.scalar
        def _(act):
            act.wait_ge(setup, 1)

            def begin(b):
                act.wait_ge(S("t5a_ps"), b + 1)
                act.activation(t5a[:, :], pA[:, :], ACT.Tanh)
                act.wait_ge(S("t5b_ps"), b + 1)
                act.activation(t5b[:, :], pB[0:32, :], ACT.Tanh).then_inc(S("t5"), 1)

            begin(0)

            def body(b, last):
                act.wait_ge(S("gate_ps"), b + 1)
                act.activation(gate[:, :], pC[:, :], ACT.Sigmoid, bias=w["gate_b"]).then_inc(S("gate"), 1)
                act.wait_ge(S("d1_ps"), b + 1)
                act.activation(td[:, :], pC[0:64, :], ACT.Tanh).then_inc(S("td"), 1)
                act.wait_ge(S("d2_ps"), b + 1)
                act.activation(dec[:, :], pC[:, :], ACT.Exp, bias=w["time_decay"]).then_inc(S("dec_e"), 1)
                act.wait_ge(S("dec_e"), b + 1)
                act.activation(dec[:, :], dec[:, :], ACT.Exp, scale=-1.0).then_inc(S("dec_sb"), 1)
                act.wait_ge(S("k_ps"), b + 1)
                act.copy(k[:, :], pD[:, :]).then_inc(S("k_sb"), 1)
                act.wait_ge(S("r_ps"), b + 1)
                act.copy(r[:, :], pC[:, :]).then_inc(S("r_sb"), 1)
                act.wait_ge(S("g_ps"), b + 1)
                act.activation(g[:, :], pD[:, :], ACT.Silu).then_inc(S("g_sb"), 1)
                act.wait_ge(S("yc"), b + 1)
                act.activation(Sf[:, 0, :], xb[:, :], ACT.Square).then_inc(S("sq"), 1)
                act.wait_ge(S("var_ps"), b + 1)
                act.activation(Ss[:, 0, :], pD[:, :], ACT.Ln, bias=eps[:, 0:1]).then_inc(S("gln"), 1)
                act.wait_ge(S("gln"), b + 1)
                act.activation(Ss[:, 1, :], Ss[:, 0, :], ACT.Exp, scale=-0.5).then_inc(S("grs"), 1)
                if not last:
                    begin(b + 1)

            loops(act, body)

        @block.vector
        def _(dve):
            def begin(b, part):
                def step(name, ins):
                    ins.then_inc(S(name), 1)
                    dve.wait_ge(S(name), b + 1)

                cur, prev, nxt = (XNT[:, b, a:a + T] for a in (1, 0, 2))
                cw = w["conv_w"]
                if part == 0:
                    step("c1", dve.tensor_scalar(dx[:, :], prev, cw[:, 0:1], None, ALU.mult))
                    step("c2", dve.scalar_tensor_tensor(xa[:, :], cur, cw[:, 1:2], dx[:, :], ALU.mult, ALU.add))
                    step("c3", dve.scalar_tensor_tensor(dx[:, :], nxt, cw[:, 2:3], xa[:, :], ALU.mult, ALU.add))
                else:
                    step("dx", dve.tensor_tensor(dx[:, :], dx[:, :], cur, ALU.subtract))
                    step("x5", dve.scalar_tensor_tensor(x5[:, :], dx[:, :], w["maa_x"], cur, ALU.mult, ALU.add))

            begin(0, 0)
            begin(0, 1)

            def body(b, last):
                def step(name, ins):
                    ins.then_inc(S(name), 1)
                    dve.wait_ge(S(name), b + 1)

                cur = XNT[:, b, 1:1 + T]
                for n, name in enumerate(mixes):
                    dst = {"w": xa, "k": xb, "v": x5, "r": xb, "g": xa}[name]
                    bank = (pA, pB)[n % 2]
                    dve.wait_ge(S("m_" + name), b + 1)
                    if name == "r":
                        dve.wait_ge(S("k_ps"), b + 1)
                    if name == "g":
                        dve.wait_ge(S("d1_ps"), b + 1)
                    step("mix_" + name, dve.scalar_tensor_tensor(dst[:, :], bank[:, :], w["maa_" + name], dx[:, :],
                                                                 ALU.add, ALU.mult))
                    if name == "v":
                        step("mix2_v", dve.tensor_tensor(x5[:, :], x5[:, :], cur, ALU.add))
                dve.wait_ge(S("k_sb"), b + 1)
                dve.wait_ge(S("r_sb"), b + 1)
                for v in range(HK):
                    n = b * HK + v
                    bank = (pA, pB)[v % 2]
                    dve.wait_ge(S("v_ps"), n + 1)
                    dve.tensor_tensor(kv[:, v % 2, :], bank[:, :], k[:, :], ALU.mult).then_inc(S("kv"), 1)
                    if v >= 2 and v not in ODD:
                        dve.wait_ge(S("ssum"), b * (HK - len(ODD)) + v // 2)
                    dve.wait_ge(S("kv"), n + 1)
                    dve.tensor_tensor_scan(Sf[:, v % 2, :], dec[:, :], kv[:, v % 2, :], 0.0, ALU.mult, ALU.add)
                    dve.tensor_tensor_scan(Sb[:, v % 2, T - 1::-1], kv[:, v % 2, ::-1], dec[:, ::-1], 0.0,
                                           ALU.add, ALU.mult).then_inc(S("bwd"), 1)
                    if v in ODD:
                        dve.wait_ge(S("bwd"), n + 1)
                        if v >= 2:
                            dve.wait_ge(S("sr"), n - 1)
                        dve.tensor_tensor(Ss[:, v % 2, :], Sf[:, v % 2, :], Sb[:, v % 2, 1:T + 1], ALU.add)\
                           .then_inc(S("ssum_d"), 1)
                dve.wait_ge(S("g_sb"), b + 1)
                if not last:
                    begin(b + 1, 0)
                dve.wait_ge(S("y_mm"), b * HK + HK)
                step("yg", dve.tensor_tensor(xa[:, :], pD[:, :], gate[:, :], ALU.mult))
                if not last:
                    begin(b + 1, 1)
                dve.wait_ge(S("mu_ps"), b + 1)
                step("yc", dve.tensor_tensor(xb[:, :], xa[:, :], pC[:, :], ALU.subtract))
                dve.wait_ge(S("grs"), b + 1)
                step("g1", dve.tensor_tensor(xa[:, :], xb[:, :], Ss[:, 1, :], ALU.mult))
                step("g2", dve.tensor_scalar(xb[:, :], xa[:, :], w["ln_w"], w["ln_b"], ALU.mult, ALU.add))
                step("gn", dve.tensor_tensor(xa[:, :], xb[:, :], g[:, :], ALU.mult))
                dve.wait_ge(S("o_ps"), b + 1)
                xv = X[:, bass.ds(b * TT, TT), :]
                dve.tensor_tensor(xv, xv, pC[:, :].rearrange("p (k d) -> p k d", k=TT), ALU.add).then_inc(S("x"), 1)

            loops(dve, body)
    ph.end()


def store_out(nc, G, out):
    ph = Phase(nc, "fin")
    stored = ph.sem("stored")
    with nc.Block() as block:
        @block.sync
        def _(sp):
            sp.dma_start(out.rearrange("(n p) d -> p n d", p=P), G["X"][:, :, :]).then_inc(stored, 16)
            sp.wait_ge(stored, 16)
    ph.end()


def pack(inputs):
    a = {k: np.asarray(v) for k, v in inputs.items()}
    cols, at = [[], [], []], {}

    def put(name, m, part=0):
        m = np.asarray(m)
        if m.shape[0] < P:
            m = np.concatenate([m, np.zeros((P - m.shape[0], m.shape[1]), m.dtype)], 0)
        at[name] = (part, sum(c.shape[1] for c in cols[part]), m.shape[1])
        cols[part].append(m)

    put("W0", a["L0_attn_W"])
    put("b0", a["L0_attn_bias"].reshape(P, 1))
    for layer in ("L0", "L3"):
        for w in ("W_r", "W_k", "W_v"):
            put(f"{layer}{w}", a[f"{layer}_ffn_{w}"].T, 2 if layer == "L3" else 0)
        for w in ("mu_r", "mu_k"):
            put(f"{layer}{w}", a[f"{layer}_ffn_{w}"].reshape(P, 1), 2 if layer == "L3" else 0)
    put("rpe", a["L1_attn_rpe_bias"][:, :256])
    put("slopes", np.asarray([[-(2.0 ** (-0.5 * (h + 1)))] for h in range(16)], np.float32))
    for m, name in enumerate("qkv"):
        put(f"L1{name}", a["L1_attn_qkv"][:, m].reshape(P, 1024))
    put("L1o", a["L1_attn_out_w"].reshape(8, P, P).transpose(1, 0, 2).reshape(P, 1024))
    for name in "qkvo":
        put(f"L2{name}", a[f"L2_attn_W{name}"], 1)
    put("gw1", a["L1_ffn_gate_w"])
    put("gb1", a["L1_ffn_gate_b"].reshape(8, 1))
    put("w1", a["L1_ffn_w1"].transpose(1, 0, 2).reshape(P, 4096))
    put("b1", a["L1_ffn_b1"].reshape(32, P).T)
    put("w2", a["L1_ffn_w2"].reshape(32, P, P).transpose(1, 0, 2).reshape(P, 4096))
    put("b2", a["L1_ffn_b2"])
    put("rw", a["L2_ffn_router_w"], 1)
    put("rb", a["L2_ffn_router_b"].reshape(8, 1), 1)
    put("x1", a["L2_ffn_w1"].transpose(1, 0, 2).reshape(P, 4096), 1)
    put("xb1", a["L2_ffn_b1"].reshape(32, P).T, 1)
    put("x2", a["L2_ffn_w2"].reshape(32, P, P).transpose(1, 0, 2).reshape(P, 4096), 1)
    put("xb2", a["L2_ffn_b2"].T, 1)
    put("ow1", a["L2_ffn_ow1"], 1)
    put("ob1", a["L2_ffn_ob1"].reshape(4, P).T, 1)
    put("ow2", a["L2_ffn_ow2"].reshape(4, P, P).transpose(1, 0, 2).reshape(P, 512), 1)
    put("Aconv_w", a["L3_attn_conv_w"].reshape(P, 3), 2)
    for name in ("maa_x", "maa_w", "maa_k", "maa_v", "maa_r", "maa_g", "time_decay", "ln_w", "ln_b", "gate_b"):
        put("A" + name, a["L3_attn_" + name].reshape(P, 1), 2)
    put("Amaa_w1", a["L3_attn_maa_w1"], 2)
    w2 = a["L3_attn_maa_w2"]
    put("Amaa_w2", np.concatenate([np.concatenate([w2[f] if g == f else np.zeros_like(w2[f]) for g in range(4)], 0)
                                   for f in range(4)], 1), 2)
    put("Amaa_w2e", w2[4], 2)
    for name in ("decay_w1", "decay_w2", "Wr", "Wk", "Wg", "Wo", "gate_w"):
        put("A" + name, a["L3_attn_" + name], 2)
    put("AWv8", np.repeat(a["L3_attn_Wv"].reshape(P, 16, 8).transpose(0, 2, 1), 8, axis=2).reshape(P, 1024), 2)
    put("Amean8", np.kron(np.eye(16), np.full((8, 8), 1 / 8)).astype(np.float32), 2)
    put("Apick", np.concatenate([np.kron(np.eye(16), np.ones((8, 1)) * (np.arange(8) == v)[None]) for v in range(8)],
                                1).astype(np.float32), 2)
    rows = np.stack([a["L1_ffn_ln_g"], a["L1_ffn_ln_b"], a["L2_ffn_ob2"]])
    return [np.ascontiguousarray(np.concatenate(c, 1)) for c in cols] + [np.ascontiguousarray(rows)], at


def build(nc, x, wts, rows, out, at, stages="0f1g23h"):
    with ExitStack() as ctx:
        def sb(name, shape, dt=F32):
            return ctx.enter_context(nc.sbuf_tensor(name, shape, dt))

        G = dict(X=sb("X", [P, NT, P]), XNT=sb("XNT", [P, B, TP]), XR=sb("XR", [P, NT, P]),
                 WA=sb("WA", [P, max(wts[0].shape[1], wts[2].shape[1])]), ident=sb("ident", [P, P]),
                 tri=sb("tri", [P, P]), ones=sb("ones", [P, P]), eps=sb("eps", [P, 1]), x_dram=x)
        G["in1"], G["in2"] = nc.alloc_semaphore("in1"), nc.alloc_semaphore("in2")
        inner = ExitStack()
        G["WB"] = inner.enter_context(nc.sbuf_tensor("WB", [P, wts[1].shape[1]], F32))

        def w(name, rows=P):
            part, lo, n = at[name]
            return (G["WA"], G["WB"], G["WA"])[part][0:rows, lo:lo + n]

        constants(nc, G, wts, at["rpe"][1])
        if "0" in stages:
            layernorm(nc, G, "n0")
            channel_mix(nc, G, "l0", w("L0W_r"), w("L0W_k"), w("L0W_v"), w("L0mu_r"), w("L0mu_k"), (w("W0"), w("b0")))

        layernorm(nc, G, "n1", lambda sp: sp.wait_ge(G["in1"], G["in1_n"]))
        tab1 = nc.dram_tensor("tab1", [16, P - 1 + T], F32).ap()
        qstack = nc.dram_tensor("qstack", [B * 16, 78, T], BF16).ap()
        ktail = nc.dram_tensor("ktail", [B * 16, 6, T], BF16).ap()
        tables(nc, G, w("rpe", 16), w("slopes", 16), tab1, qstack, ktail)
        if "f" in stages:
            moe_top2(nc, G, "f1", w("gw1"), w("gb1", 8), w("w1"), w("b1"), w("w2"), w("b2", 8), rows)
        if "1" in stages:
            attention(nc, G, w("L1q"), w("L1k"), w("L1v"), w("L1o"), tab1, 64 ** -0.5, w("w1"))

        layernorm(nc, G, "n2", lambda sp: sp.wait_ge(G["in2"], G["in2_n"]))
        if "g" in stages:
            buf = nc.dram_tensor("slots", [8 * 160 + N, P], F32).ap()
            ybuf = nc.dram_tensor("slot_out", [8 * 160 + 1, P], F32).ap()
            moe_capacity(nc, G, "f2", w("rw"), w("rb", 8), w("x1"), w("xb1"), w("x2"), w("xb2"), w("ow1"), w("ob1"),
                         w("ow2"), rows, buf, ybuf)
        if "2" in stages:
            kparts = nc.dram_tensor("kparts", [B * 16, 24, T], BF16).ap()
            with nc.sbuf_tensor("V9", [P, 4 * B, 4, TT, 9], F32) as V9:
                alibi_split(nc, G, w("L2q"), w("L2k"), w("L2v"), V9, qstack, kparts, 8 ** -0.5)
                alibi_attention(nc, G, V9, qstack, kparts, ktail)
                alibi_out(nc, G, w("L2o"))
        inner.close()

        in3 = nc.alloc_semaphore("in3")
        layernorm(nc, G, "n3", lambda sp: sp.wait_ge(in3, load_columns(sp, in3, G["WA"], wts[2])))
        if "3" in stages:
            names = ("conv_w maa_x maa_w maa_k maa_v maa_r maa_g time_decay ln_w ln_b gate_b maa_w1 maa_w2 decay_w1 decay_w2 "
                     "Wr Wk Wg Wo gate_w Wv8 mean8 pick").split()
            aw = {n: w("A" + n) for n in names}
            aw["maa_w2e"] = w("Amaa_w2e", 32)
            wkv(nc, G, "a3", aw)
        if "h" in stages:
            channel_mix(nc, G, "l3", w("L3W_r"), w("L3W_k"), w("L3W_v"), w("L3mu_r"), w("L3mu_k"))
        store_out(nc, G, out)


def kernel(**inputs):
    import concourse.bacc as bacc
    from concourse.bass_utils import run_bass_kernel_spmd as run

    nc = bacc.Bacc("TRN2", target_bir_lowering=False, num_devices=1)
    packed, at = pack(inputs)
    x = np.ascontiguousarray(np.asarray(inputs["L0_attn_x"]).reshape(N, P))
    arrays = {"in_x": x} | {f"in_w{i}": m for i, m in enumerate(packed)}
    args = {k: nc.dram_tensor(k, list(v.shape), F32, kind="ExternalInput").ap() for k, v in arrays.items()}
    out = nc.dram_tensor("out_x", [N, P], F32, kind="ExternalOutput").ap()
    build(nc, args["in_x"], [args["in_w0"], args["in_w1"], args["in_w2"]], args["in_w3"], out, at)
    result = run(nc, [arrays], core_ids=[0]).results[0]["out_x"]
    return result.reshape(B, T, P)
```
